# Optimizing a Trainium2 kernel written in Bass

```python
import numpy as np
import jax
import jax.numpy as jnp

def _softmax(x, axis=-1):
    return jax.nn.softmax(x, axis=axis)

def _gelu(x):
    return jax.nn.gelu(x, approximate=True)

def _silu(x):
    return jax.nn.silu(x)

def _sigmoid(x):
    return jax.nn.sigmoid(x)

def _layernorm(x, axis=-1, eps=1e-05):
    m = jnp.mean(x, axis=axis, keepdims=True)
    v = jnp.var(x, axis=axis, keepdims=True)
    return (x - m) / jnp.sqrt(v + eps)

def _scatter_add(tgt, idx, src, axis=0):
    return tgt.at[idx].add(src)

def _segment_sum(src, seg, n):
    return jax.ops.segment_sum(src, seg, n)
kernel_name = 'mk_gnn_preln_d4_gnn_r8_4d7754'

def setup_inputs(seed: int=0):
    np.random.seed(seed)
    _w = jnp.asarray

    def _rec_inputs():
        import jax
        import jax.numpy as jnp
        _gk = jax.random.key(seed)
        x = -0.000202 + 1 * jax.random.normal(jax.random.fold_in(_gk, 1), (12500, 64), jnp.float32)
        _s = jax.random.randint(jax.random.fold_in(_gk, 2), (100000,), 0, 12500, jnp.int32)
        _d = jax.random.randint(jax.random.fold_in(_gk, 3), (100000,), 0, 12500, jnp.int32)
        _loop = jnp.arange(12500, dtype=jnp.int32)
        src = jnp.concatenate([_s, _d, _loop])
        dst = jnp.concatenate([_d, _s, _loop])
        _o = jnp.argsort(dst, stable=True)
        src = src[_o]
        dst = dst[_o]
        edge_type_65 = jax.random.randint(jax.random.fold_in(_gk, 13), (212500,), 0, 65, jnp.int32)
        edge_weight = jax.random.uniform(jax.random.fold_in(_gk, 14), (212500,), jnp.float32, 0.0, 1)
        edge_weight1 = jax.random.uniform(jax.random.fold_in(_gk, 15), (212500, 1), jnp.float32, 0.0, 1)
        node_vec1 = jax.random.uniform(jax.random.fold_in(_gk, 16), (12500, 1), jnp.float32, 0.0, 1)
        return (x, src, dst, edge_type_65, edge_weight, edge_weight1, node_vec1)
    x, src, dst, edge_type_65, edge_weight, edge_weight1, node_vec1 = _rec_inputs()

    def _L0_gnn_setup():
        import jax, jax.numpy as jnp
        import numpy as np
        N_NODES = 12500
        N_EDGES = 200000
        F_IN = 64
        F_OUT = 64
        key = jax.random.key(seed)
        k1, k2, k3, k4, k5 = jax.random.split(key, 5)
        node_features = jax.random.normal(k1, (N_NODES, F_IN), dtype=jnp.float32)
        edge_row = jax.random.randint(k2, (N_EDGES,), 0, N_NODES, dtype=jnp.int32)
        edge_col = jax.random.randint(k3, (N_EDGES,), 0, N_NODES, dtype=jnp.int32)
        edge_vals = jax.random.uniform(k4, (N_EDGES,), dtype=jnp.float32)
        kernel = jax.random.normal(k5, (F_IN, F_OUT), dtype=jnp.float32) * (1.0 / np.sqrt(F_IN))
        bias = jnp.zeros((F_OUT,), dtype=jnp.float32)
        return {'node_features': node_features, 'edge_row': edge_row, 'edge_col': edge_col, 'edge_vals': edge_vals, 'kernel': kernel, 'bias': bias}
    _L0_gnn_all = _L0_gnn_setup()
    _L0_gnn_in = {k: v for k, v in _L0_gnn_all.items() if k in ('kernel', 'bias')}
    del _L0_gnn_all

    def _L1_gnn_setup():
        import jax, jax.numpy as jnp
        import numpy as np
        EPS = 1e-07

        def expmap0(u):
            v = u[..., 1:]
            n = jnp.clip(jnp.linalg.norm(v, axis=-1, keepdims=True), EPS)
            return jnp.concatenate([jnp.cosh(n), jnp.sinh(n) * v / n], axis=-1)

        def logmap0(x):
            d = jnp.arccosh(jnp.clip(x[..., 0:1], 1.0 + EPS))
            y = x[..., 1:]
            yn = jnp.clip(jnp.linalg.norm(y, axis=-1, keepdims=True), EPS)
            return jnp.concatenate([jnp.zeros_like(d), d * y / yn], axis=-1)

        def lorentz_dist(x, y):
            inner = -x[..., 0:1] * y[..., 0:1] + jnp.sum(x[..., 1:] * y[..., 1:], axis=-1, keepdims=True)
            return jnp.arccosh(jnp.clip(-inner, 1.0 + EPS))

        def to_poincare(x):
            return x[..., 1:] / (x[..., 0:1] + 1.0)

        def to_lorentz(p):
            sq = jnp.sum(p * p, axis=-1, keepdims=True)
            denom = jnp.clip(1.0 - sq, EPS)
            return jnp.concatenate([(1.0 + sq) / denom, 2.0 * p / denom], axis=-1)
        N, E, D = (12500, 150000, 64)
        key = jax.random.key(seed)
        ks = jax.random.split(key, 8)
        v = 0.5 * jax.random.normal(ks[0], (N, D), dtype=jnp.float32)
        v = v.at[:, 0].set(0.0)
        x = expmap0(v)
        edge_attr = jax.random.normal(ks[1], (E, 1), dtype=jnp.float32)
        edges = jax.random.randint(ks[2], (2, E), 0, N)
        node_mask = jnp.ones((N, 1), jnp.float32)
        edge_mask = jnp.ones((E, 1), jnp.float32)
        s = 1.0 / np.sqrt(D).astype(np.float32)
        W = s * jax.random.normal(ks[3], (D, D), dtype=jnp.float32)
        b = jnp.zeros((D,), jnp.float32)
        w1 = 1.0 / np.sqrt(2 * D + 2).astype(np.float32) * jax.random.normal(ks[4], (2 * D + 2, D), dtype=jnp.float32)
        b1 = jnp.zeros((D,), jnp.float32)
        w2 = s * jax.random.normal(ks[5], (D, D), dtype=jnp.float32)
        b2 = jnp.zeros((D,), jnp.float32)
        w3 = s * jax.random.normal(ks[6], (D, 1), dtype=jnp.float32)
        b3 = jnp.zeros((1,), jnp.float32)
        gamma = jnp.ones((D,), jnp.float32)
        beta = jnp.zeros((D,), jnp.float32)
        return dict(x=x, edge_attr=edge_attr, edges=edges, node_mask=node_mask, edge_mask=edge_mask, W=W, b=b, w1=w1, b1=b1, w2=w2, b2=b2, w3=w3, b3=b3, gamma=gamma, beta=beta)
    _L1_gnn_all = _L1_gnn_setup()
    _L1_gnn_in = {k: v for k, v in _L1_gnn_all.items() if k in ('W', 'b', 'w1', 'b1', 'w2', 'b2', 'w3', 'b3', 'gamma', 'beta')}
    del _L1_gnn_all

    def _L2_gnn_setup():
        import jax, jax.numpy as jnp
        import numpy as np
        N = 12500
        E = 200000
        F_IN = 64
        H = 8
        C = 8
        NEG_SLOPE = 0.2

        def gat_layer(x, src, dst, W, a_src, a_dst, b):
            h = (x @ W).reshape(N, H, C)
            alpha_s = jnp.einsum('nhc,hc->nh', h, a_src)
            alpha_d = jnp.einsum('nhc,hc->nh', h, a_dst)
            e = jax.nn.leaky_relu(alpha_s[src] + alpha_d[dst], NEG_SLOPE)
            m = jax.ops.segment_max(e, dst, num_segments=N)
            ex = jnp.exp(e - m[dst])
            denom = jax.ops.segment_sum(ex, dst, num_segments=N)
            alpha = ex / (denom[dst] + 1e-16)
            out = jax.ops.segment_sum(h[src] * alpha[:, :, None], dst, num_segments=N)
            return out.reshape(N, H * C) + b
        key = jax.random.key(seed)
        ks = jax.random.split(key, 14)
        x = jax.random.normal(ks[0], (N, F_IN), dtype=jnp.float32)
        edge_index = jax.random.randint(ks[1], (2, E), 0, N, dtype=jnp.int64)
        inp = {'x': x, 'edge_index': edge_index}
        s = 1.0 / np.sqrt(F_IN)
        for li, kbase in zip((1, 2, 3), (2, 6, 10)):
            inp[f'W{li}'] = jax.random.uniform(ks[kbase], (F_IN, H * C), jnp.float32, -s, s)
            inp[f'a_src{li}'] = jax.random.uniform(ks[kbase + 1], (H, C), jnp.float32, -s, s)
            inp[f'a_dst{li}'] = jax.random.uniform(ks[kbase + 2], (H, C), jnp.float32, -s, s)
            inp[f'b{li}'] = jnp.zeros((H * C,), jnp.float32)
        return inp
    _L2_gnn_all = _L2_gnn_setup()
    _L2_gnn_in = {k: v for k, v in _L2_gnn_all.items() if k in ('W1', 'a_src1', 'a_dst1', 'b1', 'W2', 'a_src2', 'a_dst2', 'b2', 'W3', 'a_src3', 'a_dst3', 'b3')}
    del _L2_gnn_all

    def _L3_gnn_setup():
        import jax, jax.numpy as jnp
        import numpy as np
        N, E, D, R, L = (6250, 75000, 64, 65, 2)

        def _rgcn_conv(x, src, dst, edge_type, W_r, W_root, b):
            n, d = x.shape
            r = W_r.shape[0]
            seg = dst * r + edge_type
            msg = x[src]
            agg = jax.ops.segment_sum(msg, seg, num_segments=n * r).reshape(n, r, d)
            cnt = jax.ops.segment_sum(jnp.ones((msg.shape[0],), x.dtype), seg, num_segments=n * r).reshape(n, r, 1)
            mean = agg / jnp.maximum(cnt, 1.0)
            out = jnp.einsum('nrd,rdk->nk', mean, W_r)
            return out + x @ W_root + b
        key = jax.random.key(seed)
        ks = jax.random.split(key, 10)
        x = jax.random.normal(ks[0], (N, D), dtype=jnp.float32)
        edge_index = jax.random.randint(ks[1], (2, E), 0, N, dtype=jnp.int64)
        edge_type = jax.random.randint(ks[2], (E,), 0, R, dtype=jnp.int64)
        s = 1.0 / np.sqrt(D)
        W = jax.random.normal(ks[3], (L, R, D, D), dtype=jnp.float32) * s
        root = jax.random.normal(ks[4], (L, D, D), dtype=jnp.float32) * s
        bias = jax.random.normal(ks[5], (L, D), dtype=jnp.float32) * 0.01
        res_W = jax.random.normal(ks[6], (L, D, D), dtype=jnp.float32) * s
        res_b = jax.random.normal(ks[7], (L, D), dtype=jnp.float32) * 0.01
        return {'x': x, 'edge_index': edge_index, 'edge_type': edge_type, 'W': W, 'root': root, 'bias': bias, 'res_W': res_W, 'res_b': res_b}
    _L3_gnn_all = _L3_gnn_setup()
    _L3_gnn_in = {k: v for k, v in _L3_gnn_all.items() if k in ('W', 'root', 'bias', 'res_W', 'res_b')}
    del _L3_gnn_all
    return {'x': x, 'src': src, 'dst': dst, 'edge_type_65': edge_type_65, 'edge_weight': edge_weight, 'edge_weight1': edge_weight1, 'node_vec1': node_vec1, 'L0_gnn_kernel': _L0_gnn_in['kernel'], 'L0_gnn_bias': _L0_gnn_in['bias'], 'L1_gnn_W': _L1_gnn_in['W'], 'L1_gnn_b': _L1_gnn_in['b'], 'L1_gnn_w1': _L1_gnn_in['w1'], 'L1_gnn_b1': _L1_gnn_in['b1'], 'L1_gnn_w2': _L1_gnn_in['w2'], 'L1_gnn_b2': _L1_gnn_in['b2'], 'L1_gnn_w3': _L1_gnn_in['w3'], 'L1_gnn_b3': _L1_gnn_in['b3'], 'L1_gnn_gamma': _L1_gnn_in['gamma'], 'L1_gnn_beta': _L1_gnn_in['beta'], 'L2_gnn_W1': _L2_gnn_in['W1'], 'L2_gnn_a_src1': _L2_gnn_in['a_src1'], 'L2_gnn_a_dst1': _L2_gnn_in['a_dst1'], 'L2_gnn_b1': _L2_gnn_in['b1'], 'L2_gnn_W2': _L2_gnn_in['W2'], 'L2_gnn_a_src2': _L2_gnn_in['a_src2'], 'L2_gnn_a_dst2': _L2_gnn_in['a_dst2'], 'L2_gnn_b2': _L2_gnn_in['b2'], 'L2_gnn_W3': _L2_gnn_in['W3'], 'L2_gnn_a_src3': _L2_gnn_in['a_src3'], 'L2_gnn_a_dst3': _L2_gnn_in['a_dst3'], 'L2_gnn_b3': _L2_gnn_in['b3'], 'L3_gnn_W': _L3_gnn_in['W'], 'L3_gnn_root': _L3_gnn_in['root'], 'L3_gnn_bias': _L3_gnn_in['bias'], 'L3_gnn_res_W': _L3_gnn_in['res_W'], 'L3_gnn_res_b': _L3_gnn_in['res_b']}

def reference(x, src, dst, edge_type_65, edge_weight, edge_weight1, node_vec1, L0_gnn_kernel, L0_gnn_bias, L1_gnn_W, L1_gnn_b, L1_gnn_w1, L1_gnn_b1, L1_gnn_w2, L1_gnn_b2, L1_gnn_w3, L1_gnn_b3, L1_gnn_gamma, L1_gnn_beta, L2_gnn_W1, L2_gnn_a_src1, L2_gnn_a_dst1, L2_gnn_b1, L2_gnn_W2, L2_gnn_a_src2, L2_gnn_a_dst2, L2_gnn_b2, L2_gnn_W3, L2_gnn_a_src3, L2_gnn_a_dst3, L2_gnn_b3, L3_gnn_W, L3_gnn_root, L3_gnn_bias, L3_gnn_res_W, L3_gnn_res_b):
    import jax
    import jax.numpy as jnp

    def _L0_gnn_ref(node_features, edge_row, edge_col, edge_vals, kernel, bias):
        import jax, jax.numpy as jnp
        import numpy as np
        N_NODES = 12500
        N_EDGES = 200000
        F_IN = 64
        F_OUT = 64
        transformed = node_features @ kernel
        messages = edge_vals[:, None] * transformed[edge_col]
        aggregated = jax.ops.segment_sum(messages, edge_row, num_segments=N_NODES)
        return jax.nn.relu(aggregated + bias)

    def _L1_gnn_ref(x, edge_attr, edges, node_mask, edge_mask, W, b, w1, b1, w2, b2, w3, b3, gamma, beta):
        import jax, jax.numpy as jnp
        import numpy as np
        EPS = 1e-07

        def expmap0(u):
            v = u[..., 1:]
            n = jnp.clip(jnp.linalg.norm(v, axis=-1, keepdims=True), EPS)
            return jnp.concatenate([jnp.cosh(n), jnp.sinh(n) * v / n], axis=-1)

        def logmap0(x):
            d = jnp.arccosh(jnp.clip(x[..., 0:1], 1.0 + EPS))
            y = x[..., 1:]
            yn = jnp.clip(jnp.linalg.norm(y, axis=-1, keepdims=True), EPS)
            return jnp.concatenate([jnp.zeros_like(d), d * y / yn], axis=-1)

        def lorentz_dist(x, y):
            inner = -x[..., 0:1] * y[..., 0:1] + jnp.sum(x[..., 1:] * y[..., 1:], axis=-1, keepdims=True)
            return jnp.arccosh(jnp.clip(-inner, 1.0 + EPS))

        def to_poincare(x):
            return x[..., 1:] / (x[..., 0:1] + 1.0)

        def to_lorentz(p):
            sq = jnp.sum(p * p, axis=-1, keepdims=True)
            denom = jnp.clip(1.0 - sq, EPS)
            return jnp.concatenate([(1.0 + sq) / denom, 2.0 * p / denom], axis=-1)
        row, col = (edges[0], edges[1])
        geodesic = lorentz_dist(x[row], x[col])
        h = logmap0(x) @ W + b
        in_edge = jnp.concatenate([edge_attr, geodesic], -1)
        feat = jnp.concatenate([h[row], h[col], in_edge], -1)
        a = jax.nn.silu(feat @ w1 + b1)
        a = jax.nn.silu(a @ w2 + b2)
        att = jax.nn.sigmoid(a @ w3 + b3) * edge_mask
        msg = h[col] * att
        agg = jax.ops.segment_sum(msg, row, num_segments=h.shape[0])
        h = h + agg
        mu = jnp.mean(h, -1, keepdims=True)
        var = jnp.var(h, -1, keepdims=True)
        h = (h - mu) / jnp.sqrt(var + 1e-05) * gamma + beta
        h = h.at[:, 0].set(0.0)
        h = expmap0(h)
        p = jax.nn.silu(to_poincare(h))
        return to_lorentz(p)

    def _L2_gnn_ref(x, edge_index, W1, a_src1, a_dst1, b1, W2, a_src2, a_dst2, b2, W3, a_src3, a_dst3, b3):
        import jax, jax.numpy as jnp
        import numpy as np
        N = 12500
        E = 200000
        F_IN = 64
        H = 8
        C = 8
        NEG_SLOPE = 0.2

        def gat_layer(x, src, dst, W, a_src, a_dst, b):
            h = (x @ W).reshape(N, H, C)
            alpha_s = jnp.einsum('nhc,hc->nh', h, a_src)
            alpha_d = jnp.einsum('nhc,hc->nh', h, a_dst)
            e = jax.nn.leaky_relu(alpha_s[src] + alpha_d[dst], NEG_SLOPE)
            m = jax.ops.segment_max(e, dst, num_segments=N)
            ex = jnp.exp(e - m[dst])
            denom = jax.ops.segment_sum(ex, dst, num_segments=N)
            alpha = ex / (denom[dst] + 1e-16)
            out = jax.ops.segment_sum(h[src] * alpha[:, :, None], dst, num_segments=N)
            return out.reshape(N, H * C) + b
        loop = jnp.arange(N, dtype=edge_index.dtype)
        src = jnp.concatenate([edge_index[0], loop])
        dst = jnp.concatenate([edge_index[1], loop])
        h = jax.nn.relu(gat_layer(x, src, dst, W1, a_src1, a_dst1, b1))
        h = jax.nn.relu(gat_layer(h, src, dst, W2, a_src2, a_dst2, b2))
        return gat_layer(h, src, dst, W3, a_src3, a_dst3, b3)

    def _L3_gnn_ref(x, edge_index, edge_type, W, root, bias, res_W, res_b):
        import jax, jax.numpy as jnp
        import numpy as np
        N, E, D, R, L = (6250, 75000, 64, 65, 2)

        def _rgcn_conv(x, src, dst, edge_type, W_r, W_root, b):
            n, d = x.shape
            r = W_r.shape[0]
            seg = dst * r + edge_type
            msg = x[src]
            agg = jax.ops.segment_sum(msg, seg, num_segments=n * r).reshape(n, r, d)
            cnt = jax.ops.segment_sum(jnp.ones((msg.shape[0],), x.dtype), seg, num_segments=n * r).reshape(n, r, 1)
            mean = agg / jnp.maximum(cnt, 1.0)
            out = jnp.einsum('nrd,rdk->nk', mean, W_r)
            return out + x @ W_root + b
        src, dst = (edge_index[0], edge_index[1])
        h = x
        for l in range(W.shape[0]):
            conv = _rgcn_conv(h, src, dst, edge_type, W[l], root[l], bias[l])
            conv = jax.nn.relu(conv)
            res = jax.nn.relu(h @ res_W[l] + res_b[l])
            h = conv + res
        return h
    edge_index = jnp.stack([src, dst])
    h = jnp.maximum(_layernorm(x, axis=-1), 0.0)
    x = x + _L0_gnn_ref(h, src, dst, edge_weight, L0_gnn_kernel, L0_gnn_bias)
    h = jnp.maximum(_layernorm(x, axis=-1), 0.0)
    x = x + _L1_gnn_ref(h, edge_weight1, edge_index, node_vec1, edge_weight1, L1_gnn_W, L1_gnn_b, L1_gnn_w1, L1_gnn_b1, L1_gnn_w2, L1_gnn_b2, L1_gnn_w3, L1_gnn_b3, L1_gnn_gamma, L1_gnn_beta)
    h = jnp.maximum(_layernorm(x, axis=-1), 0.0)
    x = x + _L2_gnn_ref(h, edge_index, L2_gnn_W1, L2_gnn_a_src1, L2_gnn_a_dst1, L2_gnn_b1, L2_gnn_W2, L2_gnn_a_src2, L2_gnn_a_dst2, L2_gnn_b2, L2_gnn_W3, L2_gnn_a_src3, L2_gnn_a_dst3, L2_gnn_b3)
    h = jnp.maximum(_layernorm(x, axis=-1), 0.0)
    x = x + _L3_gnn_ref(h, edge_index, edge_type_65, L3_gnn_W, L3_gnn_root, L3_gnn_bias, L3_gnn_res_W, L3_gnn_res_b)
    return x

_drawn_inputs = setup_inputs


def setup_inputs(seed=0):
    import zlib

    import numpy as np

    out = dict(_drawn_inputs(seed))
    spreads = {'L0_gnn_bias': (0.0, 0.349),
     'L1_gnn_b': (0.0, 0.1),
     'L1_gnn_b1': (0.0, 2.0),
     'L1_gnn_b2': (0.0, 2.0),
     'L1_gnn_gamma': (1.0, 0.6),
     'L1_gnn_beta': (0.0, 0.8),
     'L2_gnn_b1': (0.0, 0.8),
     'L2_gnn_b2': (0.0, 0.791),
     'L2_gnn_b3': (0.0, 0.306)}
    factors = {'edge_weight1': 64.0,
     'L1_gnn_W': 64.0,
     'L1_gnn_w1': 64.0,
     'L1_gnn_w2': 64.0,
     'L1_gnn_w3': 64.0,
     'L2_gnn_W1': 4.322,
     'L2_gnn_a_src1': 8.0,
     'L2_gnn_a_dst1': 8.0,
     'L2_gnn_W2': 2.889,
     'L2_gnn_a_src2': 8.0,
     'L2_gnn_a_dst2': 42.14,
     'L2_gnn_W3': 3.384,
     'L2_gnn_a_src3': 50.794,
     'L2_gnn_a_dst3': 64.0,
     'L3_gnn_bias': 8.0,
     'L3_gnn_res_b': 22.993}
    for name, (base, spread) in spreads.items():
        noise = np.random.default_rng([zlib.crc32(name.encode()), seed]).standard_normal(out[name].shape)
        drawn = base * np.exp(spread * noise) if base else spread * noise
        out[name] = jnp.asarray(drawn.astype(out[name].dtype))
    for name, factor in factors.items():
        out[name] = (out[name] * factor).astype(out[name].dtype)
    return out
```

```python
from contextlib import ExitStack

import concourse.bass as bass
from concourse import mybir

F32, I32, BF16 = mybir.dt.float32, mybir.dt.int32, mybir.dt.bfloat16
ALU, ACT, AX = mybir.AluOpType, mybir.ActivationFunctionType, mybir.AxisListType
ENG = mybir.EngineType
ds = bass.ds

P = 128
N, E, D = 12500, 212500, 64
H = 8
R = 65
K = 8
CE = K * P
ET = 1664
EB = ET // P
EP = ET * P
CHUNKS = ET // K
NT = 100
NR = NT * P
SPARE = P
COPIES = K
BIG = 1.0e30
LRELU = 0.2
ACOSH_MIN = 1.0 + 1e-7
SRC, REL, EW, EW1, TYPE, END, SIDX, INV = range(8)
FIELDS = 8


class Chain:

    def __init__(self, eng, sem, base=0):
        self.eng, self.sem, self.base, self.n = eng, sem, base, 0

    def __call__(self, ins):
        self.n += 1
        ins.then_inc(self.sem, 1)
        self.eng.wait_ge(self.sem, self.base + self.n)


def ready(c):
    return c + 3


def free1(c):
    return c + 2


def free2(c):
    return c + 1


def alone(eng, mark):
    eng.sem_inc(mark, 1)


def pairs(eng, body, count=CHUNKS):
    with eng.Fori(0, count // 2) as i:
        for s in range(2):
            body(i * 2 + s, s, i)


def skewed(eng, first, second, count=CHUNKS):
    first(0, 0, 0)
    with eng.Fori(0, count // 2 - 1) as i:
        first(i * 2 + 1, 1, i)
        second(i * 2, 0, i)
        first(i * 2 + 2, 0, i + 1)
        second(i * 2 + 1, 1, i)
    last = count // 2 - 1
    first(count - 1, 1, last)
    second(count - 2, 0, last)
    second(count - 1, 1, last)


def turns(eng, turn, count=CHUNKS):
    with eng.Fori(0, count // 2 - 1) as i:
        turn(i * 2, 0, i, i * 2 + 1, 1, i)
        turn(i * 2 + 1, 1, i, i * 2 + 2, 0, i + 1)
    last = count // 2 - 1
    turn(count - 2, 0, last, count - 1, 1, last)
    turn(count - 1, 1, last, None, None, None)


def staggered(eng, early, rest, late, count=CHUNKS):
    early(0, 0, 0)
    rest(0, 0, 0)

    def turn(c, s, i, c1, s1, i1):
        if c1 is not None:
            early(c1, s1, i1)
        late(c, s, i)
        if c1 is not None:
            rest(c1, s1, i1)
    turns(eng, turn, count)


def bases(nc, engine, base, c):
    _, regs = nc.values_load_multi_w_load_instructions(
        base[0:1, ds(c * K, K)], engines=(engine,), min_val=0, max_val=N,
        skip_runtime_bounds_check_because="dst is a node or the padding node")
    return regs


def spread(ap, n):
    return ap.unsqueeze(2).broadcast_to([ap.shape[0], ap.shape[1], n])


def repeat(ap, n):
    return ap.unsqueeze(1).broadcast_to([ap.shape[0], n, ap.shape[1]])


class Phase:

    def __init__(self, nc, name):
        self.nc, self.name, self.stack, self.used = nc, name, ExitStack(), []

    def __enter__(self):
        self.stack.__enter__()
        return self

    def __exit__(self, *a):
        if self.used:
            self.nc.clear_and_free_semaphores(self.used)
            self.nc.all_engine_barrier()
        return self.stack.__exit__(*a)

    def sem(self, name):
        self.used.append(self.nc.alloc_semaphore(f"{self.name}_{name}"))
        return self.used[-1]

    def sems(self, names):
        return [self.sem(n) for n in names.split()]

    def sb(self, name, shape, dt=F32):
        return self.stack.enter_context(self.nc.sbuf_tensor(f"{self.name}_{name}", shape, dt))

    def ps(self, name, shape, dt=F32):
        return self.stack.enter_context(self.nc.psum_tensor(f"{self.name}_{name}", shape, dt))


def prepare(nc, g):
    with Phase(nc, "prep") as ph:
        loaded, padded, const, turned, copied, step, stored, rows_in, zeroed = ph.sems(
            "loaded padded const turned copied step stored rows_in zeroed")
        padi = ph.sb("padi", [P, 16], I32)
        padf = ph.sb("padf", [P, 16])
        raw = [ph.sb(f"raw{n}", [P, EB, P], I32 if n < 5 else F32) for n in range(7)]
        rows = [ph.sb(f"rows{n}", [P, EB, P]) for n in range(5)]
        mask = ph.sb("mask", [P, 2, EB, P])
        dstf = ph.sb("dstf", [P, ET])
        zw = (NR + SPARE) // P * D // 2
        zero = ph.sb("zero", [P, zw])
        turn = [ph.ps(f"turn{n}", [P, 512]) for n in range(4)]
        src_r, dst_r, prev_r, next_r, type_r = range(5)
        flat = EP - E
        fields = (SRC, None, TYPE, EW, EW1, END)
        with nc.Block() as block:
            @block.gpsimd
            def _(pool):
                nc.gpsimd.iota(g.iota[:, :], [[1, P]], base=0, channel_multiplier=0,
                               allow_small_or_imprecise_dtypes=True).then_inc(const, 1)
                nc.gpsimd.iota(g.lane[:, 0:1], [[0, 1]], base=NR, channel_multiplier=1,
                               allow_small_or_imprecise_dtypes=True).then_inc(const, 1)
                nc.gpsimd.memset(g.ident[:, :], 0.0).then_inc(const, 1)
                nc.gpsimd.memset(g.lower[:, :], 1.0).then_inc(const, 1)
                nc.gpsimd.memset(g.heads[:, :], 1.0).then_inc(const, 1)
                pool.wait_ge(const, 5)
                nc.gpsimd.affine_select(out=g.ident[:, :], in_=g.ident[:, :], compare_op=ALU.not_equal,
                                        fill=1.0, base=0, pattern=[[-1, P]], channel_multiplier=1).then_inc(const, 1)
                nc.gpsimd.affine_select(out=g.lower[:, :], in_=g.lower[:, :], compare_op=ALU.is_gt,
                                        fill=0.0, base=0, pattern=[[-1, P]], channel_multiplier=1).then_inc(const, 1)
                hv = g.heads[:, 0:D].rearrange("p (h c) -> p h c", h=H)
                nc.gpsimd.affine_select(out=hv, in_=hv, compare_op=ALU.is_equal, fill=0.0, base=0,
                                        pattern=[[-1, H], [0, D // H]], channel_multiplier=1).then_inc(const, 1)
                iv = g.heads[:, D:D + 2 * H].rearrange("p (a h) -> p a h", a=2)
                nc.gpsimd.affine_select(out=iv, in_=iv, compare_op=ALU.is_equal, fill=0.0, base=0,
                                        pattern=[[0, 2], [-1, H]], channel_multiplier=1).then_inc(const, 1)
                pool.wait_ge(const, 9)
                nc.gpsimd.tensor_copy(g.ident16[:, :], g.ident[:, :])

            @block.sync
            def _(sp):
                for d, a in ((g.src_p, g.src), (g.dst_p, g.dst), (g.type_p, g.etype),
                             (g.ew_p, g.ew), (g.ew1_p, g.ew1.rearrange("e o -> (e o)"))):
                    sp.dma_start(d[16:16 + E].rearrange("(a b) -> a b", a=20), a.rearrange("(a b) -> a b", a=20)
                                 ).then_inc(loaded, 16)
                sp.wait_ge(padded, 5)
                for d, p in ((g.src_p, 0), (g.dst_p, 0), (g.type_p, 1)):
                    sp.dma_start(d[16 + E:16 + EP].rearrange("(a b) -> a b", b=4), padi[0:flat // 4, 4 * p:4 * p + 4]
                                 ).then_inc(loaded, 16)
                for d in (g.ew_p, g.ew1_p):
                    sp.dma_start(d[16 + E:16 + EP].rearrange("(a b) -> a b", b=4), padf[0:flat // 4, 0:4]
                                 ).then_inc(loaded, 16)
                for at in (0, 16 + EP):
                    sp.dma_start(g.dst_p[at:at + 16].rearrange("(a b) -> a b", a=4), padi[0:4, 8:12]).then_inc(loaded, 16)
                sp.wait_ge(loaded, 12 * 16)
                for n, (d, off) in enumerate(((g.src_p, 16), (g.dst_p, 16), (g.dst_p, 15), (g.dst_p, 17),
                                              (g.type_p, 16), (g.ew_p, 16), (g.ew1_p, 16))):
                    sp.dma_start(raw[n][:, :, :], d[off:off + EP].rearrange("(g p e) -> p g e", p=P, e=P)
                                 ).then_inc(rows_in, 16)
                sp.wait_ge(stored, 1)
                for n, m in enumerate((g.first_mask, g.last_mask)):
                    sp.dma_start(m[0:EP].rearrange("(g p e) -> p g e", p=P, e=P), mask[:, n, :, :]).then_inc(loaded, 16)
                sp.wait_ge(loaded, 14 * 16)

            @block.scalar
            def _(act):
                act.wait_ge(padded, 6)
                n = 0
                for t in g.sum0 + g.sum1:
                    for part in range(2):
                        act.dma_start(t.rearrange("(p w) d -> p (w d)", p=P)[:, part * zw:(part + 1) * zw],
                                      zero[:, :]).then_inc(zeroed, 16)
                        n += 1
                act.wait_ge(zeroed, 16 * n)

            @block.vector
            def _(dve):
                nc.vector.memset(g.ones[:, :], 1.0).then_inc(padded, 1)
                nc.vector.memset(padi[:, 0:4], N).then_inc(padded, 1)
                nc.vector.memset(padi[:, 4:8], 0).then_inc(padded, 1)
                nc.vector.memset(padi[:, 8:12], -1).then_inc(padded, 1)
                nc.vector.memset(padf[:, :], 0.0).then_inc(padded, 1)
                nc.vector.memset(zero[:, :], 0.0).then_inc(padded, 1)
                nc.vector.memset(g.halves[:, 0:1], 0.5)
                nc.vector.memset(g.halves[:, 1:2], -0.5)
                nc.vector.memset(g.edges[:, SIDX:FIELDS, :], 0.0)
                chain = Chain(dve, step)
                dve.wait_ge(rows_in, 7 * 16)
                for n in range(5):
                    chain(nc.vector.tensor_copy(rows[n][:, :, :], raw[n][:, :, :]))
                chain(nc.vector.tensor_tensor(mask[:, 0], rows[dst_r][:], rows[prev_r][:], ALU.not_equal))
                chain(nc.vector.tensor_tensor(rows[next_r][:], rows[dst_r][:], rows[next_r][:], ALU.not_equal))
                chain(nc.vector.tensor_scalar(mask[:, 1], rows[next_r][:], -BIG, None, ALU.mult))
                nc.vector.tensor_scalar(mask[:, 0], mask[:, 0], -BIG, None, ALU.mult).then_inc(stored, 1)
                bank = 0
                for f, (field, dst) in enumerate(((SRC, None), (None, dstf), (TYPE, None), (EW, None), (EW1, None),
                                                  (END, None))):
                    for b in range(0, EB, 4):
                        w = min(4, EB - b) * P
                        o = dst[:, b * P:b * P + w] if dst is not None else g.edges[:, field, b * P:b * P + w]
                        dve.wait_ge(turned, bank + 1)
                        nc.vector.tensor_copy(o, turn[bank % 2][:, 0:w]).then_inc(copied, 1)
                        bank += 1
                dve.wait_ge(copied, bank)
                nc.vector.tensor_copy(g.base[0:1, :], dstf[0:1, :]).then_inc(copied, 1)
                for n, o in enumerate(range(0, ET, 512)):
                    w = min(512, ET - o)
                    dve.wait_ge(turned, bank + 1 + n)
                    nc.vector.tensor_tensor(g.edges[:, REL, o:o + w], dstf[:, o:o + w], turn[2 + n % 2][:, 0:w],
                                            ALU.subtract).then_inc(copied, 1)
                dve.wait_ge(copied, bank + 5)

            @block.tensor
            def _(pe):
                pe.wait_ge(const, 9)
                pe.wait_ge(step, 7)
                bank = 0
                for src in (rows[src_r], rows[dst_r], rows[type_r], raw[5], raw[6], rows[next_r]):
                    for b in range(0, EB, 4):
                        if bank >= 2:
                            pe.wait_ge(copied, bank - 1)
                        for k in range(b, min(b + 4, EB)):
                            last = nc.tensor.transpose(turn[bank % 2][:, (k - b) * P:(k - b + 1) * P], src[:, k, :],
                                                       g.ident[:, :])
                        last.then_inc(turned, 1)
                        bank += 1
                pe.wait_ge(copied, bank)
                pe.wait_ge(padded, 1)
                for n, o in enumerate(range(0, ET, 512)):
                    w = min(512, ET - o)
                    if n >= 2:
                        pe.wait_ge(copied, bank + 1 + n - 1)
                    nc.tensor.matmul(turn[2 + n % 2][:, 0:w], g.ones[0:1, :], dstf[0:1, o:o + w], start=True,
                                     stop=True).then_inc(turned, 1)


def power(nc, g, pool, asked, given, n, data, exponent):
    pool.wait_ge(asked, n)
    half = g.halves[:, 0:1] if exponent > 0 else g.halves[:, 1:2]
    nc.gpsimd.tensor_tensor(data, data, half.broadcast_to([P, data.shape[1]]), ALU.pow).then_inc(given, 1)


def ask_power(dve, asked, given, n):
    dve.sem_inc(asked, 1)
    dve.wait_ge(given, n)


def layernorm_relu(nc, dve, chain, x, h, sq, stat, asked, given, n=1):
    v = nc.vector
    chain(v.tensor_reduce(stat[:, 0, :], x[:, :, :], AX.X, ALU.add))
    chain(v.tensor_scalar(stat[:, 0, :], stat[:, 0, :], 1.0 / D, None, ALU.mult))
    chain(v.tensor_tensor(h, x[:, :, :], spread(stat[:, 0, :], D), ALU.subtract))
    chain(v.tensor_tensor(sq[:, :, :], h, h, ALU.mult))
    chain(v.tensor_reduce(stat[:, 1, :], sq[:, :, :], AX.X, ALU.add))
    chain(v.tensor_scalar(stat[:, 1, :], stat[:, 1, :], 1.0 / D, 1e-5, ALU.mult, ALU.add))
    ask_power(dve, asked, given, n)
    chain(v.tensor_tensor(h, h, spread(stat[:, 1, :], D), ALU.mult))
    chain(v.tensor_scalar(h, h, 0.0, None, ALU.max))


def nodes_view(t, cols=slice(0, D)):
    return t[0:NR, cols].rearrange("(t p) d -> p t d", p=P)


def begin(nc, g):
    with Phase(nc, "begin") as ph:
        loaded, step, cleared, stored, asked, given = ph.sems("loaded step cleared stored asked given")
        x, sq, stat = ph.sb("x", [P, NT, D]), ph.sb("sq", [P, NT, D]), ph.sb("stat", [P, 2, NT])
        full, rest = N // P, N % P
        with nc.Block() as block:
            @block.sync
            def _(sp):
                sp.wait_ge(cleared, 1)
                sp.dma_start(x[:, 0:full, :], g.x[0:full * P, :].rearrange("(t p) d -> p t d", p=P)).then_inc(loaded, 16)
                sp.dma_start(x[0:rest, full, :], g.x[full * P:N, :]).then_inc(loaded, 16)
                sp.wait_ge(loaded, 32)
                sp.dma_start(nodes_view(g.xs), x[:, :, :]).then_inc(stored, 16)
                sp.wait_ge(stored, 16)

            @block.vector
            def _(dve):
                nc.vector.memset(x[:, full:NT, :], 0.0).then_inc(cleared, 1)
                dve.wait_ge(loaded, 32)
                chain = Chain(dve, step)
                layernorm_relu(nc, dve, chain, x, g.node[:, :, 0:D], sq, stat, asked, given)

            @block.gpsimd
            def _(pool):
                power(nc, g, pool, asked, given, 1, stat[:, 1, :], -0.5)


def project(nc, g, name, weights, width, stores, first=None, dots=None):
    cols = len(weights) * D
    extra = 2 * H if dots else 0
    with Phase(nc, name) as ph:
        (w_in, staged, turned, turned_c, hidden, hidden_c, made, made_c, dotted) = ph.sems(
            "w_in staged turned turned_c hidden hidden_c made made_c dotted")
        step, mark, mark_a = ph.sems("step mark mark_a")
        put = [ph.sem(f"put{s}") for s in range(2)]
        w = ph.sb("w", [D, cols])
        w1 = ph.sb("w1", [D, D])
        b1 = ph.sb("b1", [D, 1])
        av = ph.sb("av", [P, 2, D])
        tmp = ph.sb("tmp", [P, 2, D])
        stage = ph.sb("stage", [P, 2, D])
        ft = ph.sb("ft", [D, 2, P])
        hid = ph.sb("hid", [D, 2, P])
        res = ph.sb("res", [P, 2, cols + extra])
        psf, psh = ([ph.ps(f"{n}{s}", [P, 512])[0:D, 0:P] for s in range(2)] for n in ("psf", "psh"))
        psr = [ph.ps(f"psr{s}", [P, 512]) for s in range(2)]
        last_done = dotted if dots else made_c
        loads = sum(m is not None for m in weights) + (2 if first else 0) + (2 if dots else 0)
        with nc.Block() as block:
            @block.sync
            def _(sp):
                prime(sp, ph, g, put)
                for n, m in enumerate(weights):
                    if m is not None:
                        sp.dma_start(w[:, n * D:(n + 1) * D], m).then_inc(w_in, 16)
                if first:
                    sp.dma_start(w1[:, :], first[0]).then_inc(w_in, 16)
                    sp.dma_start(b1[:, :], first[1].unsqueeze(1)).then_inc(w_in, 16)
                if dots:
                    for n, a in enumerate(dots):
                        sp.dma_start(av[:, n, :], a.rearrange("h c -> (h c)").partition_broadcast(P)).then_inc(w_in, 16)

                def store(t, s, i):
                    sp.wait_ge(last_done, ready(t))
                    for table, tc, rc in stores:
                        sp.dma_start(table[ds(t * P, P), tc], res[:, s, rc]).then_inc(put[s], 16)
                pairs(sp, store, NT)
                for s in range(2):
                    sp.wait_ge(put[s], 16 * len(stores) * (NT // 2) + 16)

            @block.scalar
            def _(act):
                act.sem_inc(staged, 2)
                act.sem_inc(made_c, 2)
                act.sem_inc(hidden_c, 2)

                def head(t, s, i):
                    act.wait_ge(turned, free2(t))
                    alone(act, mark_a)
                    nc.scalar.activation(stage[:, s, :], g.node[:, ds(t, 1), 0:D].rearrange("p o d -> p (o d)"),
                                         ACT.Copy).then_inc(staged, 1)

                def tail(t, s, i):
                    if first:
                        act.wait_ge(hidden, ready(t))
                        act.wait_ge(w_in, 16 * loads)
                        nc.scalar.activation(hid[:, s, :], psh[s], ACT.Identity, bias=b1[:, 0:1]
                                             ).then_inc(hidden_c, 1)
                    act.wait_ge(made, ready(t))
                    act.wait_ge(put[s], 16 * len(stores) * i + 16)
                    nc.scalar.activation(res[:, s, 0:cols], psr[s][:, 0:cols], ACT.Copy).then_inc(made_c, 1)
                skewed(act, head, tail, NT)

            @block.vector
            def _(dve):
                dve.sem_inc(turned_c, 2)
                dve.sem_inc(dotted, 2)
                if dots:
                    dve.wait_ge(w_in, 16 * loads)

                def head(t, s, i):
                    dve.wait_ge(turned, ready(t))
                    dve.wait_ge(hidden if first else made, free2(t))
                    nc.vector.tensor_copy(ft[:, s, :], psf[s]).then_inc(turned_c, 1)

                def tail(t, s, i):
                    if not dots:
                        return
                    dve.wait_ge(made_c, ready(t))
                    chain = Chain(dve, step, t * 2)
                    chain(nc.vector.tensor_tensor(tmp[:, :, :], repeat(res[:, s, 0:D], 2), av[:, :, :], ALU.mult))
                    last = nc.vector.tensor_reduce(
                        res[:, s, D:D + 2 * H].rearrange("p (a h) -> p a h", a=2),
                        tmp[:, :, :].rearrange("p a (h c) -> p a h c", h=H), AX.X, ALU.add)
                    chain(last)
                    dve.sem_inc(dotted, 1)
                skewed(dve, head, tail, NT)

            @block.tensor
            def _(pe):
                for q in (turned, hidden, made):
                    pe.sem_inc(q, 2)

                def head(t, s, i):
                    pe.wait_ge(staged, ready(t))
                    pe.wait_ge(turned_c, free2(t))
                    nc.tensor.matmul(psf[s], stage[:, s, :], g.ident[:, :], start=True, stop=True).then_inc(turned, 1)

                def tail(t, s, i):
                    pe.wait_ge(w_in, 16 * loads)
                    pe.wait_ge(turned_c, ready(t))
                    lhs = ft
                    if first:
                        pe.wait_ge(hidden_c, free2(t))
                        alone(pe, mark)
                        nc.tensor.matmul(psh[s], w1[:, :], ft[:, s, :], start=True, stop=True).then_inc(hidden, 1)
                        pe.wait_ge(hidden_c, ready(t))
                        lhs = hid
                    pe.wait_ge(made_c, free2(t))
                    for n, m in enumerate(weights):
                        wt = g.ident[0:D, 0:D] if m is None else w[:, n * D:(n + 1) * D]
                        last = nc.tensor.matmul(psr[s][:, n * D:(n + 1) * D], lhs[:, s, :], wt, start=True, stop=True)
                    last.then_inc(made, 1)
                skewed(pe, head, tail, NT)


def edges_gcn(nc, g):
    with Phase(nc, "gcn") as ph:
        staged, src_rows, equal, weighted, mixed, mixed_c, summed, summed_c, indexed, scattered = ph.sems(
            "staged src_rows equal weighted mixed mixed_c summed summed_c indexed scattered")
        step, opened = ph.sems("step opened")
        win = [ph.sem(f"win{s}") for s in range(2)]
        half = [ph.sem(f"half{n}") for n in range(2)]
        edge = ph.sb("edge", [P, 2, 3, K])
        table = ph.sb("table", [P, 2, K, D])
        member = ph.sb("member", [P, 2, K, P])
        same = ph.sb("same", [P, 2, K, P])
        before = ph.sb("before", [P, K, P])
        mix = ph.sb("mix", [P, 2, K, P])
        msg = ph.sb("msg", [P, 2, K, D])
        small = ph.sb("small", [P, 2, K])
        index = ph.sb("index", [P, 2, K], I32)
        ps_src, ps_mix = ph.ps("ps_src", [P, K, P]), ph.ps("ps_mix", [P, K, P])
        ps_sum = [ph.ps(f"ps_sum{s}", [P, K, D]) for s in range(2)]
        with nc.Block() as block:
            @block.sync
            def _(sp):
                def load(c, s, i):
                    sp.wait_ge(summed, free2(c))
                    for k, b in enumerate(bases(nc, ENG.SP, g.base, c)):
                        sp.dma_start(table[:, s, k, :], g.gcn_table[ds(b, P), :]).then_inc(win[s], 16)
                pairs(sp, load)

            @block.scalar
            def _(act):
                for q in (staged, mixed_c, summed_c):
                    act.sem_inc(q, 2)

                def first(c, s, i):
                    act.wait_ge(weighted, free2(c))
                    act.wait_ge(indexed, free2(c))
                    nc.scalar.activation(edge[:, s, :, :], g.edges[:, SRC:EW + 1, ds(c * K, K)], ACT.Copy
                                         ).then_inc(staged, 1)

                def second(c, s, i):
                    act.wait_ge(mixed, ready(c))
                    act.wait_ge(summed, free2(c))
                    for h in range(2):
                        last = nc.scalar.activation(mix[:, s, 4 * h:4 * h + 4, :], ps_mix[:, 4 * h:4 * h + 4, :], ACT.Copy)
                    last.then_inc(mixed_c, 1)
                    act.wait_ge(summed, ready(c))
                    act.wait_ge(scattered, c + 2)
                    nc.scalar.activation(msg[:, s, :, :], ps_sum[s][:, :, :], ACT.Copy).then_inc(summed_c, 1)
                skewed(act, first, second)

            @block.vector
            def _(dve):
                for q in (equal, weighted, indexed):
                    dve.sem_inc(q, 2)

                def body(c, s, i):
                    v = nc.vector
                    chain = Chain(dve, step, c * 6)
                    dve.wait_ge(staged, ready(c))
                    dve.wait_ge(mixed, free2(c))
                    v.tensor_tensor(member[:, s], repeat(g.iota[:, :], K), spread(edge[:, s, REL, :], P), ALU.is_equal)
                    dve.wait_ge(src_rows, ready(c))
                    v.tensor_tensor(same[:, s], ps_src[:, :, :], spread(edge[:, s, SRC, :], P), ALU.is_equal
                                    ).then_inc(equal, 1)
                    dve.wait_ge(equal, ready(c))
                    chain(v.tensor_tensor(before[:, :, :], same[:, s], repeat(g.lower[:, :], K), ALU.mult))
                    v.tensor_tensor(same[:, s], same[:, s], spread(edge[:, s, EW, :], P), ALU.mult).then_inc(weighted, 1)
                    chain(v.tensor_reduce(small[:, 0, :], before[:, :, :], AX.X, ALU.add))
                    chain(v.tensor_scalar(small[:, 1, :], edge[:, s, SRC, :], -1.0, g.lane[:, 0:1], ALU.mult, ALU.add))
                    chain(v.scalar_tensor_tensor(small[:, 0, :], small[:, 0, :], 1.0, small[:, 1, :], ALU.min, ALU.mult))
                    dve.wait_ge(scattered, c + 2)
                    chain(v.tensor_tensor(index[:, s, :], small[:, 0, :], edge[:, s, SRC, :], ALU.add))
                    chain(v.tensor_copy(g.edges[:, SIDX, ds(c * K, K)], index[:, s, :]))
                    dve.sem_inc(indexed, 1)
                pairs(dve, body)

            @block.tensor
            def _(pe):
                for q in (src_rows, mixed, summed):
                    pe.sem_inc(q, 2)

                def first(c, s, i):
                    pe.wait_ge(staged, ready(c))
                    pe.wait_ge(equal, free1(c))
                    for k in range(K):
                        last = nc.tensor.transpose(ps_src[:, k, :], edge[:, s, SRC, k:k + 1].broadcast_to([P, P]),
                                                   g.ident[:, :])
                    last.then_inc(src_rows, 1)

                def second(c, s, i):
                    pe.wait_ge(weighted, ready(c))
                    pe.wait_ge(mixed_c, free1(c))
                    for k in range(K):
                        last = nc.tensor.matmul(ps_mix[:, k, :], member[:, s, k, :], same[:, s, k, :], start=True, stop=True)
                    last.then_inc(mixed, 1)
                    pe.wait_ge(mixed_c, ready(c))
                    pe.wait_ge(win[s], 16 * K * (i + 1))
                    pe.wait_ge(summed_c, free2(c))
                    for k in range(K):
                        last = nc.tensor.matmul(ps_sum[s][:, k, :], mix[:, s, k, :], table[:, s, k, :], start=True, stop=True)
                    last.then_inc(summed, 1)
                skewed(pe, first, second)

            @block.gpsimd
            def _(pool):
                pool.sem_inc(scattered, 2)
                prime(pool, ph, g, half)

                def body(c, s, i):
                    pool.wait_ge(summed_c, ready(c))
                    pool.wait_ge(indexed, ready(c))
                    scatter(nc, pool, g.sum0, msg[:, s], index[:, s], c, half, opened, scattered)
                pairs(pool, body)
                for h in range(2):
                    pool.wait_ge(half[h], 64 * CHUNKS + 16)


def prime(eng, ph, g, sems):
    spot = ph.sb("prime", [1, len(sems), 16])
    for n, sem in enumerate(sems):
        eng.dma_start(spot[0:1, n, :], g.w["L0_gnn_bias"][16 * n:16 * n + 16].unsqueeze(0)).then_inc(sem, 16)


def scatter(nc, pool, copies, msg, index, c, half, opened, scattered):
    for h, sem in enumerate((opened, scattered)):
        pool.wait_ge(half[h], c * 64 + 16)
        pool.sem_inc(sem, 1)
        for k in range(4 * h, 4 * h + 4):
            nc.gpsimd.indirect_dma_start(copies[k][:, :], bass.IndirectOffsetOnAxis(ap=index[:, k:k + 1], axis=0),
                                         msg[:, k, :], None, compute_op=ALU.add).then_inc(half[h], 16)


def after_gcn(nc, g):
    with Phase(nc, "gcn_end") as ph:
        loaded, used, step, stored, done, asked, given = ph.sems("loaded used step stored done asked given")
        part_in = [ph.sem(f"part{n}") for n in range(2)]
        x, total, stat = ph.sb("x", [P, NT, D]), ph.sb("total", [P, NT, D]), ph.sb("stat", [P, 2, NT])
        part = [ph.sb(f"part{n}", [P, NT, D]) for n in range(2)]
        bias = ph.sb("bias", [P, D])
        with nc.Block() as block:
            @block.sync
            def _(sp):
                sp.dma_start(x[:, :, :], nodes_view(g.xs)).then_inc(loaded, 16)
                sp.dma_start(bias[:, :], g.w["L0_gnn_bias"].partition_broadcast(P)).then_inc(loaded, 16)
                sum_loads(sp, g.sum0, part, part_in, used)
                sp.wait_ge(done, 1)
                sp.dma_start(nodes_view(g.xs), x[:, :, :]).then_inc(stored, 16)
                sp.wait_ge(stored, 16)

            @block.vector
            def _(dve):
                sum_adds(nc, dve, total, part, part_in, used)
                chain = Chain(dve, step)
                dve.wait_ge(loaded, 32)
                chain(nc.vector.tensor_tensor(total[:, :, :], total[:, :, :], repeat(bias[:, :], NT), ALU.add))
                chain(nc.vector.tensor_scalar(total[:, :, :], total[:, :, :], 0.0, None, ALU.max))
                chain(nc.vector.tensor_tensor(x[:, :, :], x[:, :, :], total[:, :, :], ALU.add))
                dve.sem_inc(done, 1)
                layernorm_relu(nc, dve, chain, x, g.node[:, :, 0:D], total, stat, asked, given)

            @block.gpsimd
            def _(pool):
                power(nc, g, pool, asked, given, 1, stat[:, 1, :], -0.5)


def sum_loads(sp, target, part, part_in, used):
    for n in range(COPIES):
        if n >= 2:
            sp.wait_ge(used, n - 1)
        sp.dma_start(part[n % 2][:, :, :], nodes_view(target[n])).then_inc(part_in[n % 2], 16)


def sum_adds(nc, dve, total, part, part_in, used):
    for n in range(COPIES):
        s = n % 2
        dve.wait_ge(part_in[s], 16 * (n // 2 + 1))
        if n == 0:
            nc.vector.tensor_copy(total[:, :, :], part[s][:, :, :]).then_inc(used, 1)
        else:
            nc.vector.tensor_tensor(total[:, :, :], total[:, :, :], part[s][:, :, :], ALU.add).then_inc(used, 1)
        dve.wait_ge(used, n + 1)


def acosh_argument(nc, v, chain, z, t, q):
    chain(v.tensor_scalar(z, z, ACOSH_MIN, None, ALU.max))
    chain(v.tensor_scalar(t, z, 1.0, None, ALU.subtract))
    chain(v.scalar_tensor_tensor(q, z, 1.0, t, ALU.add, ALU.mult))


def hyperbolic_in(nc, g):
    with Phase(nc, "log") as ph:
        step, ready_x, stored, asked, given, logs = ph.sems("step ready_x stored asked given logs")
        sq, stat = ph.sb("sq", [P, NT, D]), ph.sb("stat", [P, 5, NT])
        x = g.node
        d, t, q, yn = (stat[:, n, :] for n in range(4))
        with nc.Block() as block:
            @block.sync
            def _(sp):
                sp.dma_start(nodes_view(g.hyp_src, slice(D, 2 * D)), x[:, :, 0:D]).then_inc(stored, 16)
                sp.wait_ge(ready_x, 1)
                sp.dma_start(nodes_view(g.hyp_dst), sq[:, :, :]).then_inc(stored, 16)
                sp.wait_ge(stored, 32)

            @block.gpsimd
            def _(pool):
                power(nc, g, pool, asked, given, 1, q, 0.5)
                power(nc, g, pool, asked, given, 2, yn, 0.5)

            @block.scalar
            def _(act):
                act.wait_ge(ready_x, 2)
                nc.scalar.activation(d, t, ACT.Ln, bias=1.0).then_inc(logs, 1)

            @block.vector
            def _(dve):
                v = nc.vector
                chain = Chain(dve, step)
                chain(v.tensor_tensor(sq[:, :, :], x[:, :, 0:D], x[:, :, 0:D], ALU.mult))
                chain(v.tensor_reduce(yn, sq[:, :, 1:D], AX.X, ALU.add))
                chain(v.tensor_scalar(sq[:, :, :], x[:, :, 0:D], -1.0, None, ALU.mult))
                chain(v.tensor_copy(sq[:, :, 0:1], x[:, :, 0:1]))
                dve.sem_inc(ready_x, 1)
                chain(v.tensor_copy(d.unsqueeze(2), x[:, :, 0:1]))
                acosh_argument(nc, v, chain, d, t, q)
                ask_power(dve, asked, given, 1)
                chain(v.tensor_tensor(t, t, q, ALU.add))
                dve.sem_inc(ready_x, 1)
                ask_power(dve, asked, given, 2)
                chain(v.tensor_scalar(yn, yn, 1e-7, None, ALU.max))
                chain(v.reciprocal(yn, yn))
                dve.wait_ge(logs, 1)
                chain(v.tensor_tensor(d, d, yn, ALU.mult))
                dve.wait_ge(stored, 32)
                chain(v.tensor_tensor(x[:, :, 0:D], x[:, :, 0:D], spread(d, D), ALU.mult))
                chain(v.memset(x[:, :, 0:1], 0.0))


def edges_hyperbolic(nc, g):
    w = g.w
    with Phase(nc, "hyp") as ph:
        (staged, gather_at, members, turned, turned_c, dst_x, dst_h, taken, squared, logged, rooted, argued, geo,
         joined, src_rows, equal, counted, count_c) = ph.sems(
            "staged gather_at members turned turned_c dst_x dst_h taken squared logged rooted argued geo "
            "joined src_rows equal counted count_c")
        (pre, act1, pre2, act2, score, tanh, weighted, summed, summed_c, opened, scattered, w_in,
         step_a, step_b, added, cleared, mark_a, mark_p) = ph.sems(
            "pre act1 pre2 act2 score tanh weighted summed summed_c opened scattered w_in "
            "step_a step_b added cleared mark_a mark_p")
        win = [ph.sem(f"win{s}") for s in range(2)]
        got = [ph.sem(f"got{s}") for s in range(2)]
        half = [ph.sem(f"half{n}") for n in range(2)]
        edge = ph.sb("edge", [P, 2, SIDX + 1, K])
        src_at, sum_at = ph.sb("src_at", [P, 2, K], I32), ph.sb("sum_at", [P, 2, K], I32)
        table = ph.sb("table", [P, 2, K, 3 * D])
        from_src = ph.sb("from_src", [P, 2, K, 2 * D])
        member, memberT = ph.sb("member", [P, K, P], BF16), ph.sb("memberT", [P, K, P])
        same = ph.sb("same", [P, 2, K, P])
        kinds = ph.sb("kinds", [P, K, R], BF16)
        hid = ph.sb("hid", [D, 2, K, P])
        part = ph.sb("part", [P, K, D])
        msg = ph.sb("msg", [P, 2, K, D])
        prod = ph.sb("prod", [P, K, D])
        small = ph.sb("small", [P, 6, K])
        lq, rt, dist, th = (ph.sb(n, [P, K]) for n in ("lq", "rt", "dist", "th"))
        counts = ph.sb("counts", [R, NR])
        w2, w3 = ph.sb("w2", [D, D]), ph.sb("w3", [D, 1])
        b1, b2 = ph.sb("b1", [D, 1]), ph.sb("b2", [D, 1])
        b3 = ph.sb("b3", [P, 2])
        wc = ph.sb("wc", [P, 2, D])
        ps_src, ps_mlp = (ph.ps(n, [P, K, P]) for n in ("ps_src", "ps_mlp"))
        ps_turn = ph.ps("ps_turn", [P, K, P], BF16)
        ps_x, ps_q, ps_h = (ph.ps(n, [P, K, D]) for n in ("ps_x", "ps_q", "ps_h"))
        ps_cnt, ps_pre = ps_src[0:R], ps_mlp[0:D]
        ps_score = ps_mlp[:, 4, 0:K]
        ps_sum = ps_mlp[:, 0:4, :].rearrange("p k (a d) -> p (k a) d", d=D)

        def half_ready(c, h):
            return 2 * c + h + 5

        with nc.Block() as block:
            @block.sync
            def _(sp):
                for d, a in ((w2, w["L1_gnn_w2"]), (w3, w["L1_gnn_w3"]), (b1, w["L1_gnn_b1"].unsqueeze(1)),
                             (b2, w["L1_gnn_b2"].unsqueeze(1))):
                    sp.dma_start(d[:, :], a).then_inc(w_in, 16)
                sp.dma_start(b3[:, 0:1], w["L1_gnn_b3"].partition_broadcast(P)).then_inc(w_in, 16)
                for n in range(2):
                    sp.dma_start(wc[:, n, :], w["L1_gnn_w1"][2 * D + n, :].partition_broadcast(P)).then_inc(w_in, 16)

                def load(c, s, i):
                    sp.wait_ge(dst_h, free2(c))
                    for k, b in enumerate(bases(nc, ENG.SP, g.base, c)):
                        sp.dma_start(table[:, s, k, :], g.hyp_dst[ds(b, P), :]).then_inc(win[s], 16)
                pairs(sp, load)

            @block.gpsimd
            def _(pool):
                pool.sem_inc(scattered, 2)
                prime(pool, ph, g, half)

                def gather(c, s, i):
                    pool.wait_ge(pre, half_ready(c, 0) - 3)
                    pool.wait_ge(gather_at, ready(c))
                    pool.sem_inc(opened, 1)
                    for k in range(K):
                        nc.gpsimd.indirect_dma_start(
                            from_src[:, s, k, :], None, g.hyp_src[:, :],
                            bass.IndirectOffsetOnAxis(ap=src_at[:, s, k:k + 1], axis=0)).then_inc(got[s], 16)

                def send(c, s, i):
                    pool.wait_ge(summed_c, ready(c))
                    scatter(nc, pool, g.sum1, msg[:, s], sum_at[:, s], c, half, opened, scattered)
                skewed(pool, gather, send)
                for h in range(2):
                    pool.wait_ge(half[h], 64 * CHUNKS + 16)

            @block.scalar
            def _(act):
                for q in (staged, gather_at, turned_c, logged, rooted, geo, tanh, summed_c):
                    act.sem_inc(q, 2)
                for q in (act1, act2):
                    act.sem_inc(q, 4)
                act.wait_ge(w_in, 7 * 16)
                nc.scalar.activation(b3[:, 1:2], b3[:, 0:1], ACT.Copy, scale=0.5).then_inc(added, 1)
                act.wait_ge(added, 1)

                def fields(c, s, i):
                    act.wait_ge(weighted, free2(c))
                    alone(act, mark_a)
                    nc.scalar.activation(edge[:, s, :, :], g.edges[:, 0:SIDX + 1, ds(c * K, K)], ACT.Copy
                                         ).then_inc(staged, 1)
                    nc.scalar.activation(src_at[:, s, :], g.edges[:, SRC, ds(c * K, K)], ACT.Copy
                                         ).then_inc(gather_at, 1)

                def turn_out(c, s, i):
                    act.wait_ge(turned, ready(c))
                    act.wait_ge(dst_h, free1(c))
                    nc.scalar.activation(memberT[:, :, :], ps_turn[:, :, :], ACT.Copy).then_inc(turned_c, 1)

                def distance(c, s, i):
                    act.wait_ge(squared, ready(c))
                    nc.scalar.activation(lq[:, :], small[:, 2, :], ACT.Ln).then_inc(logged, 1)
                    act.wait_ge(logged, ready(c))
                    nc.scalar.activation(rt[:, :], lq[:, :], ACT.Exp, scale=0.5).then_inc(rooted, 1)
                    act.wait_ge(argued, ready(c))
                    nc.scalar.activation(dist[:, :], small[:, 3, :], ACT.Ln, bias=1.0).then_inc(geo, 1)

                def layer(c, n, bias, done_in, done_out, used):
                    for h in range(2):
                        act.wait_ge(done_in, half_ready(c, h))
                        act.wait_ge(used, half_ready(c, h) - 2)
                        nc.scalar.activation(hid[:, n, 4 * h:4 * h + 4, :], ps_pre[:, 4 * h:4 * h + 4, :], ACT.Silu,
                                             bias=bias[:, 0:1]).then_inc(done_out, 1)

                def attention(c, s, i):
                    act.wait_ge(score, half_ready(c, 1))
                    act.wait_ge(weighted, free1(c))
                    nc.scalar.activation(th[:, :], ps_score, ACT.Tanh, scale=0.5, bias=b3[:, 1:2]).then_inc(tanh, 1)

                def out(c, s, i):
                    act.wait_ge(summed, ready(c))
                    act.wait_ge(scattered, c + 2)
                    alone(act, mark_a)
                    nc.scalar.activation(sum_at[:, s, :], g.edges[:, SIDX, ds(c * K, K)], ACT.Copy)
                    nc.scalar.activation(msg[:, s, :, :], ps_sum, ACT.Copy).then_inc(summed_c, 1)

                def turn(c, s, i, c1, s1, i1):
                    if c1 is not None:
                        fields(c1, s1, i1)
                    layer(c, 0, b1, pre, act1, pre2)
                    layer(c, 1, b2, pre2, act2, score)
                    if c1 is not None:
                        turn_out(c1, s1, i1)
                    attention(c, s, i)
                    out(c, s, i)
                    if c1 is not None:
                        distance(c1, s1, i1)

                fields(0, 0, 0)
                turn_out(0, 0, 0)
                distance(0, 0, 0)
                turns(act, turn)

            @block.vector
            def _(dve):
                v = nc.vector
                for q in (members, equal, squared, taken, argued, joined, weighted, count_c):
                    dve.sem_inc(q, 2)
                v.memset(counts[:, :], 0.0).then_inc(cleared, 1)
                dve.wait_ge(cleared, 1)
                dve.wait_ge(w_in, 7 * 16)

                def zero_ones(c, s, i):
                    e = edge[:, s]
                    dve.wait_ge(staged, ready(c))
                    dve.wait_ge(counted, free1(c))
                    v.tensor_tensor(member[:, :, :], repeat(g.iota[:, :], K), spread(e[:, REL, :], P), ALU.is_equal
                                    ).then_inc(members, 1)
                    v.tensor_tensor(kinds[:, :, :], repeat(g.iota[:, 0:R], K), spread(e[:, TYPE, :], R), ALU.is_equal)
                    dve.wait_ge(src_rows, ready(c))
                    dve.wait_ge(summed, free2(c))
                    v.tensor_tensor(same[:, s], ps_src[:, :, :], spread(e[:, SRC, :], P), ALU.is_equal).then_inc(equal, 1)

                def inputs(c, s, i):
                    chain = Chain(dve, step_a, c * 20)
                    e = edge[:, s]
                    row = from_src[:, s, :, 0:D]
                    dve.wait_ge(dst_x, ready(c))
                    dve.wait_ge(got[s], 16 * K * (i + 1))
                    chain(v.tensor_tensor(prod[:, :, :], ps_x[:, :, :], from_src[:, s, :, D:2 * D], ALU.mult))
                    chain(v.tensor_reduce(small[:, 0, :], prod[:, :, :], AX.X, ALU.add))
                    acosh_argument(nc, v, chain, small[:, 0, :], small[:, 1, :], small[:, 2, :])
                    dve.sem_inc(squared, 1)
                    chain(v.tensor_tensor(row, row, ps_q[:, :, :], ALU.add))
                    dve.sem_inc(taken, 1)
                    chain(v.tensor_tensor(prod[:, :, :], spread(e[:, EW1, :], D), repeat(wc[:, 0, :], K), ALU.mult))
                    dve.wait_ge(rooted, ready(c))
                    chain(v.tensor_tensor(small[:, 3, :], small[:, 1, :], rt[:, :], ALU.add))
                    dve.sem_inc(argued, 1)
                    chain(v.tensor_tensor(row, row, prod[:, :, :], ALU.add))
                    dve.wait_ge(geo, ready(c))
                    chain(v.tensor_tensor(prod[:, :, :], spread(dist[:, :], D), repeat(wc[:, 1, :], K), ALU.mult))
                    chain(v.tensor_tensor(row, row, prod[:, :, :], ALU.add))
                    dve.sem_inc(joined, 1)
                    dve.wait_ge(counted, ready(c))
                    for k, b in enumerate(bases(nc, ENG.DVE, g.base, c)):
                        chain(v.tensor_tensor(counts[:, ds(b, P)], counts[:, ds(b, P)], ps_cnt[:, k, :], ALU.add))
                    dve.sem_inc(count_c, 1)
                    assert chain.n == 19
                    dve.sem_inc(step_a, 1)

                def messages(c, s, i):
                    chain = Chain(dve, step_b, c * 2)
                    dve.wait_ge(tanh, ready(c))
                    chain(v.tensor_scalar(small[:, 4, :], th[:, :], 0.5, 0.5, ALU.mult, ALU.add))
                    chain(v.tensor_tensor(small[:, 5, :], small[:, 4, :], edge[:, s, EW1, :], ALU.mult))
                    dve.wait_ge(dst_h, ready(c))
                    dve.wait_ge(summed, free1(c))
                    v.tensor_tensor(part[:, :, :], ps_h[:, :, :], spread(small[:, 5, :], D), ALU.mult
                                    ).then_inc(weighted, 1)

                def turn(c, s, i, c1, s1, i1):
                    if c1 is not None:
                        zero_ones(c1, s1, i1)
                    messages(c, s, i)
                    if c1 is not None:
                        inputs(c1, s1, i1)

                zero_ones(0, 0, 0)
                inputs(0, 0, 0)
                turns(dve, turn)

            @block.tensor
            def _(pe):
                for q in (turned, dst_x, dst_h, src_rows, counted, summed):
                    pe.sem_inc(q, 2)
                for q in (pre, pre2, score):
                    pe.sem_inc(q, 4)
                pe.wait_ge(w_in, 7 * 16)

                def source_rows(c, s, i):
                    pe.wait_ge(staged, ready(c))
                    pe.wait_ge(count_c, free1(c))
                    for k in range(K):
                        last = nc.tensor.transpose(ps_src[:, k, :], edge[:, s, SRC, k:k + 1].broadcast_to([P, P]),
                                                   g.ident[:, :])
                    last.then_inc(src_rows, 1)

                def turn_members(c, s, i):
                    pe.wait_ge(members, ready(c))
                    pe.wait_ge(turned_c, free1(c))
                    for k in range(K):
                        last = nc.tensor.transpose(ps_turn[:, k, :], member[:, k, :], g.ident16[:, :])
                    last.then_inc(turned, 1)

                def count(c, s, i):
                    pe.wait_ge(equal, ready(c))
                    for k in range(K):
                        last = nc.tensor.matmul(ps_cnt[:, k, :], kinds[:, k, :], member[:, k, :], start=True, stop=True)
                    last.then_inc(counted, 1)

                def from_dst(c, s, i):
                    pe.wait_ge(turned_c, ready(c))
                    pe.wait_ge(win[s], 16 * K * (i + 1))
                    pe.wait_ge(taken, free1(c))
                    for n, ps in enumerate((ps_x, ps_q)):
                        for k in range(K):
                            last = nc.tensor.matmul(ps[:, k, :], memberT[:, k, :], table[:, s, k, n * D:(n + 1) * D],
                                                    start=True, stop=True)
                    last.then_inc(dst_x, 1)

                def h_from_dst(c, s, i):
                    pe.wait_ge(weighted, free1(c))
                    for k in range(K):
                        last = nc.tensor.matmul(ps_h[:, k, :], memberT[:, k, :], table[:, s, k, 2 * D:3 * D], start=True,
                                                stop=True)
                    last.then_inc(dst_h, 1)

                def layer1(c, s, i):
                    pe.wait_ge(joined, ready(c))
                    pe.wait_ge(summed_c, free1(c))
                    alone(pe, mark_p)
                    for h in range(2):
                        for k in range(4 * h, 4 * h + 4):
                            last = nc.tensor.transpose(ps_pre[:, k, :], from_src[:, s, k, 0:D], g.ident[:, :])
                        last.then_inc(pre, 1)

                def layer2(c, s, i):
                    for h in range(2):
                        pe.wait_ge(act1, half_ready(c, h))
                        alone(pe, mark_p)
                        nc.tensor.matmul(ps_pre[:, 4 * h:4 * h + 4, :], w2[:, :], hid[:, 0, 4 * h:4 * h + 4, :],
                                         start=True, stop=True).then_inc(pre2, 1)

                def scores(c, s, i):
                    pe.wait_ge(act2, half_ready(c, 1))
                    for h in range(2):
                        for k in range(4 * h, 4 * h + 4):
                            last = nc.tensor.matmul(ps_score[:, k:k + 1], hid[:, 1, k, :], w3[:, :], start=True, stop=True)
                        last.then_inc(score, 1)

                def combine(c, s, i):
                    pe.wait_ge(weighted, ready(c))
                    for k in range(K):
                        last = nc.tensor.matmul(ps_sum[:, k, :], same[:, s, k, :], part[:, k, :], start=True, stop=True)
                    last.then_inc(summed, 1)

                def turn(c, s, i, c1, s1, i1):
                    layer1(c, s, i)
                    if c1 is not None:
                        source_rows(c1, s1, i1)
                    layer2(c, s, i)
                    if c1 is not None:
                        turn_members(c1, s1, i1)
                    scores(c, s, i)
                    if c1 is not None:
                        count(c1, s1, i1)
                        from_dst(c1, s1, i1)
                    combine(c, s, i)
                    if c1 is not None:
                        h_from_dst(c1, s1, i1)

                source_rows(0, 0, 0)
                turn_members(0, 0, 0)
                count(0, 0, 0)
                from_dst(0, 0, 0)
                h_from_dst(0, 0, 0)
                turns(pe, turn)

        columns_to_nodes(nc, g, ph, counts, R, [t[:, :, :].rearrange("p k d -> p (k d)") for t in (ps_x, ps_q)])
        with nc.Block() as block:
            @block.vector
            def _(dve):
                chain = Chain(dve, cleared, 1)
                chain(nc.vector.tensor_scalar(g.node[:, :, 0:R], g.node[:, :, 0:R], 1.0, None, ALU.max))
                chain(nc.vector.reciprocal(g.node[:, :, 0:R], g.node[:, :, 0:R]))

            @block.sync
            def _(sp):
                sp.wait_ge(cleared, 3)
                sp.dma_start(nodes_view(g.inv_count, slice(0, R)), g.node[:, :, 0:R]).then_inc(w_in, 16)
                sp.wait_ge(w_in, 8 * 16)


def columns_to_nodes(nc, g, outer, sums, rows, ps):
    with Phase(nc, outer.name + "_turn") as ph:
        staged, turned, copied, mark_a, mark_p, mark_d = ph.sems("staged turned copied mark_a mark_p mark_d")
        stage = ph.sb("stage", [rows, 2, P])
        with nc.Block() as block:
            @block.scalar
            def _(act):
                act.sem_inc(staged, 2)

                def body(t, s, i):
                    act.wait_ge(turned, free2(t))
                    alone(act, mark_a)
                    nc.scalar.activation(stage[:, s, :], sums[0:rows, ds(t * P, P)], ACT.Copy).then_inc(staged, 1)
                pairs(act, body, NT)

            @block.tensor
            def _(pe):
                pe.sem_inc(turned, 2)

                def body(t, s, i):
                    pe.wait_ge(staged, ready(t))
                    pe.wait_ge(copied, free2(t))
                    alone(pe, mark_p)
                    nc.tensor.matmul(ps[s][:, 0:rows], stage[:, s, :], g.ident[0:rows, 0:rows], start=True, stop=True
                                     ).then_inc(turned, 1)
                pairs(pe, body, NT)

            @block.vector
            def _(dve):
                dve.sem_inc(copied, 2)

                def body(t, s, i):
                    dve.wait_ge(turned, ready(t))
                    alone(dve, mark_d)
                    nc.vector.tensor_copy(g.node[:, ds(t, 1), 0:rows].rearrange("p o r -> p (o r)"), ps[s][:, 0:rows]
                                          ).then_inc(copied, 1)
                pairs(dve, body, NT)


def after_hyperbolic(nc, g):
    with Phase(nc, "hyp_end") as ph:
        loaded, used, step, stored, done, asked, given, acted = ph.sems("loaded used step stored done asked given acted")
        part_in = [ph.sem(f"part{n}") for n in range(2)]
        x, y, stat = ph.sb("x", [P, NT, D]), ph.sb("y", [P, NT, D]), ph.sb("stat", [P, 4, NT])
        part = [ph.sb(f"part{n}", [P, NT, D]) for n in range(2)]
        gamma, beta = ph.sb("gamma", [P, D]), ph.sb("beta", [P, D])
        h = g.node[:, :, 0:D]
        with nc.Block() as block:
            @block.sync
            def _(sp):
                sp.dma_start(x[:, :, :], nodes_view(g.xs)).then_inc(loaded, 16)
                sp.dma_start(h, nodes_view(g.hyp_dst, slice(2 * D, 3 * D))).then_inc(loaded, 16)
                sp.dma_start(gamma[:, :], g.w["L1_gnn_gamma"].partition_broadcast(P)).then_inc(loaded, 16)
                sp.dma_start(beta[:, :], g.w["L1_gnn_beta"].partition_broadcast(P)).then_inc(loaded, 16)
                sum_loads(sp, g.sum1, part, part_in, used)
                sp.wait_ge(done, 4)
                sp.dma_start(nodes_view(g.xs), x[:, :, :]).then_inc(stored, 16)
                sp.wait_ge(stored, 16)

            @block.gpsimd
            def _(pool):
                power(nc, g, pool, asked, given, 1, stat[:, 1, :], -0.5)
                power(nc, g, pool, asked, given, 2, stat[:, 2, :], 0.5)
                power(nc, g, pool, asked, given, 3, stat[:, 1, :], -0.5)

            @block.scalar
            def _(act):
                act.wait_ge(done, 2)
                nc.scalar.activation(stat[:, 3, :], stat[:, 2, :], ACT.Tanh, scale=0.5).then_inc(acted, 1)
                act.wait_ge(done, 3)
                nc.scalar.activation(y[:, :, :], y[:, :, :], ACT.Silu).then_inc(acted, 1)

            @block.vector
            def _(dve):
                v = nc.vector
                sum_adds(nc, dve, y, part, part_in, used)
                chain = Chain(dve, step)
                dve.wait_ge(loaded, 64)
                chain(v.tensor_tensor(y[:], y[:], h, ALU.add))
                chain(v.tensor_reduce(stat[:, 0, :], y[:], AX.X, ALU.add))
                chain(v.tensor_scalar(stat[:, 0, :], stat[:, 0, :], 1.0 / D, None, ALU.mult))
                chain(v.tensor_tensor(y[:], y[:], spread(stat[:, 0, :], D), ALU.subtract))
                chain(v.tensor_tensor(part[0][:], y[:], y[:], ALU.mult))
                chain(v.tensor_reduce(stat[:, 1, :], part[0][:], AX.X, ALU.add))
                chain(v.tensor_scalar(stat[:, 1, :], stat[:, 1, :], 1.0 / D, 1e-5, ALU.mult, ALU.add))
                ask_power(dve, asked, given, 1)
                chain(v.tensor_tensor(y[:], y[:], spread(stat[:, 1, :], D), ALU.mult))
                chain(v.tensor_tensor(y[:], y[:], repeat(gamma[:, :], NT), ALU.mult))
                chain(v.tensor_tensor(y[:], y[:], repeat(beta[:, :], NT), ALU.add))
                chain(v.tensor_tensor(part[0][:], y[:], y[:], ALU.mult))
                chain(v.tensor_reduce(stat[:, 2, :], part[0][:, :, 1:D], AX.X, ALU.add))
                ask_power(dve, asked, given, 2)
                chain(v.tensor_scalar(stat[:, 2, :], stat[:, 2, :], 1e-7, None, ALU.max))
                dve.sem_inc(done, 2)
                chain(v.reciprocal(stat[:, 0, :], stat[:, 2, :]))
                dve.wait_ge(acted, 1)
                chain(v.tensor_tensor(stat[:, 0, :], stat[:, 0, :], stat[:, 3, :], ALU.mult))
                chain(v.tensor_tensor(y[:], y[:], spread(stat[:, 0, :], D), ALU.mult))
                dve.sem_inc(done, 1)
                dve.wait_ge(acted, 2)
                chain(v.tensor_tensor(part[0][:], y[:], y[:], ALU.mult))
                chain(v.tensor_reduce(stat[:, 0, :], part[0][:, :, 1:D], AX.X, ALU.add))
                chain(v.tensor_scalar(stat[:, 1, :], stat[:, 0, :], -1.0, 1.0, ALU.mult, ALU.add))
                chain(v.tensor_scalar(stat[:, 1, :], stat[:, 1, :], 1e-7, None, ALU.max))
                chain(v.reciprocal(stat[:, 1, :], stat[:, 1, :]))
                chain(v.tensor_scalar(stat[:, 0, :], stat[:, 0, :], 1.0, None, ALU.add))
                chain(v.tensor_tensor(y[:], y[:], spread(stat[:, 1, :], D), ALU.mult))
                chain(v.tensor_scalar(y[:], y[:], 2.0, None, ALU.mult))
                chain(v.tensor_tensor(y[:, :, 0:1], stat[:, 0, :].unsqueeze(2), stat[:, 1, :].unsqueeze(2), ALU.mult))
                chain(v.tensor_tensor(x[:], x[:], y[:], ALU.add))
                layernorm_relu(nc, dve, chain, x, h, y, stat, asked, given, 3)
                dve.sem_inc(done, 1)


def edges_attention(nc, g, name):
    with Phase(nc, name) as ph:
        (staged, gather_at, members, turned, turned_c, dst_at, logit, logit_t, scanned, back, back_u, expo,
         shift_e, shift_p, shifted, filled, summed, added) = ph.sems(
            "staged gather_at members turned turned_c dst_at logit logit_t scanned back back_u expo "
            "shift_e shift_p shifted filled summed added")
        step_a, step_b, opened, cleared, mark_a, mark_p = ph.sems("step_a step_b opened cleared mark_a mark_p")
        win = [ph.sem(f"win{s}") for s in range(2)]
        got = [ph.sem(f"got{s}") for s in range(2)]
        rows = D + 2 * H
        edge = ph.sb("edge", [P, 2, END + 1, K])
        src_at = ph.sb("src_at", [P, 2, K], I32)
        table = ph.sb("table", [P, 2, K, H])
        masks = ph.sb("masks", [H, 2, 2, CE])
        from_src = ph.sb("from_src", [P, 2, K, D + H])
        spot = g.node[:, :, :].rearrange("p t d -> p (t d)")
        member, memberT = (spot[:, n * 2 * CE:(n + 1) * 2 * CE].rearrange("p (s k e) -> p s k e", s=2, k=K)
                           for n in range(2))
        leaky = ph.sb("leaky", [P, 2, K, H])
        fwd, top = ph.sb("fwd", [H, 2, CE]), ph.sb("top", [H, CE])
        arg = ph.sb("arg", [P, K, H])
        shift = ph.sb("shift", [H, 2])
        msg = ph.sb("msg", [P, 2, K, rows])
        sums = ph.sb("sums", [rows, NR])
        ps_turn, ps_log, ps_sum = (ph.ps(n, [P, K, P]) for n in ("ps_turn", "ps_log", "ps_sum"))
        ps_dst, ps_top = ph.ps("ps_dst", [P, 512]), ph.ps("ps_top", [P, 512])
        dst_v = ps_dst[:, 0:K * H].rearrange("p (k h) -> p k h", k=K)
        top_v = ps_top[:, 0:K * H].rearrange("p (k h) -> p k h", k=K)
        log_flat = ps_log[0:H, :, :].rearrange("p k e -> p (k e)")
        with nc.Block() as block:
            @block.sync
            def _(sp):
                def load(c, s, i):
                    sp.wait_ge(dst_at, free2(c))
                    sp.wait_ge(scanned, free2(c))
                    for n, m in enumerate((g.first_mask, g.last_mask)):
                        sp.dma_start(masks[:, s, n, :], m[ds(c * CE, CE)].partition_broadcast(H)).then_inc(win[s], 16)
                    for k, b in enumerate(bases(nc, ENG.SP, g.base, c)):
                        sp.dma_start(table[:, s, k, :], g.gat_dst[ds(b, P), :]).then_inc(win[s], 16)
                pairs(sp, load)

            @block.gpsimd
            def _(pool):
                def gather(c, s, i):
                    pool.wait_ge(filled, free2(c))
                    pool.wait_ge(gather_at, ready(c))
                    pool.sem_inc(opened, 1)
                    for k in range(K):
                        nc.gpsimd.indirect_dma_start(
                            from_src[:, s, k, :], None, g.gat_src[:, :],
                            bass.IndirectOffsetOnAxis(ap=src_at[:, s, k:k + 1], axis=0)).then_inc(got[s], 16)
                pairs(pool, gather)

            @block.scalar
            def _(act):
                for q in (staged, gather_at, turned_c, expo, shift_e):
                    act.sem_inc(q, 2)

                def early(c, s, i):
                    act.wait_ge(filled, free2(c))
                    alone(act, mark_a)
                    nc.scalar.activation(edge[:, s, :, :], g.edges[:, 0:END + 1, ds(c * K, K)], ACT.Copy
                                         ).then_inc(staged, 1)
                    nc.scalar.activation(src_at[:, s, :], g.edges[:, SRC, ds(c * K, K)], ACT.Copy
                                         ).then_inc(gather_at, 1)
                    act.wait_ge(turned, ready(c))
                    act.wait_ge(dst_at, free2(c))
                    for h in range(2):
                        last = nc.scalar.activation(memberT[:, s, 4 * h:4 * h + 4, :], ps_turn[:, 4 * h:4 * h + 4, :],
                                                    ACT.Copy)
                    last.then_inc(turned_c, 1)

                def late(c, s, i):
                    act.wait_ge(back_u, ready(c))
                    act.wait_ge(summed, free2(c))
                    nc.scalar.activation(msg[:, s, :, D:D + H], arg[:, :, :], ACT.Exp).then_inc(expo, 1)
                    nc.scalar.activation(shift[:, 1:2], shift[:, 0:1], ACT.Exp).then_inc(shift_e, 1)
                staggered(act, early, lambda c, s, i: None, late)

            @block.vector
            def _(dve):
                v = nc.vector
                for q in (members, logit, scanned, back_u, shifted, filled, added):
                    dve.sem_inc(q, 2)
                v.memset(sums[:, :], 0.0).then_inc(cleared, 1)
                v.memset(fwd[:, 1, :], -BIG).then_inc(cleared, 1)
                dve.wait_ge(cleared, 2)

                def early(c, s, i):
                    dve.wait_ge(staged, ready(c))
                    dve.wait_ge(summed, free2(c))
                    v.tensor_tensor(member[:, s], repeat(g.iota[:, :], K), spread(edge[:, s, REL, :], P), ALU.is_equal
                                    ).then_inc(members, 1)

                def rest(c, s, i):
                    chain = Chain(dve, step_a, c * 2)
                    dve.wait_ge(dst_at, ready(c))
                    dve.wait_ge(got[s], 16 * K * (i + 1))
                    chain(v.tensor_tensor(leaky[:, s], dst_v, from_src[:, s, :, D:D + H], ALU.add))
                    chain(v.scalar_tensor_tensor(leaky[:, s].rearrange("p k h -> p (k h)"),
                                                 leaky[:, s].rearrange("p k h -> p (k h)"), LRELU,
                                                 leaky[:, s].rearrange("p k h -> p (k h)"), ALU.mult, ALU.max))
                    dve.sem_inc(logit, 1)

                def late(c, s, i):
                    chain = Chain(dve, step_b, c * 15)
                    regs = bases(nc, ENG.DVE, g.base, c)
                    dve.wait_ge(logit_t, ready(c))
                    dve.wait_ge(win[s], 16 * (K + 2) * (i + 1))
                    before = fwd[:, 1 - s, CE - 1:CE]
                    chain(v.tensor_tensor_scan(fwd[:, s, :], masks[:, s, 0, :], log_flat, before, ALU.add, ALU.max))
                    dve.wait_ge(back, free1(c))
                    chain(v.tensor_tensor_scan(top[:, ::-1], masks[:, s, 1, ::-1], fwd[:, s, ::-1], -BIG, ALU.add,
                                               ALU.max))
                    dve.sem_inc(scanned, 1)
                    chain(v.tensor_tensor(shift[:, 0:1], before, top[:, 0:1], ALU.subtract))
                    chain(v.tensor_scalar(shift[:, 0:1], shift[:, 0:1], 0.0, None, ALU.min))
                    dve.wait_ge(back, ready(c))
                    chain(v.tensor_tensor(arg[:, :, :], leaky[:, s], top_v, ALU.subtract))
                    chain(v.tensor_tensor(msg[:, s, :, D + H:rows], top_v, spread(edge[:, s, END, :], H), ALU.mult))
                    dve.sem_inc(back_u, 1)
                    dve.wait_ge(expo, ready(c))
                    v.tensor_tensor(
                        msg[:, s, :, 0:D].rearrange("p k (h c) -> p k h c", h=H),
                        from_src[:, s, :, 0:D].rearrange("p k (h c) -> p k h c", h=H),
                        msg[:, s, :, D:D + H].unsqueeze(3).broadcast_to([P, K, H, D // H]), ALU.mult).then_inc(filled, 1)
                    dve.wait_ge(shift_p, ready(c))
                    chain(v.tensor_tensor(sums[:, ds(regs[0], 1)], sums[:, ds(regs[0], 1)], ps_sum[0:rows, 0, 0:1], ALU.mult))
                    dve.sem_inc(shifted, 1)
                    dve.wait_ge(summed, ready(c))
                    for k in range(K):
                        chain(v.tensor_tensor(sums[:, ds(regs[k], P)], sums[:, ds(regs[k], P)], ps_sum[0:rows, k, :],
                                              ALU.add))
                    dve.sem_inc(added, 1)
                    assert chain.n == 15
                staggered(dve, early, rest, late)

            @block.tensor
            def _(pe):
                for q in (turned, dst_at, logit_t, back, shift_p, summed):
                    pe.sem_inc(q, 2)

                def early(c, s, i):
                    pe.wait_ge(members, ready(c))
                    pe.wait_ge(turned_c, free1(c))
                    for k in range(K):
                        last = nc.tensor.transpose(ps_turn[:, k, :], member[:, s, k, :], g.ident[:, :])
                    last.then_inc(turned, 1)

                def rest(c, s, i):
                    pe.wait_ge(turned_c, ready(c))
                    pe.wait_ge(win[s], 16 * (K + 2) * (i + 1))
                    pe.wait_ge(logit, free1(c))
                    for k in range(K):
                        last = nc.tensor.matmul(dst_v[:, k, :], memberT[:, s, k, :], table[:, s, k, :], start=True, stop=True)
                    last.then_inc(dst_at, 1)
                    pe.wait_ge(logit, ready(c))
                    pe.wait_ge(scanned, free1(c))
                    for k in range(K):
                        last = nc.tensor.transpose(ps_log[0:H, k, :], leaky[:, s, k, :], g.ident[:, :])
                    last.then_inc(logit_t, 1)

                def late(c, s, i):
                    pe.wait_ge(scanned, ready(c))
                    pe.wait_ge(back_u, free1(c))
                    alone(pe, mark_p)
                    for k in range(K):
                        last = nc.tensor.transpose(top_v[:, k, :], top[:, k * P:(k + 1) * P], g.ident[0:H, 0:H])
                    last.then_inc(back, 1)
                    pe.wait_ge(shift_e, ready(c))
                    pe.wait_ge(added, free1(c))
                    nc.tensor.matmul(ps_sum[0:rows, 0, 0:1], g.heads[:, 0:rows], shift[:, 1:2], start=True, stop=True
                                     ).then_inc(shift_p, 1)
                    pe.wait_ge(filled, ready(c))
                    pe.wait_ge(shifted, ready(c))
                    for k in range(K):
                        last = nc.tensor.matmul(ps_sum[0:rows, k, :], msg[:, s, k, :], member[:, s, k, :], start=True,
                                                stop=True)
                    last.then_inc(summed, 1)
                staggered(pe, early, rest, late)
        columns_to_nodes(nc, g, ph, sums, rows, [ps_dst[:, :], ps_top[:, :]])


def after_attention(nc, g, name, bias, last):
    with Phase(nc, name) as ph:
        loaded, step, stored, done, asked, given, exps = ph.sems("loaded step stored done asked given exps")
        tab, ad = ph.sb("tab", [P, NT, D + H]), ph.sb("ad", [P, NT, H])
        top, own = ph.sb("top", [P, NT, H]), ph.sb("own", [P, NT, H])
        bv, stat = ph.sb("bv", [P, D]), ph.sb("stat", [P, 2, NT])
        x = ph.sb("x", [P, NT, D]) if last else None
        num, den, seen = g.node[:, :, 0:D], g.node[:, :, D:D + H], g.node[:, :, D + H:D + 2 * H]

        def by_head(ap):
            return ap.rearrange("p t (h c) -> p t h c", h=H)

        def over_head(ap):
            return ap.unsqueeze(3).broadcast_to([P, NT, H, D // H])

        with nc.Block() as block:
            @block.sync
            def _(sp):
                sp.dma_start(tab[:, :, :], nodes_view(g.gat_src, slice(0, D + H))).then_inc(loaded, 16)
                sp.dma_start(ad[:, :, :], nodes_view(g.gat_dst, slice(0, H))).then_inc(loaded, 16)
                sp.dma_start(bv[:, :], bias.partition_broadcast(P)).then_inc(loaded, 16)
                if last:
                    sp.dma_start(x[:, :, :], nodes_view(g.xs)).then_inc(loaded, 16)
                    sp.wait_ge(done, 1)
                    sp.dma_start(nodes_view(g.xs), x[:, :, :]).then_inc(stored, 16)
                    sp.wait_ge(stored, 16)

            @block.scalar
            def _(act):
                act.wait_ge(exps, 1)
                nc.scalar.activation(top[:, :, :], top[:, :, :], ACT.Exp).then_inc(exps, 1)
                nc.scalar.activation(own[:, :, :], own[:, :, :], ACT.Exp).then_inc(exps, 1)

            if last:
                @block.gpsimd
                def _(pool):
                    power(nc, g, pool, asked, given, 1, stat[:, 1, :], -0.5)

            @block.vector
            def _(dve):
                v = nc.vector
                chain = Chain(dve, step)
                dve.wait_ge(loaded, 16 * (4 if last else 3))
                chain(v.tensor_tensor(ad[:], ad[:], tab[:, :, D:D + H], ALU.add))
                chain(v.tensor_scalar(top[:], ad[:], LRELU, None, ALU.mult))
                chain(v.tensor_tensor(own[:], top[:], ad[:], ALU.max))
                chain(v.tensor_tensor(ad[:], own[:], seen, ALU.max))
                chain(v.tensor_tensor(top[:], seen, ad[:], ALU.subtract))
                chain(v.tensor_tensor(own[:], own[:], ad[:], ALU.subtract))
                dve.sem_inc(exps, 1)
                dve.wait_ge(exps, 3)
                chain(v.tensor_tensor(den, den, top[:], ALU.mult))
                chain(v.tensor_tensor(den, den, own[:], ALU.add))
                chain(v.tensor_scalar(den, den, 1e-16, None, ALU.add))
                chain(v.reciprocal(den, den))
                chain(v.tensor_tensor(by_head(num), by_head(num), over_head(top[:, :, :]), ALU.mult))
                chain(v.tensor_tensor(by_head(tab[:, :, 0:D]), by_head(tab[:, :, 0:D]), over_head(own[:, :, :]), ALU.mult))
                chain(v.tensor_tensor(num, num, tab[:, :, 0:D], ALU.add))
                chain(v.tensor_tensor(by_head(num), by_head(num), over_head(den), ALU.mult))
                chain(v.tensor_tensor(num, num, repeat(bv[:, :], NT), ALU.add))
                if not last:
                    chain(v.tensor_scalar(num, num, 0.0, None, ALU.max))
                else:
                    chain(v.tensor_tensor(x[:], x[:], num, ALU.add))
                    dve.sem_inc(done, 1)
                    layernorm_relu(nc, dve, chain, x, num, tab[:, :, 0:D], stat, asked, given)


def typed_tables(nc, g, name, weights):
    with Phase(nc, name) as ph:
        w_in, staged, turned, turned_c, made, even, odd, mark_a = ph.sems(
            "w_in staged turned turned_c made even odd mark_a")
        put = [ph.sem(f"put{s}") for s in range(2)]
        w = ph.sb("w", [D, R, D])
        stage, ft = ph.sb("stage", [P, 2, D]), ph.sb("ft", [D, 2, P])
        res = ph.sb("res", [P, 2, R * D])
        psf = [ph.ps(f"psf{s}", [P, 512])[0:D, 0:P] for s in range(2)]
        banks = [ph.ps(f"bank{n}", [P, 512]) for n in range(6)]
        groups = [(q, 8 * q, min(8, R - 8 * q)) for q in range((R + 7) // 8)]
        rows = g.typed.rearrange("(n r) d -> n (r d)", r=R)
        n_even, n_odd = 5, 4

        def copied(q, t):
            return (even, (t + 1) * n_even + q // 2 + 1) if q % 2 == 0 else (odd, (t + 1) * n_odd + q // 2 + 1)

        def copy_out(eng, move, parity, mark, t, s, i):
            eng.wait_ge(put[s], 16 * i + 16)
            for q, r, m in groups:
                if q % 2 == parity:
                    eng.wait_ge(made, (t + 1) * len(groups) + q + 1)
                    move(res[:, s, r * D:(r + m) * D], banks[q % 6][:, 0:m * D]).then_inc((even, odd)[parity], 1)

        with nc.Block() as block:
            @block.sync
            def _(sp):
                prime(sp, ph, g, put)
                sp.dma_start(w[:, :, :], weights.rearrange("r d k -> d r k")).then_inc(w_in, 16)

                def store(t, s, i):
                    for q in (8, 7):
                        sem, value = copied(q, t)
                        sp.wait_ge(sem, value)
                    sp.dma_start(rows[ds(t * P, P), :], res[:, s, :]).then_inc(put[s], 16)
                pairs(sp, store, NT)
                for s in range(2):
                    sp.wait_ge(put[s], 16 * (NT // 2) + 16)

            @block.scalar
            def _(act):
                act.sem_inc(staged, 2)
                act.sem_inc(even, n_even)

                def head(t, s, i):
                    act.wait_ge(turned, free2(t))
                    alone(act, mark_a)
                    nc.scalar.activation(stage[:, s, :], g.node[:, ds(t, 1), 0:D].rearrange("p o d -> p (o d)"),
                                         ACT.Copy).then_inc(staged, 1)

                def tail(t, s, i):
                    copy_out(act, lambda o, a: nc.scalar.activation(o, a, ACT.Copy), 0, None, t, s, i)
                skewed(act, head, tail, NT)

            @block.vector
            def _(dve):
                dve.sem_inc(turned_c, 2)
                dve.sem_inc(odd, n_odd)

                def head(t, s, i):
                    dve.wait_ge(turned, ready(t))
                    if not isinstance(t, int) or t >= 2:
                        dve.wait_ge(made, t * len(groups))
                    nc.vector.tensor_copy(ft[:, s, :], psf[s]).then_inc(turned_c, 1)

                def tail(t, s, i):
                    copy_out(dve, nc.vector.tensor_copy, 1, None, t, s, i)
                skewed(dve, head, tail, NT)

            @block.tensor
            def _(pe):
                pe.sem_inc(turned, 2)
                pe.sem_inc(made, len(groups))
                pe.wait_ge(w_in, 16)

                def head(t, s, i):
                    pe.wait_ge(staged, ready(t))
                    pe.wait_ge(turned_c, free2(t))
                    nc.tensor.matmul(psf[s], stage[:, s, :], g.ident[:, :], start=True, stop=True).then_inc(turned, 1)

                def tail(t, s, i):
                    pe.wait_ge(turned_c, ready(t))
                    for q, r, m in groups:
                        sem, value = copied(q - 6, t) if q >= 6 else copied(q + 6 if q < 3 else q, t - 1)
                        pe.wait_ge(sem, value)
                        nc.tensor.matmul(banks[q % 6][:, 0:m * D], ft[:, s, :],
                                         w[:, r:r + m, :].rearrange("d r k -> d (r k)"), start=True, stop=True
                                         ).then_inc(made, 1)
                skewed(pe, head, tail, NT)


def edges_relational(nc, g, name, first):
    with Phase(nc, name) as ph:
        (staged, gather_at, members, turned, turned_c, inverse, chosen, filled, summed, added) = ph.sems(
            "staged gather_at members turned turned_c inverse chosen filled summed added")
        step_a, step_b, opened, cleared, mark_a, mark_p = ph.sems("step_a step_b opened cleared mark_a mark_p")
        win = [ph.sem(f"win{s}") for s in range(2)]
        got = [ph.sem(f"got{s}") for s in range(2)]
        edge = ph.sb("edge", [P, 2, FIELDS, K])
        src_at = ph.sb("src_at", [P, 2, K], I32)
        spot = g.node[:, :, :].rearrange("p t d -> p (t d)")
        member, memberT = (spot[:, n * 2 * CE:(n + 1) * 2 * CE].rearrange("p (s k e) -> p s k e", s=2, k=K)
                           for n in range(2))
        table = ph.sb("table", [P, 2, K, R])
        kinds = ph.sb("kinds", [P, K, R])
        inv = ph.sb("inv", [P, 2, K])
        from_src = ph.sb("from_src", [P, 2, K, D])
        msg = ph.sb("msg", [P, 2, K, D])
        sums = ph.sb("sums", [D, NR])
        ps_turn, ps_sum = (ph.ps(n, [P, K, P]) for n in ("ps_turn", "ps_sum"))
        ps_inv = ph.ps("ps_inv", [P, 2, 512])
        inv_v = ps_inv[:, :, 0:4 * R].rearrange("p b (k r) -> p b k r", r=R)
        with nc.Block() as block:
            if first:
                @block.sync
                def _(sp):
                    def load(c, s, i):
                        sp.wait_ge(inverse, free2(c))
                        for k, b in enumerate(bases(nc, ENG.SP, g.base, c)):
                            sp.dma_start(table[:, s, k, :], g.inv_count[ds(b, P), :]).then_inc(win[s], 16)
                    pairs(sp, load)

            @block.gpsimd
            def _(pool):
                def gather(c, s, i):
                    pool.wait_ge(filled, free2(c))
                    pool.wait_ge(gather_at, ready(c))
                    pool.sem_inc(opened, 1)
                    for k in range(K):
                        nc.gpsimd.indirect_dma_start(
                            from_src[:, s, k, :], None, g.typed[:, :],
                            bass.IndirectOffsetOnAxis(ap=src_at[:, s, k:k + 1], axis=0)).then_inc(got[s], 16)
                pairs(pool, gather)

            @block.scalar
            def _(act):
                for q in (staged, gather_at, turned_c):
                    act.sem_inc(q, 2)

                def early(c, s, i):
                    act.wait_ge(filled, free2(c))
                    alone(act, mark_a)
                    nc.scalar.activation(edge[:, s, :, :], g.edges[:, :, ds(c * K, K)], ACT.Copy).then_inc(staged, 1)
                    nc.scalar.activation(src_at[:, s, :], g.edges[:, SIDX, ds(c * K, K)], ACT.Copy
                                         ).then_inc(gather_at, 1)
                    if first:
                        act.wait_ge(turned, ready(c))
                        act.wait_ge(inverse, free2(c))
                        for h in range(2):
                            last = nc.scalar.activation(memberT[:, s, 4 * h:4 * h + 4, :],
                                                        ps_turn[:, 4 * h:4 * h + 4, :], ACT.Copy)
                        last.then_inc(turned_c, 1)
                pairs(act, early)

            @block.vector
            def _(dve):
                v = nc.vector
                for q in (members, chosen, filled, added):
                    dve.sem_inc(q, 2)
                v.memset(sums[:, :], 0.0).then_inc(cleared, 1)
                dve.wait_ge(cleared, 1)

                def early(c, s, i):
                    chain = Chain(dve, step_a, c * 3)
                    dve.wait_ge(staged, ready(c))
                    dve.wait_ge(summed, free2(c))
                    v.tensor_tensor(member[:, s], repeat(g.iota[:, :], K), spread(edge[:, s, REL, :], P), ALU.is_equal
                                    ).then_inc(members, 1)
                    if first:
                        chain(v.tensor_tensor(kinds[:, :, :], repeat(g.iota[:, 0:R], K), spread(edge[:, s, TYPE, :], R),
                                              ALU.is_equal))
                        dve.wait_ge(inverse, ready(c))
                        kv = kinds[:, :, :].rearrange("p (b k) r -> p b k r", b=2)
                        chain(v.tensor_tensor(kv, kv, inv_v, ALU.mult))
                        dve.sem_inc(chosen, 1)
                        chain(v.tensor_reduce(inv[:, s, :], kinds[:, :, :], AX.X, ALU.add))
                        v.tensor_copy(g.edges[:, INV, ds(c * K, K)], inv[:, s, :])

                def late(c, s, i):
                    chain = Chain(dve, step_b, c * K)
                    dve.wait_ge(got[s], 16 * K * (i + 1))
                    v.tensor_tensor(msg[:, s], from_src[:, s], spread(inv[:, s, :] if first else edge[:, s, INV, :], D),
                                    ALU.mult).then_inc(filled, 1)
                    dve.wait_ge(summed, ready(c))
                    for k, b in enumerate(bases(nc, ENG.DVE, g.base, c)):
                        chain(v.tensor_tensor(sums[:, ds(b, P)], sums[:, ds(b, P)], ps_sum[0:D, k, :], ALU.add))
                    dve.sem_inc(added, 1)
                skewed(dve, early, late)

            @block.tensor
            def _(pe):
                for q in (turned, inverse, summed):
                    pe.sem_inc(q, 2)

                def early(c, s, i):
                    if not first:
                        return
                    pe.wait_ge(members, ready(c))
                    pe.wait_ge(turned_c, free1(c))
                    for k in range(K):
                        last = nc.tensor.transpose(ps_turn[:, k, :], member[:, s, k, :], g.ident[:, :])
                    last.then_inc(turned, 1)
                    pe.wait_ge(turned_c, ready(c))
                    pe.wait_ge(win[s], 16 * K * (i + 1))
                    pe.wait_ge(chosen, free1(c))
                    for k in range(K):
                        last = nc.tensor.matmul(inv_v[:, k // 4, k % 4, :], memberT[:, s, k, :], table[:, s, k, :],
                                                start=True, stop=True)
                    last.then_inc(inverse, 1)

                def late(c, s, i):
                    pe.wait_ge(members, ready(c))
                    pe.wait_ge(filled, ready(c))
                    pe.wait_ge(added, free1(c))
                    for k in range(K):
                        last = nc.tensor.matmul(ps_sum[0:D, k, :], msg[:, s, k, :], member[:, s, k, :], start=True,
                                                stop=True)
                    last.then_inc(summed, 1)
                skewed(pe, early, late)
        turn = [ps_inv[:, n, :] for n in range(2)]
        columns_to_nodes(nc, g, ph, sums, D, turn)


def typed_index(nc, g):
    with nc.Block() as block:
        @block.vector
        def _(dve):
            nc.vector.scalar_tensor_tensor(g.edges[:, SIDX, :], g.edges[:, SRC, :], float(R), g.edges[:, TYPE, :],
                                           ALU.mult, ALU.add)


def after_relational(nc, g, name, bias, res_bias, last):
    with Phase(nc, name) as ph:
        loaded, step, stored, done = ph.sems("loaded step stored done")
        own = ph.sb("own", [P, NT, 2 * D])
        bv = ph.sb("bv", [P, 2, D])
        x = ph.sb("x", [P, NT, D]) if last else None
        h = g.node[:, :, 0:D]
        full, rest = N // P, N % P
        with nc.Block() as block:
            @block.sync
            def _(sp):
                sp.dma_start(own[:, :, :], nodes_view(g.hyp_src, slice(0, 2 * D))).then_inc(loaded, 16)
                sp.dma_start(bv[:, 0, :], bias.partition_broadcast(P)).then_inc(loaded, 16)
                sp.dma_start(bv[:, 1, :], res_bias.partition_broadcast(P)).then_inc(loaded, 16)
                if last:
                    sp.dma_start(x[:, :, :], nodes_view(g.xs)).then_inc(loaded, 16)
                    sp.wait_ge(done, 1)
                    sp.dma_start(g.out[0:full * P, :].rearrange("(t p) d -> p t d", p=P), x[:, 0:full, :]
                                 ).then_inc(stored, 16)
                    sp.dma_start(g.out[full * P:N, :], x[0:rest, full, :]).then_inc(stored, 16)
                    sp.wait_ge(stored, 32)

            @block.vector
            def _(dve):
                v = nc.vector
                chain = Chain(dve, step)
                dve.wait_ge(loaded, 16 * (4 if last else 3))
                chain(v.tensor_tensor(h, h, own[:, :, 0:D], ALU.add))
                chain(v.tensor_tensor(h, h, repeat(bv[:, 0, :], NT), ALU.add))
                chain(v.tensor_scalar(h, h, 0.0, None, ALU.max))
                chain(v.tensor_tensor(own[:, :, D:2 * D], own[:, :, D:2 * D], repeat(bv[:, 1, :], NT), ALU.add))
                chain(v.tensor_scalar(own[:, :, D:2 * D], own[:, :, D:2 * D], 0.0, None, ALU.max))
                chain(v.tensor_tensor(h, h, own[:, :, D:2 * D], ALU.add))
                if last:
                    chain(v.tensor_tensor(x[:, :, :], x[:, :, :], h, ALU.add))
                    dve.sem_inc(done, 1)


class Shared:
    pass


def gnn_kernel(nc, w, out, upto=99):
    g = Shared()
    g.w, g.x, g.src, g.dst, g.etype = w, w["x"], w["src"], w["dst"], w["edge_type_65"]
    g.ew, g.ew1, g.out = w["edge_weight"], w["edge_weight1"], out

    def dram(name, shape, dt=F32):
        return nc.dram_tensor(name + "_dram", shape, dt, kind="Internal").ap()

    g.src_p, g.dst_p, g.type_p = (dram(f"{n}_padded", (EP + 32,), I32) for n in ("src", "dst", "type"))
    g.ew_p, g.ew1_p = (dram(f"{n}_padded", (EP + 32,)) for n in ("weight", "weight1"))
    g.first_mask, g.last_mask = dram("first_mask", (EP,)), dram("last_mask", (EP,))
    g.xs = dram("x_now", (NR, D))
    g.sum0 = [dram(f"gcn_sum{k}", (NR + SPARE, D)) for k in range(COPIES)]
    g.sum1 = [dram(f"hyp_sum{k}", (NR + SPARE, D)) for k in range(COPIES)]
    g.gcn_table = dram("gcn_table", (NR, D))
    g.hyp_src = dram("hyp_src", (NR, 2 * D))
    g.hyp_dst = dram("hyp_dst", (NR, 3 * D))
    g.gat_src = dram("gat_src", (NR, D + H))
    g.gat_dst = dram("gat_dst", (NR, H))
    g.inv_count = dram("inv_count", (NR, R))
    g.typed = dram("typed", (NR * R, D))
    with Phase(nc, "all") as ph:
        g.edges = ph.sb("edges", [P, FIELDS, ET])
        g.node = ph.sb("node", [P, NT, D + 2 * H])
        g.base = ph.sb("base", [1, ET], I32)
        g.iota, g.ident, g.lower = (ph.sb(n, [P, P]) for n in ("iota", "ident", "lower"))
        g.ident16 = ph.sb("ident16", [P, P], BF16)
        g.halves = ph.sb("halves", [P, 2])
        g.lane = ph.sb("lane", [P, 1])
        g.ones = ph.sb("ones", [1, P])
        g.heads = ph.sb("heads", [H, D + 2 * H])
        stages = [
            lambda: prepare(nc, g),
            lambda: begin(nc, g),
            lambda: project(nc, g, "gcn_in", [w["L0_gnn_kernel"]], D, [(g.gcn_table, slice(0, D), slice(0, D))]),
            lambda: edges_gcn(nc, g),
            lambda: after_gcn(nc, g),
            lambda: hyperbolic_in(nc, g),
            lambda: project(nc, g, "hyp_in", [w["L1_gnn_w1"][0:D, :], w["L1_gnn_w1"][D:2 * D, :], None], 3 * D,
                            [(g.hyp_src, slice(0, D), slice(0, D)), (g.hyp_dst, slice(D, 3 * D), slice(D, 3 * D))],
                            first=(w["L1_gnn_W"], w["L1_gnn_b"])),
            lambda: edges_hyperbolic(nc, g),
            lambda: after_hyperbolic(nc, g),
        ]
        for n in (1, 2, 3):
            stages += [
                lambda n=n: project(nc, g, f"gat_in{n}", [w[f"L2_gnn_W{n}"]], D,
                                    [(g.gat_src, slice(0, D + H), slice(0, D + H)),
                                     (g.gat_dst, slice(0, H), slice(D + H, D + 2 * H))],
                                    dots=(w[f"L2_gnn_a_src{n}"], w[f"L2_gnn_a_dst{n}"])),
                lambda n=n: edges_attention(nc, g, f"gat{n}"),
                lambda n=n: after_attention(nc, g, f"gat_end{n}", w[f"L2_gnn_b{n}"], n == 3),
            ]
        stages.append(lambda: typed_index(nc, g))
        for n in range(2):
            stages += [
                lambda n=n: project(nc, g, f"rel_in{n}", [w["L3_gnn_root"][n], w["L3_gnn_res_W"][n]], 2 * D,
                                    [(g.hyp_src, slice(0, 2 * D), slice(0, 2 * D))]),
                lambda n=n: typed_tables(nc, g, f"typed{n}", w["L3_gnn_W"][n]),
                lambda n=n: edges_relational(nc, g, f"rel{n}", n == 0),
                lambda n=n: after_relational(nc, g, f"rel_end{n}", w["L3_gnn_bias"][n], w["L3_gnn_res_b"][n], n == 1),
            ]
        for n, f in enumerate(stages):
            if n < upto:
                f()


_OUT = ((12500, 64), "float32")


def kernel(**inputs):
    import numpy as _np
    import concourse.bacc as _bacc
    from concourse import mybir as _mybir
    from concourse.bass_utils import run_bass_kernel_spmd as _run

    nc = _bacc.Bacc("TRN2", target_bir_lowering=False, num_devices=1)
    arrays, args = {}, {}
    for name, a in inputs.items():
        if name == "node_vec1":
            continue
        arrays[f"in_{name}"] = _np.ascontiguousarray(a)
        args[name] = nc.dram_tensor(f"in_{name}", a.shape, _mybir.dt.from_np(_np.asarray(a).dtype),
                                    kind="ExternalInput").ap()
    out = nc.dram_tensor("out", _OUT[0], _mybir.dt.from_np(_np.dtype(_OUT[1])), kind="ExternalOutput").ap()
    gnn_kernel(nc, args, out)
    return _run(nc, [arrays], core_ids=[0]).results[0]["out"]
```

```python
from contextlib import ExitStack

import concourse.bass as bass
from concourse import mybir

F32, I32, BF16 = mybir.dt.float32, mybir.dt.int32, mybir.dt.bfloat16
ALU, ACT, AX = mybir.AluOpType, mybir.ActivationFunctionType, mybir.AxisListType
ENG = mybir.EngineType
ds = bass.ds

P = 128
N, E, D = 12500, 212500, 64
H = 8
R = 65
K = 8
CE = K * P
ET = 1664
EB = ET // P
EP = ET * P
CHUNKS = ET // K
NT = 100
NR = NT * P
SPARE = P
COPIES = K
BIG = 1.0e30
LRELU = 0.2
ACOSH_MIN = 1.0 + 1e-7
SRC, REL, EW, EW1, TYPE, END, SIDX, INV = range(8)
FIELDS = 8


class Chain:

    def __init__(self, eng, sem, base=0):
        self.eng, self.sem, self.base, self.n = eng, sem, base, 0

    def __call__(self, ins):
        self.n += 1
        ins.then_inc(self.sem, 1)
        self.eng.wait_ge(self.sem, self.base + self.n)


START = 4


def ready(c):
    return c + START + 1


def free1(c):
    return c + START


def free2(c):
    return c + START - 1


def free4(c):
    return c + START - 3


def half_ready(c, h):
    return 2 * (c + START) + h + 1


def alone(eng, mark):
    eng.sem_inc(mark, 1)


def pairs(eng, body, count=CHUNKS):
    with eng.Fori(0, count // 2) as i:
        for s in range(2):
            body(i * 2 + s, s, i)


def skewed(eng, first, second, count=CHUNKS):
    first(0, 0, 0)
    with eng.Fori(0, count // 2 - 1) as i:
        first(i * 2 + 1, 1, i)
        second(i * 2, 0, i)
        first(i * 2 + 2, 0, i + 1)
        second(i * 2 + 1, 1, i)
    last = count // 2 - 1
    first(count - 1, 1, last)
    second(count - 2, 0, last)
    second(count - 1, 1, last)


def rounds(eng, steps, count=CHUNKS):
    def turn(t, i, q):
        for step, lead in steps:
            if not isinstance(t, int) or 0 <= t + lead < count:
                step(t + lead, (q + lead) % 4, i + (q + lead) // 4)
    for t in range(-max(lead for _, lead in steps), 0):
        turn(t, t // 4, t % 4)
    with eng.Fori(0, count // 4 - 1) as i:
        for q in range(4):
            turn(i * 4 + q, i, q)
    for t in range(count - 4, count):
        turn(t, t // 4, t % 4)


def bases(nc, engine, base, c, first=0, count=K):
    _, regs = nc.values_load_multi_w_load_instructions(
        base[0:1, ds(c * K + first, count)], engines=(engine,), min_val=0, max_val=N,
        skip_runtime_bounds_check_because="dst is a node or the padding node")
    return regs


def spread(ap, n):
    return ap.unsqueeze(2).broadcast_to([ap.shape[0], ap.shape[1], n])


def repeat(ap, n):
    return ap.unsqueeze(1).broadcast_to([ap.shape[0], n, ap.shape[1]])


class Phase:

    def __init__(self, nc, name):
        self.nc, self.name, self.stack, self.used = nc, name, ExitStack(), []

    def __enter__(self):
        self.stack.__enter__()
        return self

    def __exit__(self, *a):
        if self.used:
            self.nc.clear_and_free_semaphores(self.used)
            self.nc.all_engine_barrier()
        return self.stack.__exit__(*a)

    def sem(self, name):
        self.used.append(self.nc.alloc_semaphore(f"{self.name}_{name}"))
        return self.used[-1]

    def sems(self, names):
        return [self.sem(n) for n in names.split()]

    def sb(self, name, shape, dt=F32):
        return self.stack.enter_context(self.nc.sbuf_tensor(f"{self.name}_{name}", shape, dt))

    def ps(self, name, shape, dt=F32):
        return self.stack.enter_context(self.nc.psum_tensor(f"{self.name}_{name}", shape, dt))


def prepare(nc, g):
    with Phase(nc, "prep") as ph:
        loaded, padded, const, turned, copied, step, stored, rows_in, zeroed = ph.sems(
            "loaded padded const turned copied step stored rows_in zeroed")
        padi = ph.sb("padi", [P, 16], I32)
        padf = ph.sb("padf", [P, 16])
        raw = [ph.sb(f"raw{n}", [P, EB, P], I32 if n < 5 else F32) for n in range(7)]
        rows = [ph.sb(f"rows{n}", [P, EB, P]) for n in range(5)]
        mask = ph.sb("mask", [P, 2, EB, P])
        dstf = ph.sb("dstf", [P, ET])
        zw = (NR + SPARE) // P * D // 2
        zero = ph.sb("zero", [P, zw])
        turn = [ph.ps(f"turn{n}", [P, 512]) for n in range(4)]
        src_r, dst_r, prev_r, next_r, type_r = range(5)
        flat = EP - E
        fields = (SRC, None, TYPE, EW, EW1, END)
        with nc.Block() as block:
            @block.gpsimd
            def _(pool):
                nc.gpsimd.iota(g.iota[:, :], [[1, P]], base=0, channel_multiplier=0,
                               allow_small_or_imprecise_dtypes=True).then_inc(const, 1)
                nc.gpsimd.iota(g.lane[:, 0:1], [[0, 1]], base=NR, channel_multiplier=1,
                               allow_small_or_imprecise_dtypes=True).then_inc(const, 1)
                nc.gpsimd.memset(g.ident[:, :], 0.0).then_inc(const, 1)
                nc.gpsimd.memset(g.lower[:, :], 1.0).then_inc(const, 1)
                nc.gpsimd.memset(g.heads[:, :], 1.0).then_inc(const, 1)
                pool.wait_ge(const, 5)
                nc.gpsimd.affine_select(out=g.ident[:, :], in_=g.ident[:, :], compare_op=ALU.not_equal,
                                        fill=1.0, base=0, pattern=[[-1, P]], channel_multiplier=1).then_inc(const, 1)
                nc.gpsimd.affine_select(out=g.lower[:, :], in_=g.lower[:, :], compare_op=ALU.is_gt,
                                        fill=0.0, base=0, pattern=[[-1, P]], channel_multiplier=1).then_inc(const, 1)
                hv = g.heads[:, 0:D].rearrange("p (h c) -> p h c", h=H)
                nc.gpsimd.affine_select(out=hv, in_=hv, compare_op=ALU.is_equal, fill=0.0, base=0,
                                        pattern=[[-1, H], [0, D // H]], channel_multiplier=1).then_inc(const, 1)
                iv = g.heads[:, D:D + 2 * H].rearrange("p (a h) -> p a h", a=2)
                nc.gpsimd.affine_select(out=iv, in_=iv, compare_op=ALU.is_equal, fill=0.0, base=0,
                                        pattern=[[0, 2], [-1, H]], channel_multiplier=1).then_inc(const, 1)
                pool.wait_ge(const, 9)
                nc.gpsimd.tensor_copy(g.ident16[:, :], g.ident[:, :])

            @block.sync
            def _(sp):
                for d, a in ((g.src_p, g.src), (g.dst_p, g.dst), (g.type_p, g.etype),
                             (g.ew_p, g.ew), (g.ew1_p, g.ew1.rearrange("e o -> (e o)"))):
                    sp.dma_start(d[16:16 + E].rearrange("(a b) -> a b", a=20), a.rearrange("(a b) -> a b", a=20)
                                 ).then_inc(loaded, 16)
                sp.wait_ge(padded, 5)
                for d, p in ((g.src_p, 0), (g.dst_p, 0), (g.type_p, 1)):
                    sp.dma_start(d[16 + E:16 + EP].rearrange("(a b) -> a b", b=4), padi[0:flat // 4, 4 * p:4 * p + 4]
                                 ).then_inc(loaded, 16)
                for d in (g.ew_p, g.ew1_p):
                    sp.dma_start(d[16 + E:16 + EP].rearrange("(a b) -> a b", b=4), padf[0:flat // 4, 0:4]
                                 ).then_inc(loaded, 16)
                for at in (0, 16 + EP):
                    sp.dma_start(g.dst_p[at:at + 16].rearrange("(a b) -> a b", a=4), padi[0:4, 8:12]).then_inc(loaded, 16)
                sp.wait_ge(loaded, 12 * 16)
                for n, (d, off) in enumerate(((g.src_p, 16), (g.dst_p, 16), (g.dst_p, 15), (g.dst_p, 17),
                                              (g.type_p, 16), (g.ew_p, 16), (g.ew1_p, 16))):
                    sp.dma_start(raw[n][:, :, :], d[off:off + EP].rearrange("(g p e) -> p g e", p=P, e=P)
                                 ).then_inc(rows_in, 16)
                sp.wait_ge(stored, 1)
                for n, m in enumerate((g.first_mask, g.last_mask)):
                    sp.dma_start(m[0:EP].rearrange("(g p e) -> p g e", p=P, e=P), mask[:, n, :, :]).then_inc(loaded, 16)
                sp.wait_ge(loaded, 14 * 16)

            @block.scalar
            def _(act):
                act.wait_ge(padded, 6)
                n = 0
                for t in g.sum0 + g.sum1:
                    for part in range(2):
                        act.dma_start(t.rearrange("(p w) d -> p (w d)", p=P)[:, part * zw:(part + 1) * zw],
                                      zero[:, :]).then_inc(zeroed, 16)
                        n += 1
                act.wait_ge(zeroed, 16 * n)

            @block.vector
            def _(dve):
                nc.vector.memset(g.ones[:, :], 1.0).then_inc(padded, 1)
                nc.vector.memset(padi[:, 0:4], N).then_inc(padded, 1)
                nc.vector.memset(padi[:, 4:8], 0).then_inc(padded, 1)
                nc.vector.memset(padi[:, 8:12], -1).then_inc(padded, 1)
                nc.vector.memset(padf[:, :], 0.0).then_inc(padded, 1)
                nc.vector.memset(zero[:, :], 0.0).then_inc(padded, 1)
                nc.vector.memset(g.halves[:, 0:1], 0.5)
                nc.vector.memset(g.halves[:, 1:2], -0.5)
                nc.vector.memset(g.edges[:, SIDX:FIELDS, :], 0.0)
                chain = Chain(dve, step)
                dve.wait_ge(rows_in, 7 * 16)
                for n in range(5):
                    chain(nc.vector.tensor_copy(rows[n][:, :, :], raw[n][:, :, :]))
                chain(nc.vector.tensor_tensor(mask[:, 0], rows[dst_r][:], rows[prev_r][:], ALU.not_equal))
                chain(nc.vector.tensor_tensor(rows[next_r][:], rows[dst_r][:], rows[next_r][:], ALU.not_equal))
                chain(nc.vector.tensor_scalar(mask[:, 1], rows[next_r][:], -BIG, None, ALU.mult))
                nc.vector.tensor_scalar(mask[:, 0], mask[:, 0], -BIG, None, ALU.mult).then_inc(stored, 1)
                bank = 0
                for f, (field, dst) in enumerate(((SRC, None), (None, dstf), (TYPE, None), (EW, None), (EW1, None),
                                                  (END, None))):
                    for b in range(0, EB, 4):
                        w = min(4, EB - b) * P
                        o = dst[:, b * P:b * P + w] if dst is not None else g.edges[:, field, b * P:b * P + w]
                        dve.wait_ge(turned, bank + 1)
                        nc.vector.tensor_copy(o, turn[bank % 2][:, 0:w]).then_inc(copied, 1)
                        bank += 1
                dve.wait_ge(copied, bank)
                nc.vector.tensor_copy(g.base[0:1, :], dstf[0:1, :]).then_inc(copied, 1)
                for n, o in enumerate(range(0, ET, 512)):
                    w = min(512, ET - o)
                    dve.wait_ge(turned, bank + 1 + n)
                    nc.vector.tensor_tensor(g.edges[:, REL, o:o + w], dstf[:, o:o + w], turn[2 + n % 2][:, 0:w],
                                            ALU.subtract).then_inc(copied, 1)
                dve.wait_ge(copied, bank + 5)

            @block.tensor
            def _(pe):
                pe.wait_ge(const, 9)
                pe.wait_ge(step, 7)
                bank = 0
                for src in (rows[src_r], rows[dst_r], rows[type_r], raw[5], raw[6], rows[next_r]):
                    for b in range(0, EB, 4):
                        if bank >= 2:
                            pe.wait_ge(copied, bank - 1)
                        for k in range(b, min(b + 4, EB)):
                            last = nc.tensor.transpose(turn[bank % 2][:, (k - b) * P:(k - b + 1) * P], src[:, k, :],
                                                       g.ident[:, :])
                        last.then_inc(turned, 1)
                        bank += 1
                pe.wait_ge(copied, bank)
                pe.wait_ge(padded, 1)
                for n, o in enumerate(range(0, ET, 512)):
                    w = min(512, ET - o)
                    if n >= 2:
                        pe.wait_ge(copied, bank + 1 + n - 1)
                    nc.tensor.matmul(turn[2 + n % 2][:, 0:w], g.ones[0:1, :], dstf[0:1, o:o + w], start=True,
                                     stop=True).then_inc(turned, 1)


def power(nc, g, pool, asked, given, n, data, exponent):
    pool.wait_ge(asked, n)
    half = g.halves[:, 0:1] if exponent > 0 else g.halves[:, 1:2]
    nc.gpsimd.tensor_tensor(data, data, half.broadcast_to([P, data.shape[1]]), ALU.pow).then_inc(given, 1)


def ask_power(dve, asked, given, n):
    dve.sem_inc(asked, 1)
    dve.wait_ge(given, n)


def layernorm_relu(nc, dve, chain, x, h, sq, stat, asked, given, n=1):
    v = nc.vector
    chain(v.tensor_reduce(stat[:, 0, :], x[:, :, :], AX.X, ALU.add))
    chain(v.tensor_scalar(stat[:, 0, :], stat[:, 0, :], 1.0 / D, None, ALU.mult))
    chain(v.tensor_tensor(h, x[:, :, :], spread(stat[:, 0, :], D), ALU.subtract))
    chain(v.tensor_tensor(sq[:, :, :], h, h, ALU.mult))
    chain(v.tensor_reduce(stat[:, 1, :], sq[:, :, :], AX.X, ALU.add))
    chain(v.tensor_scalar(stat[:, 1, :], stat[:, 1, :], 1.0 / D, 1e-5, ALU.mult, ALU.add))
    ask_power(dve, asked, given, n)
    chain(v.tensor_tensor(h, h, spread(stat[:, 1, :], D), ALU.mult))
    chain(v.tensor_scalar(h, h, 0.0, None, ALU.max))


def nodes_view(t, cols=slice(0, D)):
    return t[0:NR, cols].rearrange("(t p) d -> p t d", p=P)


def begin(nc, g):
    with Phase(nc, "begin") as ph:
        loaded, step, cleared, stored, asked, given = ph.sems("loaded step cleared stored asked given")
        x, sq, stat = ph.sb("x", [P, NT, D]), ph.sb("sq", [P, NT, D]), ph.sb("stat", [P, 2, NT])
        full, rest = N // P, N % P
        with nc.Block() as block:
            @block.sync
            def _(sp):
                sp.wait_ge(cleared, 1)
                sp.dma_start(x[:, 0:full, :], g.x[0:full * P, :].rearrange("(t p) d -> p t d", p=P)).then_inc(loaded, 16)
                sp.dma_start(x[0:rest, full, :], g.x[full * P:N, :]).then_inc(loaded, 16)
                sp.wait_ge(loaded, 32)
                sp.dma_start(nodes_view(g.xs), x[:, :, :]).then_inc(stored, 16)
                sp.wait_ge(stored, 16)

            @block.vector
            def _(dve):
                nc.vector.memset(x[:, full:NT, :], 0.0).then_inc(cleared, 1)
                dve.wait_ge(loaded, 32)
                chain = Chain(dve, step)
                layernorm_relu(nc, dve, chain, x, g.node[:, :, 0:D], sq, stat, asked, given)

            @block.gpsimd
            def _(pool):
                power(nc, g, pool, asked, given, 1, stat[:, 1, :], -0.5)


def project(nc, g, name, weights, width, stores, first=None, dots=None):
    cols = len(weights) * D
    extra = 2 * H if dots else 0
    with Phase(nc, name) as ph:
        (w_in, staged, turned, turned_c, hidden, hidden_c, made, made_c, dotted) = ph.sems(
            "w_in staged turned turned_c hidden hidden_c made made_c dotted")
        step, mark, mark_a = ph.sems("step mark mark_a")
        put = [ph.sem(f"put{s}") for s in range(2)]
        w = ph.sb("w", [D, cols])
        w1 = ph.sb("w1", [D, D])
        b1 = ph.sb("b1", [D, 1])
        av = ph.sb("av", [P, 2, D])
        tmp = ph.sb("tmp", [P, 2, D])
        stage = ph.sb("stage", [P, 2, D])
        ft = ph.sb("ft", [D, 2, P])
        hid = ph.sb("hid", [D, 2, P])
        res = ph.sb("res", [P, 2, cols + extra])
        psf, psh = ([ph.ps(f"{n}{s}", [P, 512])[0:D, 0:P] for s in range(2)] for n in ("psf", "psh"))
        psr = [ph.ps(f"psr{s}", [P, 512]) for s in range(2)]
        last_done = dotted if dots else made_c
        loads = sum(m is not None for m in weights) + (2 if first else 0) + (2 if dots else 0)
        with nc.Block() as block:
            @block.sync
            def _(sp):
                prime(sp, ph, g, put)
                for n, m in enumerate(weights):
                    if m is not None:
                        sp.dma_start(w[:, n * D:(n + 1) * D], m).then_inc(w_in, 16)
                if first:
                    sp.dma_start(w1[:, :], first[0]).then_inc(w_in, 16)
                    sp.dma_start(b1[:, :], first[1].unsqueeze(1)).then_inc(w_in, 16)
                if dots:
                    for n, a in enumerate(dots):
                        sp.dma_start(av[:, n, :], a.rearrange("h c -> (h c)").partition_broadcast(P)).then_inc(w_in, 16)

                def store(t, s, i):
                    sp.wait_ge(last_done, ready(t))
                    for table, tc, rc in stores:
                        sp.dma_start(table[ds(t * P, P), tc], res[:, s, rc]).then_inc(put[s], 16)
                pairs(sp, store, NT)
                for s in range(2):
                    sp.wait_ge(put[s], 16 * len(stores) * (NT // 2) + 16)

            @block.scalar
            def _(act):
                act.sem_inc(staged, START)
                act.sem_inc(made_c, START)
                act.sem_inc(hidden_c, START)

                def head(t, s, i):
                    act.wait_ge(turned, free2(t))
                    alone(act, mark_a)
                    nc.scalar.activation(stage[:, s, :], g.node[:, ds(t, 1), 0:D].rearrange("p o d -> p (o d)"),
                                         ACT.Copy).then_inc(staged, 1)

                def tail(t, s, i):
                    if first:
                        act.wait_ge(hidden, ready(t))
                        act.wait_ge(w_in, 16 * loads)
                        nc.scalar.activation(hid[:, s, :], psh[s], ACT.Identity, bias=b1[:, 0:1]
                                             ).then_inc(hidden_c, 1)
                    act.wait_ge(made, ready(t))
                    act.wait_ge(put[s], 16 * len(stores) * i + 16)
                    nc.scalar.activation(res[:, s, 0:cols], psr[s][:, 0:cols], ACT.Copy).then_inc(made_c, 1)
                skewed(act, head, tail, NT)

            @block.vector
            def _(dve):
                dve.sem_inc(turned_c, START)
                dve.sem_inc(dotted, START)
                if dots:
                    dve.wait_ge(w_in, 16 * loads)

                def head(t, s, i):
                    dve.wait_ge(turned, ready(t))
                    dve.wait_ge(hidden if first else made, free2(t))
                    nc.vector.tensor_copy(ft[:, s, :], psf[s]).then_inc(turned_c, 1)

                def tail(t, s, i):
                    if not dots:
                        return
                    dve.wait_ge(made_c, ready(t))
                    chain = Chain(dve, step, t * 2)
                    chain(nc.vector.tensor_tensor(tmp[:, :, :], repeat(res[:, s, 0:D], 2), av[:, :, :], ALU.mult))
                    last = nc.vector.tensor_reduce(
                        res[:, s, D:D + 2 * H].rearrange("p (a h) -> p a h", a=2),
                        tmp[:, :, :].rearrange("p a (h c) -> p a h c", h=H), AX.X, ALU.add)
                    chain(last)
                    dve.sem_inc(dotted, 1)
                skewed(dve, head, tail, NT)

            @block.tensor
            def _(pe):
                for q in (turned, hidden, made):
                    pe.sem_inc(q, START)

                def head(t, s, i):
                    pe.wait_ge(staged, ready(t))
                    pe.wait_ge(turned_c, free2(t))
                    nc.tensor.matmul(psf[s], stage[:, s, :], g.ident[:, :], start=True, stop=True).then_inc(turned, 1)

                def tail(t, s, i):
                    pe.wait_ge(w_in, 16 * loads)
                    pe.wait_ge(turned_c, ready(t))
                    lhs = ft
                    if first:
                        pe.wait_ge(hidden_c, free2(t))
                        alone(pe, mark)
                        nc.tensor.matmul(psh[s], w1[:, :], ft[:, s, :], start=True, stop=True).then_inc(hidden, 1)
                        pe.wait_ge(hidden_c, ready(t))
                        lhs = hid
                    pe.wait_ge(made_c, free2(t))
                    for n, m in enumerate(weights):
                        wt = g.ident[0:D, 0:D] if m is None else w[:, n * D:(n + 1) * D]
                        last = nc.tensor.matmul(psr[s][:, n * D:(n + 1) * D], lhs[:, s, :], wt, start=True, stop=True)
                    last.then_inc(made, 1)
                skewed(pe, head, tail, NT)


def edges_gcn(nc, g):
    with Phase(nc, "gcn") as ph:
        staged, src_rows, equal, weighted, mixed, mixed_c, summed, summed_c, indexed, scattered = ph.sems(
            "staged src_rows equal weighted mixed mixed_c summed summed_c indexed scattered")
        step, opened = ph.sems("step opened")
        win = [ph.sem(f"win{s}") for s in range(2)]
        half = [ph.sem(f"half{n}") for n in range(2)]
        edge = ph.sb("edge", [P, 2, 3, K])
        table = ph.sb("table", [P, 2, K, D])
        member = ph.sb("member", [P, 2, K, P])
        same = ph.sb("same", [P, 2, K, P])
        before = ph.sb("before", [P, K, P])
        mix = ph.sb("mix", [P, 2, K, P])
        msg = ph.sb("msg", [P, 2, K, D])
        small = ph.sb("small", [P, 2, K])
        index = ph.sb("index", [P, 2, K], I32)
        ps_src, ps_mix = ph.ps("ps_src", [P, K, P]), ph.ps("ps_mix", [P, K, P])
        ps_sum = [ph.ps(f"ps_sum{s}", [P, K, D]) for s in range(2)]
        with nc.Block() as block:
            @block.sync
            def _(sp):
                def load(c, s, i):
                    sp.wait_ge(summed, free2(c))
                    for k, b in enumerate(bases(nc, ENG.SP, g.base, c)):
                        sp.dma_start(table[:, s, k, :], g.gcn_table[ds(b, P), :]).then_inc(win[s], 16)
                pairs(sp, load)

            @block.scalar
            def _(act):
                for q in (staged, mixed_c, summed_c):
                    act.sem_inc(q, START)

                def first(c, s, i):
                    act.wait_ge(weighted, free2(c))
                    act.wait_ge(indexed, free2(c))
                    nc.scalar.activation(edge[:, s, :, :], g.edges[:, SRC:EW + 1, ds(c * K, K)], ACT.Copy
                                         ).then_inc(staged, 1)

                def second(c, s, i):
                    act.wait_ge(mixed, ready(c))
                    act.wait_ge(summed, free2(c))
                    for h in range(2):
                        last = nc.scalar.activation(mix[:, s, 4 * h:4 * h + 4, :], ps_mix[:, 4 * h:4 * h + 4, :], ACT.Copy)
                    last.then_inc(mixed_c, 1)
                    act.wait_ge(summed, ready(c))
                    act.wait_ge(scattered, free1(c))
                    nc.scalar.activation(msg[:, s, :, :], ps_sum[s][:, :, :], ACT.Copy).then_inc(summed_c, 1)
                skewed(act, first, second)

            @block.vector
            def _(dve):
                for q in (equal, weighted, indexed):
                    dve.sem_inc(q, START)

                def body(c, s, i):
                    v = nc.vector
                    chain = Chain(dve, step, c * 6)
                    dve.wait_ge(staged, ready(c))
                    dve.wait_ge(mixed, free2(c))
                    v.tensor_tensor(member[:, s], repeat(g.iota[:, :], K), spread(edge[:, s, REL, :], P), ALU.is_equal)
                    dve.wait_ge(src_rows, ready(c))
                    v.tensor_tensor(same[:, s], ps_src[:, :, :], spread(edge[:, s, SRC, :], P), ALU.is_equal
                                    ).then_inc(equal, 1)
                    dve.wait_ge(equal, ready(c))
                    chain(v.tensor_tensor(before[:, :, :], same[:, s], repeat(g.lower[:, :], K), ALU.mult))
                    v.tensor_tensor(same[:, s], same[:, s], spread(edge[:, s, EW, :], P), ALU.mult).then_inc(weighted, 1)
                    chain(v.tensor_reduce(small[:, 0, :], before[:, :, :], AX.X, ALU.add))
                    chain(v.tensor_scalar(small[:, 1, :], edge[:, s, SRC, :], -1.0, g.lane[:, 0:1], ALU.mult, ALU.add))
                    chain(v.scalar_tensor_tensor(small[:, 0, :], small[:, 0, :], 1.0, small[:, 1, :], ALU.min, ALU.mult))
                    dve.wait_ge(scattered, free1(c))
                    chain(v.tensor_tensor(index[:, s, :], small[:, 0, :], edge[:, s, SRC, :], ALU.add))
                    chain(v.tensor_copy(g.edges[:, SIDX, ds(c * K, K)], index[:, s, :]))
                    dve.sem_inc(indexed, 1)
                pairs(dve, body)

            @block.tensor
            def _(pe):
                for q in (src_rows, mixed, summed):
                    pe.sem_inc(q, START)

                def first(c, s, i):
                    pe.wait_ge(staged, ready(c))
                    pe.wait_ge(equal, free1(c))
                    for k in range(K):
                        last = nc.tensor.transpose(ps_src[:, k, :], edge[:, s, SRC, k:k + 1].broadcast_to([P, P]),
                                                   g.ident[:, :])
                    last.then_inc(src_rows, 1)

                def second(c, s, i):
                    pe.wait_ge(weighted, ready(c))
                    pe.wait_ge(mixed_c, free1(c))
                    for k in range(K):
                        last = nc.tensor.matmul(ps_mix[:, k, :], member[:, s, k, :], same[:, s, k, :], start=True, stop=True)
                    last.then_inc(mixed, 1)
                    pe.wait_ge(mixed_c, ready(c))
                    pe.wait_ge(win[s], 16 * K * (i + 1))
                    pe.wait_ge(summed_c, free2(c))
                    for k in range(K):
                        last = nc.tensor.matmul(ps_sum[s][:, k, :], mix[:, s, k, :], table[:, s, k, :], start=True, stop=True)
                    last.then_inc(summed, 1)
                skewed(pe, first, second)

            @block.gpsimd
            def _(pool):
                pool.sem_inc(scattered, START)
                prime(pool, ph, g, half)

                def body(c, s, i):
                    pool.wait_ge(summed_c, ready(c))
                    pool.wait_ge(indexed, ready(c))
                    scatter(nc, pool, g.sum0, msg[:, s], index[:, s], c, half, opened, scattered)
                pairs(pool, body)
                for h in range(2):
                    pool.wait_ge(half[h], 64 * CHUNKS + 16)


def prime(eng, ph, g, sems):
    spot = ph.sb("prime", [1, len(sems), 16])
    for n, sem in enumerate(sems):
        eng.dma_start(spot[0:1, n, :], g.w["L0_gnn_bias"][16 * n:16 * n + 16].unsqueeze(0)).then_inc(sem, 16)


def scatter(nc, pool, copies, msg, index, c, half, opened, scattered):
    for h, sem in enumerate((opened, scattered)):
        pool.wait_ge(half[h], c * 64 + 16)
        pool.sem_inc(sem, 1)
        for k in range(4 * h, 4 * h + 4):
            nc.gpsimd.indirect_dma_start(copies[k][:, :], bass.IndirectOffsetOnAxis(ap=index[:, k:k + 1], axis=0),
                                         msg[:, k, :], None, compute_op=ALU.add).then_inc(half[h], 16)


def after_gcn(nc, g):
    with Phase(nc, "gcn_end") as ph:
        loaded, used, step, stored, done, asked, given = ph.sems("loaded used step stored done asked given")
        part_in = [ph.sem(f"part{n}") for n in range(2)]
        x, total, stat = ph.sb("x", [P, NT, D]), ph.sb("total", [P, NT, D]), ph.sb("stat", [P, 2, NT])
        part = [ph.sb(f"part{n}", [P, NT, D]) for n in range(2)]
        bias = ph.sb("bias", [P, D])
        with nc.Block() as block:
            @block.sync
            def _(sp):
                sp.dma_start(x[:, :, :], nodes_view(g.xs)).then_inc(loaded, 16)
                sp.dma_start(bias[:, :], g.w["L0_gnn_bias"].partition_broadcast(P)).then_inc(loaded, 16)
                sum_loads(sp, g.sum0, part, part_in, used)
                sp.wait_ge(done, 1)
                sp.dma_start(nodes_view(g.xs), x[:, :, :]).then_inc(stored, 16)
                sp.wait_ge(stored, 16)

            @block.vector
            def _(dve):
                sum_adds(nc, dve, total, part, part_in, used)
                chain = Chain(dve, step)
                dve.wait_ge(loaded, 32)
                chain(nc.vector.tensor_tensor(total[:, :, :], total[:, :, :], repeat(bias[:, :], NT), ALU.add))
                chain(nc.vector.tensor_scalar(total[:, :, :], total[:, :, :], 0.0, None, ALU.max))
                chain(nc.vector.tensor_tensor(x[:, :, :], x[:, :, :], total[:, :, :], ALU.add))
                dve.sem_inc(done, 1)
                layernorm_relu(nc, dve, chain, x, g.node[:, :, 0:D], total, stat, asked, given)

            @block.gpsimd
            def _(pool):
                power(nc, g, pool, asked, given, 1, stat[:, 1, :], -0.5)


def sum_loads(sp, target, part, part_in, used):
    for n in range(COPIES):
        if n >= 2:
            sp.wait_ge(used, n - 1)
        sp.dma_start(part[n % 2][:, :, :], nodes_view(target[n])).then_inc(part_in[n % 2], 16)


def sum_adds(nc, dve, total, part, part_in, used):
    for n in range(COPIES):
        s = n % 2
        dve.wait_ge(part_in[s], 16 * (n // 2 + 1))
        if n == 0:
            nc.vector.tensor_copy(total[:, :, :], part[s][:, :, :]).then_inc(used, 1)
        else:
            nc.vector.tensor_tensor(total[:, :, :], total[:, :, :], part[s][:, :, :], ALU.add).then_inc(used, 1)
        dve.wait_ge(used, n + 1)


def acosh_argument(nc, v, chain, z, t, q):
    chain(v.tensor_scalar(z, z, ACOSH_MIN, None, ALU.max))
    chain(v.tensor_scalar(t, z, 1.0, None, ALU.subtract))
    chain(v.scalar_tensor_tensor(q, z, 1.0, t, ALU.add, ALU.mult))


def hyperbolic_in(nc, g):
    with Phase(nc, "log") as ph:
        step, ready_x, stored, asked, given, logs = ph.sems("step ready_x stored asked given logs")
        sq, stat = ph.sb("sq", [P, NT, D]), ph.sb("stat", [P, 5, NT])
        x = g.node
        d, t, q, yn = (stat[:, n, :] for n in range(4))
        with nc.Block() as block:
            @block.sync
            def _(sp):
                sp.dma_start(nodes_view(g.hyp_src, slice(D, 2 * D)), x[:, :, 0:D]).then_inc(stored, 16)
                sp.wait_ge(ready_x, 1)
                sp.dma_start(nodes_view(g.hyp_dst), sq[:, :, :]).then_inc(stored, 16)
                sp.wait_ge(stored, 32)

            @block.gpsimd
            def _(pool):
                power(nc, g, pool, asked, given, 1, q, 0.5)
                power(nc, g, pool, asked, given, 2, yn, 0.5)

            @block.scalar
            def _(act):
                act.wait_ge(ready_x, 2)
                nc.scalar.activation(d, t, ACT.Ln, bias=1.0).then_inc(logs, 1)

            @block.vector
            def _(dve):
                v = nc.vector
                chain = Chain(dve, step)
                chain(v.tensor_tensor(sq[:, :, :], x[:, :, 0:D], x[:, :, 0:D], ALU.mult))
                chain(v.tensor_reduce(yn, sq[:, :, 1:D], AX.X, ALU.add))
                chain(v.tensor_scalar(sq[:, :, :], x[:, :, 0:D], -1.0, None, ALU.mult))
                chain(v.tensor_copy(sq[:, :, 0:1], x[:, :, 0:1]))
                dve.sem_inc(ready_x, 1)
                chain(v.tensor_copy(d.unsqueeze(2), x[:, :, 0:1]))
                acosh_argument(nc, v, chain, d, t, q)
                ask_power(dve, asked, given, 1)
                chain(v.tensor_tensor(t, t, q, ALU.add))
                dve.sem_inc(ready_x, 1)
                ask_power(dve, asked, given, 2)
                chain(v.tensor_scalar(yn, yn, 1e-7, None, ALU.max))
                chain(v.reciprocal(yn, yn))
                dve.wait_ge(logs, 1)
                chain(v.tensor_tensor(d, d, yn, ALU.mult))
                dve.wait_ge(stored, 32)
                chain(v.tensor_tensor(x[:, :, 0:D], x[:, :, 0:D], spread(d, D), ALU.mult))
                chain(v.memset(x[:, :, 0:1], 0.0))


def edges_hyperbolic(nc, g):
    w = g.w
    with Phase(nc, "hyp") as ph:
        (staged, gather_at, members, turned, turned_c, from_dst, h_kept, taken, squared, logged, rooted, argued, geo,
         joined, src_rows, equal, counted, count_c) = ph.sems(
            "staged gather_at members turned turned_c from_dst h_kept taken squared logged rooted argued geo "
            "joined src_rows equal counted count_c")
        (pre, act1, pre2, act2, score, tanh, weighted, summed, summed_c, opened, scattered, w_in,
         step_a, step_b, step_c, step_d, added, cleared, inverted, kept, mark_a, mark_p) = ph.sems(
            "pre act1 pre2 act2 score tanh weighted summed summed_c opened scattered w_in "
            "step_a step_b step_c step_d added cleared inverted kept mark_a mark_p")
        win, got = ([ph.sem(f"{n}{q}") for q in range(4)] for n in ("win", "got"))
        half = [ph.sem(f"half{n}") for n in range(2)]
        edge = ph.sb("edge", [P, 4, SIDX + 1, K])
        src_at, sum_at = ph.sb("src_at", [P, 4, K], I32), ph.sb("sum_at", [P, 2, K], I32)
        table = ph.sb("table", [P, 2, K, 3 * D])
        from_src = ph.sb("from_src", [P, 4, K, 2 * D])
        spot = g.node[:, :, :].rearrange("p t d -> p (t d)")
        memberT = spot[:, 0:2 * CE].rearrange("p (s k e) -> p s k e", s=2, k=K)
        same = spot[:, 2 * CE:6 * CE].rearrange("p (s k e) -> p s k e", s=4, k=K)
        row = ph.sb("row", [P, K, D])
        hid = ph.sb("hid", [P, 2, K // 2, P])
        from_h = ph.sb("from_h", [P, 2, K, D])
        member = ph.sb("member", [P, K, P], BF16)
        kinds = ph.sb("kinds", [P, K, R], BF16)
        part = ph.sb("part", [P, K, D])
        msg = ph.sb("msg", [P, 2, K, D])
        prod = ph.sb("prod", [P, K, D])
        small = ph.sb("small", [P, 6, K])
        lq, rt, dist, th = (ph.sb(n, [P, K]) for n in ("lq", "rt", "dist", "th"))
        counts = ph.sb("counts", [R, NR])
        w2, w3 = ph.sb("w2", [P, 2, D]), ph.sb("w3", [P, 2])
        b1, b2 = ph.sb("b1", [P, 1]), ph.sb("b2", [P, 1])
        b3 = ph.sb("b3", [P, 2])
        wc = ph.sb("wc", [P, 2, D])
        ps_src = ph.ps("ps_src", [P, K, P])
        ps_a, ps_b = ph.ps("ps_a", [P, 512]), ph.ps("ps_b", [P, 512])
        ps_dst = ph.ps("ps_dst", [P, K // 2, 512])
        ps_cnt = ps_src[0:R]
        ps_pre, ps_score, ps_turn = ps_a[:, :], ps_a[:, 0:K], ps_a[:, :].bitcast(BF16).rearrange("p (k e) -> p k e", k=K)
        ps_pre2, ps_sum = ps_b[:, :], ps_b[:, :].rearrange("p (k d) -> p k d", k=K)
        x_dst, q_dst, h_dst = (ps_dst[:, :, 0:6 * D].rearrange("p a (b n d) -> p a b n d", b=2, n=3)[:, :, :, n, :]
                               for n in range(3))

        def pairs_of(ap):
            return ap.rearrange("p (a b) d -> p a b d", b=2)

        with nc.Block() as block:
            @block.sync
            def _(sp):
                sp.wait_ge(cleared, 3)
                for n in range(2):
                    half_p = slice(n * D, (n + 1) * D)
                    for d, a in ((w2[half_p, n, :], w["L1_gnn_w2"]), (w3[half_p, n:n + 1], w["L1_gnn_w3"]),
                                 (b1[half_p, :], w["L1_gnn_b1"].unsqueeze(1)), (b2[half_p, :], w["L1_gnn_b2"].unsqueeze(1))):
                        sp.dma_start(d, a).then_inc(w_in, 16)
                sp.dma_start(b3[:, 0:1], w["L1_gnn_b3"].partition_broadcast(P)).then_inc(w_in, 16)
                for n in range(2):
                    sp.dma_start(wc[:, n, :], w["L1_gnn_w1"][2 * D + n, :].partition_broadcast(P)).then_inc(w_in, 16)

                def load(c, q, i):
                    sp.wait_ge(from_dst, free2(c))
                    for k, b in enumerate(bases(nc, ENG.SP, g.base, c)):
                        sp.dma_start(table[:, q % 2, k, :], g.hyp_dst[ds(b, P), :]).then_inc(win[q], 16)
                rounds(sp, [(load, 0)])

            @block.gpsimd
            def _(pool):
                pool.sem_inc(scattered, START)
                prime(pool, ph, g, half)

                def gather(c, q, i):
                    pool.wait_ge(joined, free4(c))
                    pool.wait_ge(gather_at, ready(c))
                    pool.sem_inc(opened, 1)
                    for k in range(K):
                        nc.gpsimd.indirect_dma_start(
                            from_src[:, q, k, :], None, g.hyp_src[:, :],
                            bass.IndirectOffsetOnAxis(ap=src_at[:, q, k:k + 1], axis=0)).then_inc(got[q], 16)

                def send(c, q, i):
                    pool.wait_ge(summed_c, ready(c))
                    scatter(nc, pool, g.sum1, msg[:, q % 2], sum_at[:, q % 2], c, half, opened, scattered)
                rounds(pool, [(gather, 3), (send, 0)])
                for h in range(2):
                    pool.wait_ge(half[h], 64 * CHUNKS + 16)

            @block.scalar
            def _(act):
                for q in (staged, gather_at, turned_c, logged, rooted, geo, tanh, summed_c, act1, act2, h_kept):
                    act.sem_inc(q, START)
                act.wait_ge(w_in, 11 * 16)
                nc.scalar.activation(b3[:, 1:2], b3[:, 0:1], ACT.Copy, scale=0.5).then_inc(added, 1)
                act.wait_ge(added, 1)

                def fields(c, q, i):
                    act.wait_ge(weighted, free4(c))
                    alone(act, mark_a)
                    nc.scalar.activation(edge[:, q, :, :], g.edges[:, 0:SIDX + 1, ds(c * K, K)], ACT.Copy
                                         ).then_inc(staged, 1)
                    nc.scalar.activation(src_at[:, q, :], g.edges[:, SRC, ds(c * K, K)], ACT.Copy
                                         ).then_inc(gather_at, 1)

                def turn_out(c, q, i):
                    act.wait_ge(turned, ready(c))
                    act.wait_ge(from_dst, free2(c))
                    nc.scalar.activation(memberT[:, q % 2, :, :], ps_turn[:, :, :], ACT.Copy).then_inc(turned_c, 1)

                def distance(c, q, i):
                    act.wait_ge(squared, ready(c))
                    alone(act, mark_a)
                    nc.scalar.preload_act_table_set("natural_log_exp_and_others")
                    nc.scalar.activation(lq[:, :], small[:, 2, :], ACT.Ln).then_inc(logged, 1)
                    act.wait_ge(logged, ready(c))
                    nc.scalar.activation(rt[:, :], lq[:, :], ACT.Exp, scale=0.5).then_inc(rooted, 1)
                    act.wait_ge(argued, ready(c))
                    nc.scalar.activation(dist[:, :], small[:, 3, :], ACT.Ln, bias=1.0).then_inc(geo, 1)

                def keep_h(c, q, i):
                    act.wait_ge(taken, ready(c))
                    act.wait_ge(weighted, free2(c))
                    nc.scalar.activation(pairs_of(from_h[:, q % 2]), h_dst, ACT.Copy).then_inc(h_kept, 1)

                def layer1(c, q, i):
                    act.wait_ge(pre, ready(c))
                    act.wait_ge(pre2, free1(c))
                    nc.scalar.activation(hid[:, 0].rearrange("p k e -> p (k e)"), ps_pre, ACT.Silu, bias=b1[:, 0:1]
                                         ).then_inc(act1, 1)

                def layer2(c, q, i):
                    act.wait_ge(pre2, ready(c))
                    act.wait_ge(score, free1(c))
                    nc.scalar.activation(hid[:, 1].rearrange("p k e -> p (k e)"), ps_pre2, ACT.Silu, bias=b2[:, 0:1]
                                         ).then_inc(act2, 1)

                def attention(c, q, i):
                    act.wait_ge(score, ready(c))
                    act.wait_ge(weighted, free1(c))
                    nc.scalar.activation(th[:, :], ps_score, ACT.Tanh, scale=0.5, bias=b3[:, 1:2]).then_inc(tanh, 1)

                def out(c, q, i):
                    act.wait_ge(summed, ready(c))
                    act.wait_ge(scattered, free1(c))
                    alone(act, mark_a)
                    nc.scalar.activation(sum_at[:, q % 2, :], g.edges[:, SIDX, ds(c * K, K)], ACT.Copy)
                    nc.scalar.activation(msg[:, q % 2, :, :], ps_sum, ACT.Copy).then_inc(summed_c, 1)
                rounds(act, [(layer1, 0), (layer2, 0), (keep_h, 1), (fields, 3), (attention, 0), (distance, 1),
                             (turn_out, 2), (out, 0)])

            @block.vector
            def _(dve):
                v = nc.vector
                for q in (members, equal, squared, taken, argued, joined, weighted, count_c):
                    dve.sem_inc(q, START)
                v.memset(w2[:, :, :], 0.0).then_inc(cleared, 1)
                v.memset(w3[:, :], 0.0).then_inc(cleared, 1)
                v.memset(counts[:, :], 0.0).then_inc(cleared, 1)
                dve.wait_ge(cleared, 3)
                dve.wait_ge(w_in, 11 * 16)

                def zero_ones(c, q, i):
                    dve.wait_ge(staged, ready(c))
                    dve.wait_ge(counted, free1(c))
                    v.tensor_tensor(member[:, :, :], repeat(g.iota[:, :], K), spread(edge[:, q, REL, :], P), ALU.is_equal
                                    ).then_inc(members, 1)

                def relations(c, q, i):
                    v.tensor_tensor(kinds[:, :, :], repeat(g.iota[:, 0:R], K), spread(edge[:, q, TYPE, :], R),
                                    ALU.is_equal)

                def same_src(c, q, i):
                    dve.wait_ge(src_rows, ready(c))
                    dve.wait_ge(summed, free4(c))
                    v.tensor_tensor(same[:, q], ps_src[:, :, :], spread(edge[:, q, SRC, :], P), ALU.is_equal
                                    ).then_inc(equal, 1)

                def argument(c, q, i):
                    regs = bases(nc, ENG.DVE, g.base, c)
                    src = from_src[:, q, :, 0:D]
                    z, t, square = (small[:, n, :] for n in range(3))

                    def count_tile(k):
                        if k:
                            dve.wait_ge(step_c, c * K + k)
                        window = counts[:, ds(regs[k], P)]
                        v.tensor_tensor(window, window, ps_cnt[:, k, :], ALU.add).then_inc(step_c, 1)

                    dve.wait_ge(from_dst, ready(c))
                    dve.wait_ge(got[q], 16 * K * (i + 1))
                    v.tensor_tensor(pairs_of(prod[:, :, :]), x_dst, pairs_of(from_src[:, q, :, D:2 * D]), ALU.mult
                                    ).then_inc(step_a, 1)
                    dve.wait_ge(counted, ready(c))
                    count_tile(0)
                    dve.wait_ge(step_a, c * 6 + 1)
                    v.tensor_reduce(z, prod[:, :, :], AX.X, ALU.add).then_inc(step_a, 1)
                    count_tile(1)
                    dve.wait_ge(step_a, c * 6 + 2)
                    v.tensor_scalar(z, z, ACOSH_MIN, None, ALU.max).then_inc(step_a, 1)
                    count_tile(2)
                    dve.wait_ge(step_a, c * 6 + 3)
                    v.tensor_scalar(t, z, 1.0, None, ALU.subtract).then_inc(step_a, 1)
                    count_tile(3)
                    dve.wait_ge(step_a, c * 6 + 4)
                    v.scalar_tensor_tensor(square, z, 1.0, t, ALU.add, ALU.mult).then_inc(step_a, 1)
                    count_tile(4)
                    dve.wait_ge(step_a, c * 6 + 5)
                    dve.sem_inc(squared, 1)
                    v.tensor_tensor(pairs_of(src), pairs_of(src), q_dst, ALU.add).then_inc(step_a, 1)
                    count_tile(5)
                    dve.wait_ge(step_a, c * 6 + 6)
                    dve.sem_inc(taken, 1)

                def last_counts(c, q, i):
                    regs = bases(nc, ENG.DVE, g.base, c, K - 2, 2)
                    for n, k in enumerate((K - 2, K - 1)):
                        dve.wait_ge(step_c, c * K + k)
                        window = counts[:, ds(regs[n], P)]
                        v.tensor_tensor(window, window, ps_cnt[:, k, :], ALU.add).then_inc(step_c, 1)
                    dve.wait_ge(step_c, c * K + K)
                    dve.sem_inc(count_c, 1)

                def inputs(c, q, i):
                    chain = Chain(dve, step_b, c * 5)
                    src = from_src[:, q, :, 0:D]
                    dve.wait_ge(rooted, ready(c))
                    chain(v.tensor_tensor(small[:, 3, :], small[:, 1, :], rt[:, :], ALU.add))
                    dve.sem_inc(argued, 1)
                    chain(v.tensor_tensor(prod[:, :, :], spread(edge[:, q, EW1, :], D), repeat(wc[:, 0, :], K), ALU.mult))
                    chain(v.tensor_tensor(src, src, prod[:, :, :], ALU.add))
                    dve.wait_ge(geo, ready(c))
                    chain(v.tensor_tensor(prod[:, :, :], spread(dist[:, :], D), repeat(wc[:, 1, :], K), ALU.mult))
                    dve.wait_ge(pre, free1(c))
                    chain(v.tensor_tensor(row[:, :, :], src, prod[:, :, :], ALU.add))
                    dve.sem_inc(joined, 1)

                def messages(c, q, i):
                    chain = Chain(dve, step_d, c * 2)
                    dve.wait_ge(tanh, ready(c))
                    chain(v.tensor_scalar(small[:, 4, :], th[:, :], 0.5, 0.5, ALU.mult, ALU.add))
                    chain(v.tensor_tensor(small[:, 5, :], small[:, 4, :], edge[:, q, EW1, :], ALU.mult))
                    dve.wait_ge(h_kept, ready(c))
                    dve.wait_ge(summed, free1(c))
                    v.tensor_tensor(part[:, :, :], from_h[:, q % 2], spread(small[:, 5, :], D), ALU.mult
                                    ).then_inc(weighted, 1)
                rounds(dve, [(argument, 1), (zero_ones, 2), (last_counts, 1), (relations, 2), (messages, 0), (same_src, 2), (inputs, 1)])

            @block.tensor
            def _(pe):
                for q in (turned, from_dst, src_rows, counted, summed, pre, pre2, score):
                    pe.sem_inc(q, START)
                pe.wait_ge(w_in, 11 * 16)

                def source_rows(c, q, i):
                    pe.wait_ge(staged, ready(c))
                    pe.wait_ge(count_c, free1(c))
                    for k in range(K):
                        last = nc.tensor.transpose(ps_src[:, k, :], edge[:, q, SRC, k:k + 1].broadcast_to([P, P]),
                                                   g.ident[:, :])
                    last.then_inc(src_rows, 1)

                def turn_members(c, q, i):
                    pe.wait_ge(members, ready(c))
                    pe.wait_ge(tanh, free2(c))
                    for k in range(K):
                        last = nc.tensor.transpose(ps_turn[:, k, :], member[:, k, :], g.ident16[:, :])
                    last.then_inc(turned, 1)

                def count(c, q, i):
                    pe.wait_ge(equal, ready(c))
                    for k in range(K):
                        last = nc.tensor.matmul(ps_cnt[:, k, :], kinds[:, k, :], member[:, k, :], start=True, stop=True)
                    last.then_inc(counted, 1)

                def read_dst(c, q, i):
                    pe.wait_ge(turned_c, ready(c))
                    pe.wait_ge(win[q], 16 * K * (i + 1))
                    pe.wait_ge(taken, free1(c))
                    pe.wait_ge(h_kept, free1(c))
                    for k in range(K):
                        last = nc.tensor.matmul(ps_dst[:, k // 2, k % 2 * 3 * D:(k % 2 + 1) * 3 * D],
                                                memberT[:, q % 2, k, :], table[:, q % 2, k, :], start=True, stop=True)
                    last.then_inc(from_dst, 1)

                def layer1(c, q, i):
                    pe.wait_ge(joined, ready(c))
                    if not isinstance(c, int) or c < CHUNKS - 1:
                        pe.wait_ge(turned_c, ready(c + 1))
                    alone(pe, mark_p)
                    for k in range(0, K, 2):
                        last = nc.tensor.transpose(ps_pre[:, k // 2 * P:(k // 2 + 1) * P],
                                                   row[:, k:k + 2, :].rearrange("p k d -> p (k d)"), g.ident[:, :])
                    last.then_inc(pre, 1)

                def layer2(c, q, i):
                    pe.wait_ge(act1, ready(c))
                    pe.wait_ge(summed_c, free1(c))
                    alone(pe, mark_p)
                    nc.tensor.matmul(ps_pre2, w2[:, :, :].rearrange("p a d -> p (a d)"),
                                     hid[:, 0].rearrange("p k e -> p (k e)"), start=True, stop=True).then_inc(pre2, 1)

                def scores(c, q, i):
                    pe.wait_ge(act2, ready(c))
                    for k in range(0, K, 2):
                        last = nc.tensor.matmul(ps_score[:, k:k + 2], hid[:, 1, k // 2, :], w3[:, :], start=True, stop=True)
                    last.then_inc(score, 1)

                def combine(c, q, i):
                    pe.wait_ge(weighted, ready(c))
                    for k in range(K):
                        last = nc.tensor.matmul(ps_sum[:, k, :], same[:, q, k, :], part[:, k, :], start=True, stop=True)
                    last.then_inc(summed, 1)
                rounds(pe, [(layer1, 0), (layer2, 0), (scores, 0), (turn_members, 2), (source_rows, 2), (combine, 0),
                            (count, 2), (read_dst, 2)])

        columns_to_nodes(nc, g, ph, counts, R, [ps_dst[:, n, :] for n in range(2)])
        with nc.Block() as block:
            @block.vector
            def _(dve):
                chain = Chain(dve, inverted)
                chain(nc.vector.tensor_scalar(g.node[:, :, 0:R], g.node[:, :, 0:R], 1.0, None, ALU.max))
                chain(nc.vector.reciprocal(g.node[:, :, 0:R], g.node[:, :, 0:R]))

            @block.sync
            def _(sp):
                sp.wait_ge(inverted, 2)
                sp.dma_start(nodes_view(g.inv_count, slice(0, R)), g.node[:, :, 0:R]).then_inc(kept, 16)
                sp.wait_ge(kept, 16)


def columns_to_nodes(nc, g, outer, sums, rows, ps):
    with Phase(nc, outer.name + "_turn") as ph:
        staged, turned, copied, mark_a, mark_p, mark_d = ph.sems("staged turned copied mark_a mark_p mark_d")
        stage = ph.sb("stage", [rows, 2, P])
        with nc.Block() as block:
            @block.scalar
            def _(act):
                act.sem_inc(staged, START)

                def body(t, s, i):
                    act.wait_ge(turned, free2(t))
                    alone(act, mark_a)
                    nc.scalar.activation(stage[:, s, :], sums[0:rows, ds(t * P, P)], ACT.Copy).then_inc(staged, 1)
                pairs(act, body, NT)

            @block.tensor
            def _(pe):
                pe.sem_inc(turned, START)

                def body(t, s, i):
                    pe.wait_ge(staged, ready(t))
                    pe.wait_ge(copied, free2(t))
                    alone(pe, mark_p)
                    nc.tensor.matmul(ps[s][:, 0:rows], stage[:, s, :], g.ident[0:rows, 0:rows], start=True, stop=True
                                     ).then_inc(turned, 1)
                pairs(pe, body, NT)

            @block.vector
            def _(dve):
                dve.sem_inc(copied, START)

                def body(t, s, i):
                    dve.wait_ge(turned, ready(t))
                    alone(dve, mark_d)
                    nc.vector.tensor_copy(g.node[:, ds(t, 1), 0:rows].rearrange("p o r -> p (o r)"), ps[s][:, 0:rows]
                                          ).then_inc(copied, 1)
                pairs(dve, body, NT)


def after_hyperbolic(nc, g):
    with Phase(nc, "hyp_end") as ph:
        loaded, used, step, stored, done, asked, given, acted = ph.sems("loaded used step stored done asked given acted")
        part_in = [ph.sem(f"part{n}") for n in range(2)]
        x, y, stat = ph.sb("x", [P, NT, D]), ph.sb("y", [P, NT, D]), ph.sb("stat", [P, 4, NT])
        part = [ph.sb(f"part{n}", [P, NT, D]) for n in range(2)]
        gamma, beta = ph.sb("gamma", [P, D]), ph.sb("beta", [P, D])
        h = g.node[:, :, 0:D]
        with nc.Block() as block:
            @block.sync
            def _(sp):
                sp.dma_start(x[:, :, :], nodes_view(g.xs)).then_inc(loaded, 16)
                sp.dma_start(h, nodes_view(g.hyp_dst, slice(2 * D, 3 * D))).then_inc(loaded, 16)
                sp.dma_start(gamma[:, :], g.w["L1_gnn_gamma"].partition_broadcast(P)).then_inc(loaded, 16)
                sp.dma_start(beta[:, :], g.w["L1_gnn_beta"].partition_broadcast(P)).then_inc(loaded, 16)
                sum_loads(sp, g.sum1, part, part_in, used)
                sp.wait_ge(done, 4)
                sp.dma_start(nodes_view(g.xs), x[:, :, :]).then_inc(stored, 16)
                sp.wait_ge(stored, 16)

            @block.gpsimd
            def _(pool):
                power(nc, g, pool, asked, given, 1, stat[:, 1, :], -0.5)
                power(nc, g, pool, asked, given, 2, stat[:, 2, :], 0.5)
                power(nc, g, pool, asked, given, 3, stat[:, 1, :], -0.5)

            @block.scalar
            def _(act):
                act.wait_ge(done, 2)
                nc.scalar.activation(stat[:, 3, :], stat[:, 2, :], ACT.Tanh, scale=0.5).then_inc(acted, 1)
                act.wait_ge(done, 3)
                nc.scalar.activation(y[:, :, :], y[:, :, :], ACT.Silu).then_inc(acted, 1)

            @block.vector
            def _(dve):
                v = nc.vector
                sum_adds(nc, dve, y, part, part_in, used)
                chain = Chain(dve, step)
                dve.wait_ge(loaded, 64)
                chain(v.tensor_tensor(y[:], y[:], h, ALU.add))
                chain(v.tensor_reduce(stat[:, 0, :], y[:], AX.X, ALU.add))
                chain(v.tensor_scalar(stat[:, 0, :], stat[:, 0, :], 1.0 / D, None, ALU.mult))
                chain(v.tensor_tensor(y[:], y[:], spread(stat[:, 0, :], D), ALU.subtract))
                chain(v.tensor_tensor(part[0][:], y[:], y[:], ALU.mult))
                chain(v.tensor_reduce(stat[:, 1, :], part[0][:], AX.X, ALU.add))
                chain(v.tensor_scalar(stat[:, 1, :], stat[:, 1, :], 1.0 / D, 1e-5, ALU.mult, ALU.add))
                ask_power(dve, asked, given, 1)
                chain(v.tensor_tensor(y[:], y[:], spread(stat[:, 1, :], D), ALU.mult))
                chain(v.tensor_tensor(y[:], y[:], repeat(gamma[:, :], NT), ALU.mult))
                chain(v.tensor_tensor(y[:], y[:], repeat(beta[:, :], NT), ALU.add))
                chain(v.tensor_tensor(part[0][:], y[:], y[:], ALU.mult))
                chain(v.tensor_reduce(stat[:, 2, :], part[0][:, :, 1:D], AX.X, ALU.add))
                ask_power(dve, asked, given, 2)
                chain(v.tensor_scalar(stat[:, 2, :], stat[:, 2, :], 1e-7, None, ALU.max))
                dve.sem_inc(done, 2)
                chain(v.reciprocal(stat[:, 0, :], stat[:, 2, :]))
                dve.wait_ge(acted, 1)
                chain(v.tensor_tensor(stat[:, 0, :], stat[:, 0, :], stat[:, 3, :], ALU.mult))
                chain(v.tensor_tensor(y[:], y[:], spread(stat[:, 0, :], D), ALU.mult))
                dve.sem_inc(done, 1)
                dve.wait_ge(acted, 2)
                chain(v.tensor_tensor(part[0][:], y[:], y[:], ALU.mult))
                chain(v.tensor_reduce(stat[:, 0, :], part[0][:, :, 1:D], AX.X, ALU.add))
                chain(v.tensor_scalar(stat[:, 1, :], stat[:, 0, :], -1.0, 1.0, ALU.mult, ALU.add))
                chain(v.tensor_scalar(stat[:, 1, :], stat[:, 1, :], 1e-7, None, ALU.max))
                chain(v.reciprocal(stat[:, 1, :], stat[:, 1, :]))
                chain(v.tensor_scalar(stat[:, 0, :], stat[:, 0, :], 1.0, None, ALU.add))
                chain(v.tensor_tensor(y[:], y[:], spread(stat[:, 1, :], D), ALU.mult))
                chain(v.tensor_scalar(y[:], y[:], 2.0, None, ALU.mult))
                chain(v.tensor_tensor(y[:, :, 0:1], stat[:, 0, :].unsqueeze(2), stat[:, 1, :].unsqueeze(2), ALU.mult))
                chain(v.tensor_tensor(x[:], x[:], y[:], ALU.add))
                layernorm_relu(nc, dve, chain, x, h, y, stat, asked, given, 3)
                dve.sem_inc(done, 1)


def edges_attention(nc, g, name):
    with Phase(nc, name) as ph:
        (staged, gather_at, members, turned, turned_c, dst_at, logit, logit_t, scanned, back, back_u, tops, expo,
         shift_e, shifted, filled, summed, added) = ph.sems(
            "staged gather_at members turned turned_c dst_at logit logit_t scanned back back_u tops expo "
            "shift_e shifted filled summed added")
        step_a, step_b, step_c, opened, cleared, mark_a, mark_p = ph.sems(
            "step_a step_b step_c opened cleared mark_a mark_p")
        win, mask_in, got = ([ph.sem(f"{n}{q}") for q in range(4)] for n in ("win", "mask_in", "got"))
        rows = D + 2 * H
        edge = ph.sb("edge", [P, 4, END + 1, K])
        src_at = ph.sb("src_at", [P, 4, K], I32)
        table = ph.sb("table", [P, 4, K, H])
        masks = ph.sb("masks", [H, 2, 2, CE])
        from_src = ph.sb("from_src", [P, 4, K, D + H])
        spot = g.node[:, :, :].rearrange("p t d -> p (t d)")
        member = spot[:, 0:4 * CE].rearrange("p (s k e) -> p s k e", s=4, k=K)
        memberT = spot[:, 4 * CE:5 * CE].rearrange("p (k e) -> p k e", k=K)
        leaky = ph.sb("leaky", [P, 2, K, H])
        fwd, top = ph.sb("fwd", [H, 2, CE]), ph.sb("top", [H, CE])
        arg = ph.sb("arg", [P, K, H])
        shift = ph.sb("shift", [H, 2])
        msg = ph.sb("msg", [P, 2, K, rows])
        sums = ph.sb("sums", [rows, NR])
        ps_turn, ps_log, ps_sum = (ph.ps(n, [P, K, P]) for n in ("ps_turn", "ps_log", "ps_sum"))
        ps_dst, ps_top = ph.ps("ps_dst", [P, 512]), ph.ps("ps_top", [P, 512])
        dst_v = ps_dst[:, 0:K * H].rearrange("p (k h) -> p k h", k=K)
        top_v = ps_top[:, 0:K * H].rearrange("p (k h) -> p k h", k=K)
        log_flat = ps_log[0:H, :, :].rearrange("p k e -> p (k e)")
        with nc.Block() as block:
            @block.sync
            def _(sp):
                def load_masks(c, q, i):
                    sp.wait_ge(scanned, free2(c))
                    for n, m in enumerate((g.first_mask, g.last_mask)):
                        sp.dma_start(masks[:, q % 2, n, :], m[ds(c * CE, CE)].partition_broadcast(H)
                                     ).then_inc(mask_in[q], 16)

                def load_windows(c, q, i):
                    sp.wait_ge(dst_at, free4(c))
                    for k, b in enumerate(bases(nc, ENG.SP, g.base, c)):
                        sp.dma_start(table[:, q, k, :], g.gat_dst[ds(b, P), :]).then_inc(win[q], 16)
                rounds(sp, [(load_windows, 3), (load_masks, 1)])

            @block.gpsimd
            def _(pool):
                def gather(c, q, i):
                    pool.wait_ge(filled, free4(c))
                    pool.wait_ge(gather_at, ready(c))
                    pool.sem_inc(opened, 1)
                    for k in range(K):
                        nc.gpsimd.indirect_dma_start(
                            from_src[:, q, k, :], None, g.gat_src[:, :],
                            bass.IndirectOffsetOnAxis(ap=src_at[:, q, k:k + 1], axis=0)).then_inc(got[q], 16)
                rounds(pool, [(gather, 0)])

            @block.scalar
            def _(act):
                for q in (staged, gather_at, turned_c, expo, shift_e):
                    act.sem_inc(q, START)

                def fields(c, q, i):
                    act.wait_ge(filled, free4(c))
                    alone(act, mark_a)
                    nc.scalar.activation(src_at[:, q, :], g.edges[:, SRC, ds(c * K, K)], ACT.Copy
                                         ).then_inc(gather_at, 1)
                    nc.scalar.activation(edge[:, q, :, :], g.edges[:, 0:END + 1, ds(c * K, K)], ACT.Copy
                                         ).then_inc(staged, 1)

                def turn_out(c, q, i):
                    act.wait_ge(turned, ready(c))
                    act.wait_ge(dst_at, free1(c))
                    for h in range(2):
                        last = nc.scalar.activation(memberT[:, 4 * h:4 * h + 4, :], ps_turn[:, 4 * h:4 * h + 4, :],
                                                    ACT.Copy)
                    last.then_inc(turned_c, 1)

                def exponents(c, q, i):
                    act.wait_ge(back_u, ready(c))
                    nc.scalar.activation(msg[:, q % 2, :, D:D + H], arg[:, :, :], ACT.Exp).then_inc(expo, 1)

                def exp_shift(c, q, i):
                    act.wait_ge(scanned, ready(c))
                    nc.scalar.activation(shift[:, 1:2], shift[:, 0:1], ACT.Exp).then_inc(shift_e, 1)
                rounds(act, [(fields, 4), (exponents, 1), (turn_out, 3), (exp_shift, 2)])

            @block.vector
            def _(dve):
                v = nc.vector
                for q in (members, logit, scanned, back_u, shifted, filled):
                    dve.sem_inc(q, START)
                dve.sem_inc(added, 2 * START)
                v.memset(sums[:, :], 0.0).then_inc(cleared, 1)
                v.memset(fwd[:, 1, :], -BIG).then_inc(cleared, 1)
                dve.wait_ge(cleared, 2)

                def zero_ones(c, q, i):
                    dve.wait_ge(staged, ready(c))
                    dve.wait_ge(summed, half_ready(c, 1) - 8)
                    v.tensor_tensor(member[:, q], repeat(g.iota[:, :], K), spread(edge[:, q, REL, :], P), ALU.is_equal
                                    ).then_inc(members, 1)

                def tops_of(c, q, i):
                    dve.wait_ge(back, ready(c))
                    dve.wait_ge(summed, half_ready(c, 1) - 4)
                    v.tensor_tensor(msg[:, q % 2, :, D + H:rows], top_v, spread(edge[:, q, END, :], H), ALU.mult
                                    ).then_inc(tops, 1)

                def arguments(c, q, i):
                    dve.wait_ge(expo, free1(c))
                    v.tensor_tensor(arg[:, :, :], leaky[:, q % 2], top_v, ALU.subtract).then_inc(back_u, 1)

                def logits(c, q, i):
                    dve.wait_ge(dst_at, ready(c))
                    dve.wait_ge(got[q], 16 * K * (i + 1))
                    v.tensor_tensor(leaky[:, q % 2], dst_v, from_src[:, q, :, D:D + H], ALU.add).then_inc(step_a, 1)

                def leaky_logits(c, q, i):
                    one = leaky[:, q % 2].rearrange("p k h -> p (k h)")
                    dve.wait_ge(step_a, c + 1)
                    v.scalar_tensor_tensor(one, one, LRELU, one, ALU.mult, ALU.max).then_inc(logit, 1)

                def messages(c, q, i):
                    s = q % 2
                    dve.wait_ge(expo, ready(c))
                    v.tensor_tensor(
                        msg[:, s, :, 0:D].rearrange("p k (h c) -> p k h c", h=H),
                        from_src[:, q, :, 0:D].rearrange("p k (h c) -> p k h c", h=H),
                        msg[:, s, :, D:D + H].unsqueeze(3).broadcast_to([P, K, H, D // H]), ALU.mult).then_inc(filled, 1)

                def maxima_so_far(c, q, i):
                    s = q % 2
                    dve.wait_ge(logit_t, ready(c))
                    dve.wait_ge(mask_in[q], 16 * 2 * (i + 1))
                    v.tensor_tensor_scan(fwd[:, s, :], masks[:, s, 0, :], log_flat, fwd[:, 1 - s, CE - 1:CE], ALU.add,
                                         ALU.max).then_inc(step_b, 1)

                def maxima(c, q, i):
                    s = q % 2
                    dve.wait_ge(step_b, c * 3 + 1)
                    dve.wait_ge(back, free1(c))
                    v.tensor_tensor_scan(top[:, ::-1], masks[:, s, 1, ::-1], fwd[:, s, ::-1], -BIG, ALU.add, ALU.max
                                         ).then_inc(step_b, 1)

                def shift_by(c, q, i):
                    dve.wait_ge(step_b, c * 3 + 2)
                    v.tensor_tensor(shift[:, 0:1], fwd[:, 1 - q % 2, CE - 1:CE], top[:, 0:1], ALU.subtract
                                    ).then_inc(step_b, 1)
                    dve.wait_ge(step_b, c * 3 + 3)
                    v.tensor_scalar(shift[:, 0:1], shift[:, 0:1], 0.0, None, ALU.min).then_inc(scanned, 1)

                def rescale(c, q, i):
                    (first,) = bases(nc, ENG.DVE, g.base, c, 0, 1)
                    v.tensor_tensor(sums[:, ds(first, 1)], sums[:, ds(first, 1)], ps_top[0:rows, K * H:K * H + 1],
                                    ALU.mult).then_inc(shifted, 1)

                def add(first, count):
                    def step(c, q, i):
                        regs = bases(nc, ENG.DVE, g.base, c, first, count)
                        for n in range(count):
                            k = first + n
                            if k == 0:
                                dve.wait_ge(shifted, ready(c))
                            else:
                                dve.wait_ge(step_c, c * K + k)
                            if k % 4 == 0:
                                dve.wait_ge(summed, half_ready(c, k // 4))
                            window = sums[:, ds(regs[n], P)]
                            v.tensor_tensor(window, window, ps_sum[0:rows, k, :], ALU.add).then_inc(step_c, 1)
                            if k % 4 == 3:
                                dve.wait_ge(step_c, c * K + k + 1)
                                dve.sem_inc(added, 1)
                    return step
                rounds(dve, [(tops_of, 1), (add(0, 1), 0), (arguments, 1), (add(1, 1), 0), (logits, 2), (add(2, 1), 0),
                             (leaky_logits, 2), (add(3, 1), 0), (messages, 1), (add(4, 1), 0), (maxima_so_far, 2),
                             (add(5, 1), 0), (maxima, 2), (add(6, 1), 0), (shift_by, 2), (add(7, 1), 0), (rescale, 1),
                             (zero_ones, 4)])

            @block.tensor
            def _(pe):
                for q in (turned, dst_at, logit_t, back):
                    pe.sem_inc(q, START)
                pe.sem_inc(summed, 2 * START)

                def turn_members(c, q, i):
                    pe.wait_ge(members, ready(c))
                    pe.wait_ge(turned_c, free1(c))
                    for k in range(K):
                        last = nc.tensor.transpose(ps_turn[:, k, :], member[:, q, k, :], g.ident[:, :])
                    last.then_inc(turned, 1)

                def read_dst(c, q, i):
                    pe.wait_ge(turned_c, ready(c))
                    pe.wait_ge(win[q], 16 * K * (i + 1))
                    pe.wait_ge(logit, free1(c))
                    for k in range(K):
                        last = nc.tensor.matmul(dst_v[:, k, :], memberT[:, k, :], table[:, q, k, :], start=True, stop=True)
                    last.then_inc(dst_at, 1)

                def turn_logits(c, q, i):
                    pe.wait_ge(logit, ready(c))
                    pe.wait_ge(scanned, free1(c))
                    for k in range(K):
                        last = nc.tensor.transpose(ps_log[0:H, k, :], leaky[:, q % 2, k, :], g.ident[:, :])
                    last.then_inc(logit_t, 1)

                def turn_maxima(c, q, i):
                    pe.wait_ge(scanned, ready(c))
                    pe.wait_ge(back_u, free1(c))
                    pe.wait_ge(shifted, free1(c))
                    alone(pe, mark_p)
                    for k in range(K):
                        nc.tensor.transpose(top_v[:, k, :], top[:, k * P:(k + 1) * P], g.ident[0:H, 0:H])
                    pe.wait_ge(shift_e, ready(c))
                    nc.tensor.matmul(ps_top[0:rows, K * H:K * H + 1], g.heads[:, 0:rows], shift[:, 1:2], start=True,
                                     stop=True).then_inc(back, 1)

                def product(h):
                    def step(c, q, i):
                        pe.wait_ge(filled, ready(c))
                        pe.wait_ge(tops, c + 1)
                        pe.wait_ge(added, half_ready(c, h) - 2)
                        for k in range(4 * h, 4 * h + 4):
                            last = nc.tensor.matmul(ps_sum[0:rows, k, :], msg[:, q % 2, k, :], member[:, q, k, :],
                                                    start=True, stop=True)
                        last.then_inc(summed, 1)
                    return step
                rounds(pe, [(turn_logits, 2), (product(0), 1), (read_dst, 3), (turn_maxima, 2), (product(1), 1),
                            (turn_members, 4)])
        columns_to_nodes(nc, g, ph, sums, rows, [ps_dst[:, :], ps_top[:, :]])


def after_attention(nc, g, name, bias, last):
    with Phase(nc, name) as ph:
        loaded, step, stored, done, asked, given, exps = ph.sems("loaded step stored done asked given exps")
        tab, ad = ph.sb("tab", [P, NT, D + H]), ph.sb("ad", [P, NT, H])
        top, own = ph.sb("top", [P, NT, H]), ph.sb("own", [P, NT, H])
        bv, stat = ph.sb("bv", [P, D]), ph.sb("stat", [P, 2, NT])
        x = ph.sb("x", [P, NT, D]) if last else None
        num, den, seen = g.node[:, :, 0:D], g.node[:, :, D:D + H], g.node[:, :, D + H:D + 2 * H]

        def by_head(ap):
            return ap.rearrange("p t (h c) -> p t h c", h=H)

        def over_head(ap):
            return ap.unsqueeze(3).broadcast_to([P, NT, H, D // H])

        with nc.Block() as block:
            @block.sync
            def _(sp):
                sp.dma_start(tab[:, :, :], nodes_view(g.gat_src, slice(0, D + H))).then_inc(loaded, 16)
                sp.dma_start(ad[:, :, :], nodes_view(g.gat_dst, slice(0, H))).then_inc(loaded, 16)
                sp.dma_start(bv[:, :], bias.partition_broadcast(P)).then_inc(loaded, 16)
                if last:
                    sp.dma_start(x[:, :, :], nodes_view(g.xs)).then_inc(loaded, 16)
                    sp.wait_ge(done, 1)
                    sp.dma_start(nodes_view(g.xs), x[:, :, :]).then_inc(stored, 16)
                    sp.wait_ge(stored, 16)

            @block.scalar
            def _(act):
                act.wait_ge(exps, 1)
                nc.scalar.activation(top[:, :, :], top[:, :, :], ACT.Exp).then_inc(exps, 1)
                nc.scalar.activation(own[:, :, :], own[:, :, :], ACT.Exp).then_inc(exps, 1)

            if last:
                @block.gpsimd
                def _(pool):
                    power(nc, g, pool, asked, given, 1, stat[:, 1, :], -0.5)

            @block.vector
            def _(dve):
                v = nc.vector
                chain = Chain(dve, step)
                dve.wait_ge(loaded, 16 * (4 if last else 3))
                chain(v.tensor_tensor(ad[:], ad[:], tab[:, :, D:D + H], ALU.add))
                chain(v.tensor_scalar(top[:], ad[:], LRELU, None, ALU.mult))
                chain(v.tensor_tensor(own[:], top[:], ad[:], ALU.max))
                chain(v.tensor_tensor(ad[:], own[:], seen, ALU.max))
                chain(v.tensor_tensor(top[:], seen, ad[:], ALU.subtract))
                chain(v.tensor_tensor(own[:], own[:], ad[:], ALU.subtract))
                dve.sem_inc(exps, 1)
                dve.wait_ge(exps, 3)
                chain(v.tensor_tensor(den, den, top[:], ALU.mult))
                chain(v.tensor_tensor(den, den, own[:], ALU.add))
                chain(v.tensor_scalar(den, den, 1e-16, None, ALU.add))
                chain(v.reciprocal(den, den))
                chain(v.tensor_tensor(by_head(num), by_head(num), over_head(top[:, :, :]), ALU.mult))
                chain(v.tensor_tensor(by_head(tab[:, :, 0:D]), by_head(tab[:, :, 0:D]), over_head(own[:, :, :]), ALU.mult))
                chain(v.tensor_tensor(num, num, tab[:, :, 0:D], ALU.add))
                chain(v.tensor_tensor(by_head(num), by_head(num), over_head(den), ALU.mult))
                chain(v.tensor_tensor(num, num, repeat(bv[:, :], NT), ALU.add))
                if not last:
                    chain(v.tensor_scalar(num, num, 0.0, None, ALU.max))
                else:
                    chain(v.tensor_tensor(x[:], x[:], num, ALU.add))
                    dve.sem_inc(done, 1)
                    layernorm_relu(nc, dve, chain, x, num, tab[:, :, 0:D], stat, asked, given)


def typed_tables(nc, g, name, weights):
    with Phase(nc, name) as ph:
        w_in, staged, turned, turned_c, made, even, odd, mark_a = ph.sems(
            "w_in staged turned turned_c made even odd mark_a")
        put = [ph.sem(f"put{s}") for s in range(2)]
        w = ph.sb("w", [D, R, D])
        stage, ft = ph.sb("stage", [P, 2, D]), ph.sb("ft", [D, 2, P])
        res = ph.sb("res", [P, 2, R * D])
        psf = [ph.ps(f"psf{s}", [P, 512])[0:D, 0:P] for s in range(2)]
        banks = [ph.ps(f"bank{n}", [P, 512]) for n in range(6)]
        groups = [(q, 8 * q, min(8, R - 8 * q)) for q in range((R + 7) // 8)]
        rows = g.typed.rearrange("(n r) d -> n (r d)", r=R)
        n_even, n_odd = 5, 4

        def copied(q, t):
            return (even, (t + 1) * n_even + q // 2 + 1) if q % 2 == 0 else (odd, (t + 1) * n_odd + q // 2 + 1)

        def copy_out(eng, move, parity, mark, t, s, i):
            eng.wait_ge(put[s], 16 * i + 16)
            for q, r, m in groups:
                if q % 2 == parity:
                    eng.wait_ge(made, (t + 1) * len(groups) + q + 1)
                    move(res[:, s, r * D:(r + m) * D], banks[q % 6][:, 0:m * D]).then_inc((even, odd)[parity], 1)

        with nc.Block() as block:
            @block.sync
            def _(sp):
                prime(sp, ph, g, put)
                sp.dma_start(w[:, :, :], weights.rearrange("r d k -> d r k")).then_inc(w_in, 16)

                def store(t, s, i):
                    for q in (8, 7):
                        sem, value = copied(q, t)
                        sp.wait_ge(sem, value)
                    sp.dma_start(rows[ds(t * P, P), :], res[:, s, :]).then_inc(put[s], 16)
                pairs(sp, store, NT)
                for s in range(2):
                    sp.wait_ge(put[s], 16 * (NT // 2) + 16)

            @block.scalar
            def _(act):
                act.sem_inc(staged, START)
                act.sem_inc(even, n_even)

                def head(t, s, i):
                    act.wait_ge(turned, free2(t))
                    alone(act, mark_a)
                    nc.scalar.activation(stage[:, s, :], g.node[:, ds(t, 1), 0:D].rearrange("p o d -> p (o d)"),
                                         ACT.Copy).then_inc(staged, 1)

                def tail(t, s, i):
                    copy_out(act, lambda o, a: nc.scalar.activation(o, a, ACT.Copy), 0, None, t, s, i)
                skewed(act, head, tail, NT)

            @block.vector
            def _(dve):
                dve.sem_inc(turned_c, START)
                dve.sem_inc(odd, n_odd)

                def head(t, s, i):
                    dve.wait_ge(turned, ready(t))
                    if not isinstance(t, int) or t >= 2:
                        dve.wait_ge(made, t * len(groups))
                    nc.vector.tensor_copy(ft[:, s, :], psf[s]).then_inc(turned_c, 1)

                def tail(t, s, i):
                    copy_out(dve, nc.vector.tensor_copy, 1, None, t, s, i)
                skewed(dve, head, tail, NT)

            @block.tensor
            def _(pe):
                pe.sem_inc(turned, START)
                pe.sem_inc(made, len(groups))
                pe.wait_ge(w_in, 16)

                def head(t, s, i):
                    pe.wait_ge(staged, ready(t))
                    pe.wait_ge(turned_c, free2(t))
                    nc.tensor.matmul(psf[s], stage[:, s, :], g.ident[:, :], start=True, stop=True).then_inc(turned, 1)

                def tail(t, s, i):
                    pe.wait_ge(turned_c, ready(t))
                    for q, r, m in groups:
                        sem, value = copied(q - 6, t) if q >= 6 else copied(q + 6 if q < 3 else q, t - 1)
                        pe.wait_ge(sem, value)
                        nc.tensor.matmul(banks[q % 6][:, 0:m * D], ft[:, s, :],
                                         w[:, r:r + m, :].rearrange("d r k -> d (r k)"), start=True, stop=True
                                         ).then_inc(made, 1)
                skewed(pe, head, tail, NT)


def edges_relational(nc, g, name, first):
    with Phase(nc, name) as ph:
        (staged, gather_at, members, turned, turned_c, inverse, chosen, filled, summed, added) = ph.sems(
            "staged gather_at members turned turned_c inverse chosen filled summed added")
        step_a, step_b, opened, cleared, mark_a = ph.sems("step_a step_b opened cleared mark_a")
        win, got = ([ph.sem(f"{n}{q}") for q in range(4)] for n in ("win", "got"))
        edge = ph.sb("edge", [P, 4, FIELDS, K])
        src_at = ph.sb("src_at", [P, 4, K], I32)
        spot = g.node[:, :, :].rearrange("p t d -> p (t d)")
        member = spot[:, 0:4 * CE].rearrange("p (s k e) -> p s k e", s=4, k=K)
        memberT = spot[:, 4 * CE:5 * CE].rearrange("p (k e) -> p k e", k=K)
        table = ph.sb("table", [P, 2, K, R])
        kinds = ph.sb("kinds", [P, K, R])
        inv = ph.sb("inv", [P, 2, K])
        from_src = ph.sb("from_src", [P, 4, K, D])
        msg = ph.sb("msg", [P, 2, K, D])
        sums = ph.sb("sums", [D, NR])
        ps_turn, ps_sum = (ph.ps(n, [P, K, P]) for n in ("ps_turn", "ps_sum"))
        ps_inv = ph.ps("ps_inv", [P, 2, 512])
        inv_v = ps_inv[:, :, 0:4 * R].rearrange("p b (k r) -> p b k r", r=R)
        with nc.Block() as block:
            if first:
                @block.sync
                def _(sp):
                    def load(c, q, i):
                        sp.wait_ge(inverse, free2(c))
                        for k, b in enumerate(bases(nc, ENG.SP, g.base, c)):
                            sp.dma_start(table[:, q % 2, k, :], g.inv_count[ds(b, P), :]).then_inc(win[q], 16)
                    rounds(sp, [(load, 0)])

            @block.gpsimd
            def _(pool):
                def gather(c, q, i):
                    pool.wait_ge(filled, free4(c))
                    pool.wait_ge(gather_at, ready(c))
                    pool.sem_inc(opened, 1)
                    for k in range(K):
                        nc.gpsimd.indirect_dma_start(
                            from_src[:, q, k, :], None, g.typed[:, :],
                            bass.IndirectOffsetOnAxis(ap=src_at[:, q, k:k + 1], axis=0)).then_inc(got[q], 16)
                rounds(pool, [(gather, 0)])

            @block.scalar
            def _(act):
                for q in (staged, gather_at, turned_c):
                    act.sem_inc(q, START)

                def fields(c, q, i):
                    act.wait_ge(filled, free4(c))
                    alone(act, mark_a)
                    nc.scalar.activation(src_at[:, q, :], g.edges[:, SIDX, ds(c * K, K)], ACT.Copy
                                         ).then_inc(gather_at, 1)
                    nc.scalar.activation(edge[:, q, :, :], g.edges[:, :, ds(c * K, K)], ACT.Copy).then_inc(staged, 1)

                def turn_out(c, q, i):
                    act.wait_ge(turned, ready(c))
                    act.wait_ge(inverse, free1(c))
                    for h in range(2):
                        last = nc.scalar.activation(memberT[:, 4 * h:4 * h + 4, :], ps_turn[:, 4 * h:4 * h + 4, :],
                                                    ACT.Copy)
                    last.then_inc(turned_c, 1)
                rounds(act, [(fields, 4)] + ([(turn_out, 3)] if first else []))

            @block.vector
            def _(dve):
                v = nc.vector
                for q in (members, chosen, filled, added):
                    dve.sem_inc(q, START)
                v.memset(sums[:, :], 0.0).then_inc(cleared, 1)
                dve.wait_ge(cleared, 1)

                def zero_ones(c, q, i):
                    dve.wait_ge(staged, ready(c))
                    dve.wait_ge(summed, free4(c))
                    v.tensor_tensor(member[:, q], repeat(g.iota[:, :], K), spread(edge[:, q, REL, :], P), ALU.is_equal
                                    ).then_inc(members, 1)

                def choose(c, q, i):
                    chain = Chain(dve, step_a, c * 4)
                    chain(v.tensor_tensor(kinds[:, :, :], repeat(g.iota[:, 0:R], K), spread(edge[:, q, TYPE, :], R),
                                          ALU.is_equal))
                    dve.wait_ge(inverse, ready(c))
                    kv = kinds[:, :, :].rearrange("p (b k) r -> p b k r", b=2)
                    chain(v.tensor_tensor(kv, kv, inv_v, ALU.mult))
                    dve.sem_inc(chosen, 1)
                    chain(v.tensor_reduce(inv[:, q % 2, :], kinds[:, :, :], AX.X, ALU.add))
                    chain(v.tensor_copy(g.edges[:, INV, ds(c * K, K)], inv[:, q % 2, :]))

                def messages(c, q, i):
                    dve.wait_ge(got[q], 16 * K * (i + 1))
                    dve.wait_ge(summed, free2(c))
                    v.tensor_tensor(msg[:, q % 2], from_src[:, q],
                                    spread(inv[:, q % 2, :] if first else edge[:, q, INV, :], D),
                                    ALU.mult).then_inc(filled, 1)

                def add(c, q, i):
                    chain = Chain(dve, step_b, c * K)
                    regs = bases(nc, ENG.DVE, g.base, c)
                    dve.wait_ge(summed, ready(c))
                    for k, b in enumerate(regs):
                        chain(v.tensor_tensor(sums[:, ds(b, P)], sums[:, ds(b, P)], ps_sum[0:D, k, :], ALU.add))
                    dve.sem_inc(added, 1)
                rounds(dve, [(messages, 1)] + ([(choose, 2)] if first else []) + [(zero_ones, 3), (add, 0)])

            @block.tensor
            def _(pe):
                for q in (turned, inverse, summed):
                    pe.sem_inc(q, START)

                def turn_members(c, q, i):
                    pe.wait_ge(members, ready(c))
                    pe.wait_ge(turned_c, free1(c))
                    for k in range(K):
                        last = nc.tensor.transpose(ps_turn[:, k, :], member[:, q, k, :], g.ident[:, :])
                    last.then_inc(turned, 1)

                def from_dst(c, q, i):
                    pe.wait_ge(turned_c, ready(c))
                    pe.wait_ge(win[q], 16 * K * (i + 1))
                    pe.wait_ge(chosen, free1(c))
                    for k in range(K):
                        last = nc.tensor.matmul(inv_v[:, k // 4, k % 4, :], memberT[:, k, :], table[:, q % 2, k, :],
                                                start=True, stop=True)
                    last.then_inc(inverse, 1)

                def product(c, q, i):
                    pe.wait_ge(members, ready(c))
                    pe.wait_ge(filled, ready(c))
                    pe.wait_ge(added, free1(c))
                    for k in range(K):
                        last = nc.tensor.matmul(ps_sum[0:D, k, :], msg[:, q % 2, k, :], member[:, q, k, :], start=True,
                                                stop=True)
                    last.then_inc(summed, 1)
                if first:
                    rounds(pe, [(from_dst, 2), (product, 1), (turn_members, 3)])
                else:
                    rounds(pe, [(product, 1)])
        turn = [ps_inv[:, n, :] for n in range(2)]
        columns_to_nodes(nc, g, ph, sums, D, turn)


def typed_index(nc, g):
    with nc.Block() as block:
        @block.vector
        def _(dve):
            nc.vector.scalar_tensor_tensor(g.edges[:, SIDX, :], g.edges[:, SRC, :], float(R), g.edges[:, TYPE, :],
                                           ALU.mult, ALU.add)


def after_relational(nc, g, name, bias, res_bias, last):
    with Phase(nc, name) as ph:
        loaded, step, stored, done = ph.sems("loaded step stored done")
        own = ph.sb("own", [P, NT, 2 * D])
        bv = ph.sb("bv", [P, 2, D])
        x = ph.sb("x", [P, NT, D]) if last else None
        h = g.node[:, :, 0:D]
        full, rest = N // P, N % P
        with nc.Block() as block:
            @block.sync
            def _(sp):
                sp.dma_start(own[:, :, :], nodes_view(g.hyp_src, slice(0, 2 * D))).then_inc(loaded, 16)
                sp.dma_start(bv[:, 0, :], bias.partition_broadcast(P)).then_inc(loaded, 16)
                sp.dma_start(bv[:, 1, :], res_bias.partition_broadcast(P)).then_inc(loaded, 16)
                if last:
                    sp.dma_start(x[:, :, :], nodes_view(g.xs)).then_inc(loaded, 16)
                    sp.wait_ge(done, 1)
                    sp.dma_start(g.out[0:full * P, :].rearrange("(t p) d -> p t d", p=P), x[:, 0:full, :]
                                 ).then_inc(stored, 16)
                    sp.dma_start(g.out[full * P:N, :], x[0:rest, full, :]).then_inc(stored, 16)
                    sp.wait_ge(stored, 32)

            @block.vector
            def _(dve):
                v = nc.vector
                chain = Chain(dve, step)
                dve.wait_ge(loaded, 16 * (4 if last else 3))
                chain(v.tensor_tensor(h, h, own[:, :, 0:D], ALU.add))
                chain(v.tensor_tensor(h, h, repeat(bv[:, 0, :], NT), ALU.add))
                chain(v.tensor_scalar(h, h, 0.0, None, ALU.max))
                chain(v.tensor_tensor(own[:, :, D:2 * D], own[:, :, D:2 * D], repeat(bv[:, 1, :], NT), ALU.add))
                chain(v.tensor_scalar(own[:, :, D:2 * D], own[:, :, D:2 * D], 0.0, None, ALU.max))
                chain(v.tensor_tensor(h, h, own[:, :, D:2 * D], ALU.add))
                if last:
                    chain(v.tensor_tensor(x[:, :, :], x[:, :, :], h, ALU.add))
                    dve.sem_inc(done, 1)


class Shared:
    pass


def gnn_kernel(nc, w, out, upto=99):
    g = Shared()
    g.w, g.x, g.src, g.dst, g.etype = w, w["x"], w["src"], w["dst"], w["edge_type_65"]
    g.ew, g.ew1, g.out = w["edge_weight"], w["edge_weight1"], out

    def dram(name, shape, dt=F32):
        return nc.dram_tensor(name + "_dram", shape, dt, kind="Internal").ap()

    g.src_p, g.dst_p, g.type_p = (dram(f"{n}_padded", (EP + 32,), I32) for n in ("src", "dst", "type"))
    g.ew_p, g.ew1_p = (dram(f"{n}_padded", (EP + 32,)) for n in ("weight", "weight1"))
    g.first_mask, g.last_mask = dram("first_mask", (EP,)), dram("last_mask", (EP,))
    g.xs = dram("x_now", (NR, D))
    g.sum0 = [dram(f"gcn_sum{k}", (NR + SPARE, D)) for k in range(COPIES)]
    g.sum1 = [dram(f"hyp_sum{k}", (NR + SPARE, D)) for k in range(COPIES)]
    g.gcn_table = dram("gcn_table", (NR, D))
    g.hyp_src = dram("hyp_src", (NR, 2 * D))
    g.hyp_dst = dram("hyp_dst", (NR, 3 * D))
    g.gat_src = dram("gat_src", (NR, D + H))
    g.gat_dst = dram("gat_dst", (NR, H))
    g.inv_count = dram("inv_count", (NR, R))
    g.typed = dram("typed", (NR * R, D))
    with Phase(nc, "all") as ph:
        g.edges = ph.sb("edges", [P, FIELDS, ET])
        g.node = ph.sb("node", [P, NT, D + 2 * H])
        g.base = ph.sb("base", [1, ET], I32)
        g.iota, g.ident, g.lower = (ph.sb(n, [P, P]) for n in ("iota", "ident", "lower"))
        g.ident16 = ph.sb("ident16", [P, P], BF16)
        g.halves = ph.sb("halves", [P, 2])
        g.lane = ph.sb("lane", [P, 1])
        g.ones = ph.sb("ones", [1, P])
        g.heads = ph.sb("heads", [H, D + 2 * H])
        stages = [
            lambda: prepare(nc, g),
            lambda: begin(nc, g),
            lambda: project(nc, g, "gcn_in", [w["L0_gnn_kernel"]], D, [(g.gcn_table, slice(0, D), slice(0, D))]),
            lambda: edges_gcn(nc, g),
            lambda: after_gcn(nc, g),
            lambda: hyperbolic_in(nc, g),
            lambda: project(nc, g, "hyp_in", [w["L1_gnn_w1"][0:D, :], w["L1_gnn_w1"][D:2 * D, :], None], 3 * D,
                            [(g.hyp_src, slice(0, D), slice(0, D)), (g.hyp_dst, slice(D, 3 * D), slice(D, 3 * D))],
                            first=(w["L1_gnn_W"], w["L1_gnn_b"])),
            lambda: edges_hyperbolic(nc, g),
            lambda: after_hyperbolic(nc, g),
        ]
        for n in (1, 2, 3):
            stages += [
                lambda n=n: project(nc, g, f"gat_in{n}", [w[f"L2_gnn_W{n}"]], D,
                                    [(g.gat_src, slice(0, D + H), slice(0, D + H)),
                                     (g.gat_dst, slice(0, H), slice(D + H, D + 2 * H))],
                                    dots=(w[f"L2_gnn_a_src{n}"], w[f"L2_gnn_a_dst{n}"])),
                lambda n=n: edges_attention(nc, g, f"gat{n}"),
                lambda n=n: after_attention(nc, g, f"gat_end{n}", w[f"L2_gnn_b{n}"], n == 3),
            ]
        stages.append(lambda: typed_index(nc, g))
        for n in range(2):
            stages += [
                lambda n=n: project(nc, g, f"rel_in{n}", [w["L3_gnn_root"][n], w["L3_gnn_res_W"][n]], 2 * D,
                                    [(g.hyp_src, slice(0, 2 * D), slice(0, 2 * D))]),
                lambda n=n: typed_tables(nc, g, f"typed{n}", w["L3_gnn_W"][n]),
                lambda n=n: edges_relational(nc, g, f"rel{n}", n == 0),
                lambda n=n: after_relational(nc, g, f"rel_end{n}", w["L3_gnn_bias"][n], w["L3_gnn_res_b"][n], n == 1),
            ]
        for n, f in enumerate(stages):
            if n < upto:
                f()


_OUT = ((12500, 64), "float32")


def kernel(**inputs):
    import numpy as _np
    import concourse.bacc as _bacc
    from concourse import mybir as _mybir
    from concourse.bass_utils import run_bass_kernel_spmd as _run

    nc = _bacc.Bacc("TRN2", target_bir_lowering=False, num_devices=1)
    arrays, args = {}, {}
    for name, a in inputs.items():
        if name == "node_vec1":
            continue
        arrays[f"in_{name}"] = _np.ascontiguousarray(a)
        args[name] = nc.dram_tensor(f"in_{name}", a.shape, _mybir.dt.from_np(_np.asarray(a).dtype),
                                    kind="ExternalInput").ap()
    out = nc.dram_tensor("out", _OUT[0], _mybir.dt.from_np(_np.dtype(_OUT[1])), kind="ExternalOutput").ap()
    gnn_kernel(nc, args, out)
    return _run(nc, [arrays], core_ids=[0]).results[0]["out"]
```

```python
from contextlib import ExitStack

import concourse.bass as bass
from concourse import mybir

F32, I32, BF16 = mybir.dt.float32, mybir.dt.int32, mybir.dt.bfloat16
ALU, ACT, AX = mybir.AluOpType, mybir.ActivationFunctionType, mybir.AxisListType
ENG = mybir.EngineType
ds = bass.ds

P = 128
N, E, D = 12500, 212500, 64
H = 8
R = 65
K = 8
CE = K * P
ET = 1664
EB = ET // P
EP = ET * P
CHUNKS = ET // K
NT = 100
NR = NT * P
G = 4
SPARE = P
COPIES = K
ZERO = (NR + SPARE) // P * D // 2
BIG = 1.0e30
LRELU = 0.2
ACOSH_MIN = 1.0 + 1e-7
SRC, REL, EW, EW1, TYPE, END, SIDX, INV = range(8)
FIELDS = 8


class Chain:

    def __init__(self, eng, sem, base=0):
        self.eng, self.sem, self.base, self.n = eng, sem, base, 0

    def __call__(self, ins):
        self.n += 1
        ins.then_inc(self.sem, 1)
        self.eng.wait_ge(self.sem, self.base + self.n)


START = 4


def ready(c):
    return c + START + 1


def free1(c):
    return c + START


def free2(c):
    return c + START - 1


def free4(c):
    return c + START - 3


def half_ready(c, h):
    return 2 * (c + START) + h + 1


def alone(eng, mark):
    eng.sem_inc(mark, 1)


def pairs(eng, body, count=CHUNKS):
    with eng.Fori(0, count // 2) as i:
        for s in range(2):
            body(i * 2 + s, s, i)
    if count % 2:
        body(count - 1, 0, count // 2)


def skewed(eng, first, second, count=CHUNKS):
    first(0, 0, 0)
    last = (count - 1) // 2
    with eng.Fori(0, last) as i:
        first(i * 2 + 1, 1, i)
        second(i * 2, 0, i)
        first(i * 2 + 2, 0, i + 1)
        second(i * 2 + 1, 1, i)
    if count % 2 == 0:
        first(count - 1, 1, last)
        second(count - 2, 0, last)
        second(count - 1, 1, last)
    else:
        second(count - 1, 0, last)


def rounds(eng, steps, count=CHUNKS):
    def turn(t, i, q):
        for step, lead in steps:
            if not isinstance(t, int) or 0 <= t + lead < count:
                step(t + lead, (q + lead) % 4, i + (q + lead) // 4)
    for t in range(-max(lead for _, lead in steps), 0):
        turn(t, t // 4, t % 4)
    with eng.Fori(0, count // 4 - 1) as i:
        for q in range(4):
            turn(i * 4 + q, i, q)
    for t in range(count - 4, count):
        turn(t, t // 4, t % 4)


def bases(nc, engine, base, c, first=0, count=K):
    _, regs = nc.values_load_multi_w_load_instructions(
        base[0:1, ds(c * K + first, count)], engines=(engine,), min_val=0, max_val=N,
        skip_runtime_bounds_check_because="dst is a node or the padding node")
    return regs


def spread(ap, n):
    return ap.unsqueeze(2).broadcast_to([ap.shape[0], ap.shape[1], n])


def repeat(ap, n):
    return ap.unsqueeze(1).broadcast_to([ap.shape[0], n, ap.shape[1]])


class Phase:

    def __init__(self, nc, name):
        self.nc, self.name, self.stack, self.used = nc, name, ExitStack(), []

    def __enter__(self):
        self.stack.__enter__()
        return self

    def __exit__(self, *a):
        if self.used:
            self.nc.clear_and_free_semaphores(self.used)
            self.nc.all_engine_barrier()
        return self.stack.__exit__(*a)

    def sem(self, name):
        self.used.append(self.nc.alloc_semaphore(f"{self.name}_{name}"))
        return self.used[-1]

    def sems(self, names):
        return [self.sem(n) for n in names.split()]

    def sb(self, name, shape, dt=F32):
        return self.stack.enter_context(self.nc.sbuf_tensor(f"{self.name}_{name}", shape, dt))

    def ps(self, name, shape, dt=F32):
        return self.stack.enter_context(self.nc.psum_tensor(f"{self.name}_{name}", shape, dt))


def clear(eng, targets, zero, sem):
    for t in targets:
        for n in range(2):
            eng.dma_start(t.rearrange("(p w) d -> p (w d)", p=P)[:, n * ZERO:(n + 1) * ZERO], zero[:, :]).then_inc(sem, 16)


def prepare(nc, g):
    with Phase(nc, "prep") as ph:
        loaded, padded, const, turned, copied, step, stored, rows_in, zeroed = ph.sems(
            "loaded padded const turned copied step stored rows_in zeroed")
        padi = ph.sb("padi", [P, 16], I32)
        padf = ph.sb("padf", [P, 16])
        raw = [ph.sb(f"raw{n}", [P, EB, P], I32 if n < 5 else F32) for n in range(7)]
        rows = [ph.sb(f"rows{n}", [P, EB, P]) for n in range(5)]
        mask = ph.sb("mask", [P, 2, EB, P])
        dstf = ph.sb("dstf", [P, ET])
        zero = ph.sb("zero", [P, ZERO])
        turn = [ph.ps(f"turn{n}", [P, 512]) for n in range(4)]
        src_r, dst_r, prev_r, next_r, type_r = range(5)
        flat = EP - E
        fields = (SRC, None, TYPE, EW, EW1, END)
        with nc.Block() as block:
            @block.gpsimd
            def _(pool):
                nc.gpsimd.iota(g.iota[:, :], [[1, P]], base=0, channel_multiplier=0,
                               allow_small_or_imprecise_dtypes=True).then_inc(const, 1)
                nc.gpsimd.iota(g.lane[:, 0:1], [[0, 1]], base=NR, channel_multiplier=1,
                               allow_small_or_imprecise_dtypes=True).then_inc(const, 1)
                nc.gpsimd.memset(g.ident[:, :], 0.0).then_inc(const, 1)
                nc.gpsimd.memset(g.lower[:, :], 1.0).then_inc(const, 1)
                nc.gpsimd.memset(g.heads[:, :], 1.0).then_inc(const, 1)
                pool.wait_ge(const, 5)
                nc.gpsimd.affine_select(out=g.ident[:, :], in_=g.ident[:, :], compare_op=ALU.not_equal,
                                        fill=1.0, base=0, pattern=[[-1, P]], channel_multiplier=1).then_inc(const, 1)
                nc.gpsimd.affine_select(out=g.lower[:, :], in_=g.lower[:, :], compare_op=ALU.is_gt,
                                        fill=0.0, base=0, pattern=[[-1, P]], channel_multiplier=1).then_inc(const, 1)
                hv = g.heads[:, 0:D].rearrange("p (h c) -> p h c", h=H)
                nc.gpsimd.affine_select(out=hv, in_=hv, compare_op=ALU.is_equal, fill=0.0, base=0,
                                        pattern=[[-1, H], [0, D // H]], channel_multiplier=1).then_inc(const, 1)
                iv = g.heads[:, D:D + 2 * H].rearrange("p (a h) -> p a h", a=2)
                nc.gpsimd.affine_select(out=iv, in_=iv, compare_op=ALU.is_equal, fill=0.0, base=0,
                                        pattern=[[0, 2], [-1, H]], channel_multiplier=1).then_inc(const, 1)
                pool.wait_ge(const, 9)
                nc.gpsimd.tensor_copy(g.ident16[:, :], g.ident[:, :])

            @block.sync
            def _(sp):
                for d, a in ((g.src_p, g.src), (g.dst_p, g.dst), (g.type_p, g.etype),
                             (g.ew_p, g.ew), (g.ew1_p, g.ew1.rearrange("e o -> (e o)"))):
                    sp.dma_start(d[16:16 + E].rearrange("(a b) -> a b", a=20), a.rearrange("(a b) -> a b", a=20)
                                 ).then_inc(loaded, 16)
                sp.wait_ge(padded, 5)
                for d, p in ((g.src_p, 0), (g.dst_p, 0), (g.type_p, 1)):
                    sp.dma_start(d[16 + E:16 + EP].rearrange("(a b) -> a b", b=4), padi[0:flat // 4, 4 * p:4 * p + 4]
                                 ).then_inc(loaded, 16)
                for d in (g.ew_p, g.ew1_p):
                    sp.dma_start(d[16 + E:16 + EP].rearrange("(a b) -> a b", b=4), padf[0:flat // 4, 0:4]
                                 ).then_inc(loaded, 16)
                for at in (0, 16 + EP):
                    sp.dma_start(g.dst_p[at:at + 16].rearrange("(a b) -> a b", a=4), padi[0:4, 8:12]).then_inc(loaded, 16)
                sp.wait_ge(loaded, 12 * 16)
                for n, (d, off) in enumerate(((g.src_p, 16), (g.dst_p, 16), (g.dst_p, 15), (g.dst_p, 17),
                                              (g.type_p, 16), (g.ew_p, 16), (g.ew1_p, 16))):
                    sp.dma_start(raw[n][:, :, :], d[off:off + EP].rearrange("(g p e) -> p g e", p=P, e=P)
                                 ).then_inc(rows_in, 16)
                sp.wait_ge(stored, 1)
                for n, m in enumerate((g.first_mask, g.last_mask)):
                    sp.dma_start(m[0:EP].rearrange("(g p e) -> p g e", p=P, e=P), mask[:, n, :, :]).then_inc(loaded, 16)
                sp.wait_ge(loaded, 14 * 16)

            @block.scalar
            def _(act):
                act.wait_ge(padded, 6)
                clear(act, g.sum0, zero, zeroed)
                act.wait_ge(zeroed, 16 * 2 * COPIES)

            @block.vector
            def _(dve):
                nc.vector.memset(g.ones[:, :], 1.0).then_inc(padded, 1)
                nc.vector.memset(padi[:, 0:4], N).then_inc(padded, 1)
                nc.vector.memset(padi[:, 4:8], 0).then_inc(padded, 1)
                nc.vector.memset(padi[:, 8:12], -1).then_inc(padded, 1)
                nc.vector.memset(padf[:, :], 0.0).then_inc(padded, 1)
                nc.vector.memset(zero[:, :], 0.0).then_inc(padded, 1)
                nc.vector.memset(g.halves[:, 0:1], 0.5)
                nc.vector.memset(g.halves[:, 1:2], -0.5)
                nc.vector.memset(g.edges[:, SIDX:FIELDS, :], 0.0)
                chain = Chain(dve, step)
                dve.wait_ge(rows_in, 7 * 16)
                for n in range(5):
                    chain(nc.vector.tensor_copy(rows[n][:, :, :], raw[n][:, :, :]))
                chain(nc.vector.tensor_tensor(mask[:, 0], rows[dst_r][:], rows[prev_r][:], ALU.not_equal))
                chain(nc.vector.tensor_tensor(rows[next_r][:], rows[dst_r][:], rows[next_r][:], ALU.not_equal))
                chain(nc.vector.tensor_scalar(mask[:, 1], rows[next_r][:], -BIG, None, ALU.mult))
                nc.vector.tensor_scalar(mask[:, 0], mask[:, 0], -BIG, None, ALU.mult).then_inc(stored, 1)
                bank = 0
                for f, (field, dst) in enumerate(((SRC, None), (None, dstf), (TYPE, None), (EW, None), (EW1, None),
                                                  (END, None))):
                    for b in range(0, EB, 4):
                        w = min(4, EB - b) * P
                        o = dst[:, b * P:b * P + w] if dst is not None else g.edges[:, field, b * P:b * P + w]
                        dve.wait_ge(turned, bank + 1)
                        nc.vector.tensor_copy(o, turn[bank % 2][:, 0:w]).then_inc(copied, 1)
                        bank += 1
                dve.wait_ge(copied, bank)
                nc.vector.tensor_copy(g.base[0:1, :], dstf[0:1, :]).then_inc(copied, 1)
                for n, o in enumerate(range(0, ET, 512)):
                    w = min(512, ET - o)
                    dve.wait_ge(turned, bank + 1 + n)
                    nc.vector.tensor_tensor(g.edges[:, REL, o:o + w], dstf[:, o:o + w], turn[2 + n % 2][:, 0:w],
                                            ALU.subtract).then_inc(copied, 1)
                dve.wait_ge(copied, bank + 5)

            @block.tensor
            def _(pe):
                pe.wait_ge(const, 9)
                pe.wait_ge(step, 7)
                bank = 0
                for src in (rows[src_r], rows[dst_r], rows[type_r], raw[5], raw[6], rows[next_r]):
                    for b in range(0, EB, 4):
                        if bank >= 2:
                            pe.wait_ge(copied, bank - 1)
                        for k in range(b, min(b + 4, EB)):
                            last = nc.tensor.transpose(turn[bank % 2][:, (k - b) * P:(k - b + 1) * P], src[:, k, :],
                                                       g.ident[:, :])
                        last.then_inc(turned, 1)
                        bank += 1
                pe.wait_ge(copied, bank)
                pe.wait_ge(padded, 1)
                for n, o in enumerate(range(0, ET, 512)):
                    w = min(512, ET - o)
                    if n >= 2:
                        pe.wait_ge(copied, bank + 1 + n - 1)
                    nc.tensor.matmul(turn[2 + n % 2][:, 0:w], g.ones[0:1, :], dstf[0:1, o:o + w], start=True,
                                     stop=True).then_inc(turned, 1)


def power(nc, g, pool, asked, given, n, data, exponent):
    pool.wait_ge(asked, n)
    half = g.halves[:, 0:1] if exponent > 0 else g.halves[:, 1:2]
    nc.gpsimd.tensor_tensor(data, data, half.broadcast_to([P, data.shape[1]]), ALU.pow).then_inc(given, 1)


def ask_power(dve, asked, given, n):
    dve.sem_inc(asked, 1)
    dve.wait_ge(given, n)


def layernorm_relu(nc, dve, chain, x, h, sq, stat, asked, given, n=1):
    v = nc.vector
    chain(v.tensor_reduce(stat[:, 0, :], x[:, :, :], AX.X, ALU.add))
    chain(v.tensor_scalar(stat[:, 0, :], stat[:, 0, :], 1.0 / D, None, ALU.mult))
    chain(v.tensor_tensor(h, x[:, :, :], spread(stat[:, 0, :], D), ALU.subtract))
    chain(v.tensor_tensor(sq[:, :, :], h, h, ALU.mult))
    chain(v.tensor_reduce(stat[:, 1, :], sq[:, :, :], AX.X, ALU.add))
    chain(v.tensor_scalar(stat[:, 1, :], stat[:, 1, :], 1.0 / D, 1e-5, ALU.mult, ALU.add))
    ask_power(dve, asked, given, n)
    chain(v.tensor_tensor(h, h, spread(stat[:, 1, :], D), ALU.mult))
    chain(v.tensor_scalar(h, h, 0.0, None, ALU.max))


def nodes_view(t, cols=slice(0, D)):
    return t[0:NR, cols].rearrange("(t p) d -> p t d", p=P)


def begin(nc, g):
    with Phase(nc, "begin") as ph:
        loaded, step, cleared, stored, asked, given = ph.sems("loaded step cleared stored asked given")
        x, sq, stat = ph.sb("x", [P, NT, D]), ph.sb("sq", [P, NT, D]), ph.sb("stat", [P, 2, NT])
        full, rest = N // P, N % P
        with nc.Block() as block:
            @block.sync
            def _(sp):
                sp.wait_ge(cleared, 1)
                sp.dma_start(x[:, 0:full, :], g.x[0:full * P, :].rearrange("(t p) d -> p t d", p=P)).then_inc(loaded, 16)
                sp.dma_start(x[0:rest, full, :], g.x[full * P:N, :]).then_inc(loaded, 16)
                sp.wait_ge(loaded, 32)
                sp.dma_start(nodes_view(g.xs), x[:, :, :]).then_inc(stored, 16)
                sp.wait_ge(stored, 16)

            @block.vector
            def _(dve):
                nc.vector.memset(x[:, full:NT, :], 0.0).then_inc(cleared, 1)
                dve.wait_ge(loaded, 32)
                chain = Chain(dve, step)
                layernorm_relu(nc, dve, chain, x, g.node[:, :, 0:D], sq, stat, asked, given)

            @block.gpsimd
            def _(pool):
                power(nc, g, pool, asked, given, 1, stat[:, 1, :], -0.5)


def project(nc, g, name, weights, stores, first=None, dots=None, split=None):
    cols = len(weights) * D
    extra = 2 * H if dots else 0
    groups = NT // G
    with Phase(nc, name) as ph:
        (w_in, staged, turned, turned_c, hidden, hidden_c, made, made_c, dotted) = ph.sems(
            "w_in staged turned turned_c hidden hidden_c made made_c dotted")
        step, mark, mark_a = ph.sems("step mark mark_a")
        put = [ph.sem(f"put{s}") for s in range(2)]
        puts = len(stores) + (split is not None)
        parts, rest = ph.sb("parts", [P, 2, G, 3, H], BF16), ph.sb("rest", [P, G, H])
        w = ph.sb("w", [D, cols])
        w1, b1 = ph.sb("w1", [D, D]), ph.sb("b1", [D, 1])
        av = ph.sb("av", [P, 2, D])
        tmp = ph.sb("tmp", [P, G, 2, D])
        stage = ph.sb("stage", [P, 2, G, D])
        ft, hid = ph.sb("ft", [D, 2, G * P]), ph.sb("hid", [D, 2, G * P])
        res = ph.sb("res", [P, 2, G, cols + extra])
        psf, psh = ([ph.ps(f"{n}{s}", [D, G * P]) for s in range(2)] for n in ("psf", "psh"))
        psr = [ph.ps(f"psr{s}", [P, 2, 512])[:, :, 0:2 * cols].rearrange("p b (j c) -> p b j c", j=2) for s in range(2)]
        last_done = dotted if dots else made_c
        loads = sum(m is not None for m in weights) + (2 if first else 0) + (2 if dots else 0)
        with nc.Block() as block:
            @block.sync
            def _(sp):
                prime(sp, ph, g, put)
                for n, m in enumerate(weights):
                    if m is not None:
                        sp.dma_start(w[:, n * D:(n + 1) * D], m).then_inc(w_in, 16)
                if first:
                    sp.dma_start(w1[:, :], first[0]).then_inc(w_in, 16)
                    sp.dma_start(b1[:, :], first[1].unsqueeze(1)).then_inc(w_in, 16)
                if dots:
                    for n, a in enumerate(dots):
                        sp.dma_start(av[:, n, :], a.rearrange("h c -> (h c)").partition_broadcast(P)).then_inc(w_in, 16)

                def store(t, s, i):
                    sp.wait_ge(last_done, ready(t))
                    for table, tc, rc in stores:
                        sp.dma_start(table[ds(t * (G * P), G * P), tc].rearrange("(j p) d -> p j d", p=P),
                                     res[:, s, :, rc]).then_inc(put[s], 16)
                    if split is not None:
                        sp.dma_start(split[ds(t * (G * P), G * P), :].rearrange("(j p) d -> p j d", p=P),
                                     parts[:, s, :, :, :].rearrange("p j a h -> p j (a h)")).then_inc(put[s], 16)
                pairs(sp, store, groups)
                for s in range(2):
                    sp.wait_ge(put[s], 16 * puts * ((groups + 1 - s) // 2) + 16)

            @block.scalar
            def _(act):
                for q in (staged, made_c, hidden_c):
                    act.sem_inc(q, START)

                def head(t, s, i):
                    act.wait_ge(turned, free2(t))
                    alone(act, mark_a)
                    nc.scalar.activation(stage[:, s, :, :], g.node[:, ds(t * G, G), 0:D], ACT.Copy).then_inc(staged, 1)

                def tail(t, s, i):
                    if first:
                        act.wait_ge(hidden, ready(t))
                        act.wait_ge(w_in, 16 * loads)
                        nc.scalar.activation(hid[:, s, :], psh[s][:, :], ACT.Identity, bias=b1[:, 0:1]
                                             ).then_inc(hidden_c, 1)
                    act.wait_ge(made, ready(t))
                    act.wait_ge(put[s], 16 * puts * i + 16)
                    nc.scalar.activation(res[:, s, :, 0:cols].rearrange("p (b j) c -> p b j c", j=2), psr[s], ACT.Copy
                                         ).then_inc(made_c, 1)
                skewed(act, head, tail, groups)

            @block.vector
            def _(dve):
                dve.sem_inc(turned_c, START)
                dve.sem_inc(dotted, START)
                if dots:
                    dve.wait_ge(w_in, 16 * loads)

                def head(t, s, i):
                    dve.wait_ge(turned, ready(t))
                    dve.wait_ge(hidden if first else made, free2(t))
                    nc.vector.tensor_copy(ft[:, s, :], psf[s][:, :]).then_inc(turned_c, 1)

                def tail(t, s, i):
                    if not dots:
                        return
                    dve.wait_ge(made_c, ready(t))
                    chain = Chain(dve, step, t * (7 if split is not None else 2))
                    chain(nc.vector.tensor_tensor(tmp[:, :, :, :],
                                                  res[:, s, :, 0:D].unsqueeze(2).broadcast_to([P, G, 2, D]),
                                                  av[:, :, :].unsqueeze(1).broadcast_to([P, G, 2, D]), ALU.mult))
                    chain(nc.vector.tensor_reduce(res[:, s, :, D:D + 2 * H],
                                                  tmp[:, :, :, :].rearrange("p j a (h c) -> p j (a h) c", h=H),
                                                  AX.X, ALU.add))
                    if split is not None:
                        value = res[:, s, :, D + H:D + 2 * H]
                        chain(nc.vector.tensor_copy(parts[:, s, :, 0, :], value))
                        chain(nc.vector.tensor_tensor(rest[:, :, :], value, parts[:, s, :, 0, :], ALU.subtract))
                        chain(nc.vector.tensor_copy(parts[:, s, :, 1, :], rest[:, :, :]))
                        chain(nc.vector.tensor_tensor(rest[:, :, :], rest[:, :, :], parts[:, s, :, 1, :], ALU.subtract))
                        chain(nc.vector.tensor_copy(parts[:, s, :, 2, :], rest[:, :, :]))
                    dve.sem_inc(dotted, 1)
                skewed(dve, head, tail, groups)

            @block.tensor
            def _(pe):
                for q in (turned, hidden, made):
                    pe.sem_inc(q, START)

                def head(t, s, i):
                    pe.wait_ge(staged, ready(t))
                    pe.wait_ge(turned_c, free2(t))
                    alone(pe, mark)
                    for j in range(G):
                        last = nc.tensor.transpose(psf[s][:, j * P:(j + 1) * P], stage[:, s, j, :], g.ident[:, :])
                    last.then_inc(turned, 1)

                def tail(t, s, i):
                    pe.wait_ge(w_in, 16 * loads)
                    pe.wait_ge(turned_c, ready(t))
                    lhs = ft
                    if first:
                        pe.wait_ge(hidden_c, free2(t))
                        alone(pe, mark)
                        nc.tensor.matmul(psh[s][:, :], w1[:, :], ft[:, s, :], start=True, stop=True).then_inc(hidden, 1)
                        pe.wait_ge(hidden_c, ready(t))
                        lhs = hid
                    pe.wait_ge(made_c, free2(t))
                    for j in range(G):
                        tile = lhs[:, s, j * P:(j + 1) * P]
                        if all(m is not None for m in weights):
                            last = nc.tensor.matmul(psr[s][:, j // 2, j % 2, :], tile, w[:, :], start=True, stop=True)
                        else:
                            for n, m in enumerate(weights):
                                wt = g.ident[0:D, 0:D] if m is None else w[:, n * D:(n + 1) * D]
                                last = nc.tensor.matmul(psr[s][:, j // 2, j % 2, n * D:(n + 1) * D], tile, wt,
                                                        start=True, stop=True)
                    last.then_inc(made, 1)
                skewed(pe, head, tail, groups)


def edges_gcn(nc, g):
    with Phase(nc, "gcn") as ph:
        staged, src_rows, equal, weighted, mixed, mixed_c, summed, summed_c, indexed, scattered = ph.sems(
            "staged src_rows equal weighted mixed mixed_c summed summed_c indexed scattered")
        step, opened, blank, zeroed = ph.sems("step opened blank zeroed")
        win = [ph.sem(f"win{s}") for s in range(2)]
        half = [ph.sem(f"half{n}") for n in range(2)]
        zero = ph.sb("zero", [P, ZERO])
        edge = ph.sb("edge", [P, 2, 3, K])
        table = ph.sb("table", [P, 2, K, D])
        member = ph.sb("member", [P, 2, K, P])
        same = ph.sb("same", [P, 2, K, P])
        before = ph.sb("before", [P, K, P])
        mix = ph.sb("mix", [P, 2, K, P])
        msg = ph.sb("msg", [P, 2, K, D])
        small = ph.sb("small", [P, 2, K])
        index = ph.sb("index", [P, 2, K], I32)
        ps_src, ps_mix = ph.ps("ps_src", [P, K, P]), ph.ps("ps_mix", [P, K, P])
        ps_sum = [ph.ps(f"ps_sum{s}", [P, K, D]) for s in range(2)]
        with nc.Block() as block:
            @block.sync
            def _(sp):
                def load(c, s, i):
                    sp.wait_ge(summed, free2(c))
                    for k, b in enumerate(bases(nc, ENG.SP, g.base, c)):
                        sp.dma_start(table[:, s, k, :], g.gcn_table[ds(b, P), :]).then_inc(win[s], 16)
                pairs(sp, load)

            @block.scalar
            def _(act):
                for q in (staged, mixed_c, summed_c):
                    act.sem_inc(q, START)
                act.wait_ge(blank, 1)
                clear(act, g.sum1, zero, zeroed)

                def first(c, s, i):
                    act.wait_ge(weighted, free2(c))
                    act.wait_ge(indexed, free2(c))
                    nc.scalar.activation(edge[:, s, :, :], g.edges[:, SRC:EW + 1, ds(c * K, K)], ACT.Copy
                                         ).then_inc(staged, 1)

                def second(c, s, i):
                    act.wait_ge(mixed, ready(c))
                    act.wait_ge(summed, free2(c))
                    for h in range(2):
                        last = nc.scalar.activation(mix[:, s, 4 * h:4 * h + 4, :], ps_mix[:, 4 * h:4 * h + 4, :], ACT.Copy)
                    last.then_inc(mixed_c, 1)
                    act.wait_ge(summed, ready(c))
                    act.wait_ge(scattered, free1(c))
                    nc.scalar.activation(msg[:, s, :, :], ps_sum[s][:, :, :], ACT.Copy).then_inc(summed_c, 1)
                skewed(act, first, second)
                act.wait_ge(zeroed, 16 * 2 * COPIES)

            @block.vector
            def _(dve):
                nc.vector.memset(zero[:, :], 0.0).then_inc(blank, 1)
                for q in (equal, weighted, indexed):
                    dve.sem_inc(q, START)

                def body(c, s, i):
                    v = nc.vector
                    chain = Chain(dve, step, c * 6)
                    dve.wait_ge(staged, ready(c))
                    dve.wait_ge(mixed, free2(c))
                    v.tensor_tensor(member[:, s], repeat(g.iota[:, :], K), spread(edge[:, s, REL, :], P), ALU.is_equal)
                    dve.wait_ge(src_rows, ready(c))
                    v.tensor_tensor(same[:, s], ps_src[:, :, :], spread(edge[:, s, SRC, :], P), ALU.is_equal
                                    ).then_inc(equal, 1)
                    dve.wait_ge(equal, ready(c))
                    chain(v.tensor_tensor(before[:, :, :], same[:, s], repeat(g.lower[:, :], K), ALU.mult))
                    v.tensor_tensor(same[:, s], same[:, s], spread(edge[:, s, EW, :], P), ALU.mult).then_inc(weighted, 1)
                    chain(v.tensor_reduce(small[:, 0, :], before[:, :, :], AX.X, ALU.add))
                    chain(v.tensor_scalar(small[:, 1, :], edge[:, s, SRC, :], -1.0, g.lane[:, 0:1], ALU.mult, ALU.add))
                    chain(v.scalar_tensor_tensor(small[:, 0, :], small[:, 0, :], 1.0, small[:, 1, :], ALU.min, ALU.mult))
                    dve.wait_ge(scattered, free1(c))
                    chain(v.tensor_tensor(index[:, s, :], small[:, 0, :], edge[:, s, SRC, :], ALU.add))
                    chain(v.tensor_copy(g.edges[:, SIDX, ds(c * K, K)], index[:, s, :]))
                    dve.sem_inc(indexed, 1)
                pairs(dve, body)

            @block.tensor
            def _(pe):
                for q in (src_rows, mixed, summed):
                    pe.sem_inc(q, START)

                def first(c, s, i):
                    pe.wait_ge(staged, ready(c))
                    pe.wait_ge(equal, free1(c))
                    for k in range(K):
                        last = nc.tensor.transpose(ps_src[:, k, :], edge[:, s, SRC, k:k + 1].broadcast_to([P, P]),
                                                   g.ident[:, :])
                    last.then_inc(src_rows, 1)

                def second(c, s, i):
                    pe.wait_ge(weighted, ready(c))
                    pe.wait_ge(mixed_c, free1(c))
                    for k in range(K):
                        last = nc.tensor.matmul(ps_mix[:, k, :], member[:, s, k, :], same[:, s, k, :], start=True, stop=True)
                    last.then_inc(mixed, 1)
                    pe.wait_ge(mixed_c, ready(c))
                    pe.wait_ge(win[s], 16 * K * (i + 1))
                    pe.wait_ge(summed_c, free2(c))
                    for k in range(K):
                        last = nc.tensor.matmul(ps_sum[s][:, k, :], mix[:, s, k, :], table[:, s, k, :],
                                                start=True, stop=True)
                    last.then_inc(summed, 1)
                skewed(pe, first, second)

            @block.gpsimd
            def _(pool):
                pool.sem_inc(scattered, START)
                prime(pool, ph, g, half)

                def body(c, s, i):
                    pool.wait_ge(summed_c, ready(c))
                    pool.wait_ge(indexed, ready(c))
                    scatter(nc, pool, g.sum0, msg[:, s], index[:, s], c, half, opened, scattered)
                pairs(pool, body)
                for h in range(2):
                    pool.wait_ge(half[h], 64 * CHUNKS + 16)


def prime(eng, ph, g, sems):
    spot = ph.sb("prime", [1, len(sems), 16])
    for n, sem in enumerate(sems):
        eng.dma_start(spot[0:1, n, :], g.w["L0_gnn_bias"][16 * n:16 * n + 16].unsqueeze(0)).then_inc(sem, 16)


def scatter(nc, pool, copies, msg, index, c, half, opened, scattered):
    for h, sem in enumerate((opened, scattered)):
        pool.wait_ge(half[h], c * 64 + 16)
        pool.sem_inc(sem, 1)
        for k in range(4 * h, 4 * h + 4):
            nc.gpsimd.indirect_dma_start(copies[k][:, :], bass.IndirectOffsetOnAxis(ap=index[:, k:k + 1], axis=0),
                                         msg[:, k, :], None, compute_op=ALU.add).then_inc(half[h], 16)


def after_gcn(nc, g):
    with Phase(nc, "gcn_end") as ph:
        loaded, used, step, stored, done, asked, given = ph.sems("loaded used step stored done asked given")
        part_in = [ph.sem(f"part{n}") for n in range(2)]
        x, total, stat = ph.sb("x", [P, NT, D]), ph.sb("total", [P, NT, D]), ph.sb("stat", [P, 2, NT])
        part = [ph.sb(f"part{n}", [P, NT, D]) for n in range(2)]
        bias = ph.sb("bias", [P, D])
        with nc.Block() as block:
            @block.sync
            def _(sp):
                sp.dma_start(x[:, :, :], nodes_view(g.xs)).then_inc(loaded, 16)
                sp.dma_start(bias[:, :], g.w["L0_gnn_bias"].partition_broadcast(P)).then_inc(loaded, 16)
                sum_loads(sp, g.sum0, part, part_in, used)
                sp.wait_ge(done, 1)
                sp.dma_start(nodes_view(g.xs), x[:, :, :]).then_inc(stored, 16)
                sp.wait_ge(stored, 16)

            @block.vector
            def _(dve):
                sum_adds(nc, dve, total, part, part_in, used)
                chain = Chain(dve, step)
                dve.wait_ge(loaded, 32)
                chain(nc.vector.tensor_tensor(total[:, :, :], total[:, :, :], repeat(bias[:, :], NT), ALU.add))
                chain(nc.vector.tensor_scalar(total[:, :, :], total[:, :, :], 0.0, None, ALU.max))
                chain(nc.vector.tensor_tensor(x[:, :, :], x[:, :, :], total[:, :, :], ALU.add))
                dve.sem_inc(done, 1)
                layernorm_relu(nc, dve, chain, x, g.node[:, :, 0:D], total, stat, asked, given)

            @block.gpsimd
            def _(pool):
                power(nc, g, pool, asked, given, 1, stat[:, 1, :], -0.5)


def sum_loads(sp, target, part, part_in, used):
    for n in range(COPIES):
        if n >= 2:
            sp.wait_ge(used, n - 1)
        sp.dma_start(part[n % 2][:, :, :], nodes_view(target[n])).then_inc(part_in[n % 2], 16)


def sum_adds(nc, dve, total, part, part_in, used):
    for n in range(COPIES):
        s = n % 2
        dve.wait_ge(part_in[s], 16 * (n // 2 + 1))
        if n == 0:
            nc.vector.tensor_copy(total[:, :, :], part[s][:, :, :]).then_inc(used, 1)
        else:
            nc.vector.tensor_tensor(total[:, :, :], total[:, :, :], part[s][:, :, :], ALU.add).then_inc(used, 1)
        dve.wait_ge(used, n + 1)


def acosh_argument(nc, v, chain, z, t, q):
    chain(v.tensor_scalar(z, z, ACOSH_MIN, None, ALU.max))
    chain(v.tensor_scalar(t, z, 1.0, None, ALU.subtract))
    chain(v.scalar_tensor_tensor(q, z, 1.0, t, ALU.add, ALU.mult))


def hyperbolic_in(nc, g):
    with Phase(nc, "log") as ph:
        step, ready_x, stored, asked, given, logs = ph.sems("step ready_x stored asked given logs")
        sq, stat = ph.sb("sq", [P, NT, D]), ph.sb("stat", [P, 5, NT])
        x = g.node
        d, t, q, yn = (stat[:, n, :] for n in range(4))
        with nc.Block() as block:
            @block.sync
            def _(sp):
                sp.dma_start(nodes_view(g.hyp_src, slice(D, 2 * D)), x[:, :, 0:D]).then_inc(stored, 16)
                sp.wait_ge(ready_x, 1)
                sp.dma_start(nodes_view(g.hyp_dst), sq[:, :, :]).then_inc(stored, 16)
                sp.wait_ge(stored, 32)

            @block.gpsimd
            def _(pool):
                power(nc, g, pool, asked, given, 1, q, 0.5)
                power(nc, g, pool, asked, given, 2, yn, 0.5)

            @block.scalar
            def _(act):
                act.wait_ge(ready_x, 2)
                nc.scalar.activation(d, t, ACT.Ln, bias=1.0).then_inc(logs, 1)

            @block.vector
            def _(dve):
                v = nc.vector
                chain = Chain(dve, step)
                chain(v.tensor_tensor(sq[:, :, :], x[:, :, 0:D], x[:, :, 0:D], ALU.mult))
                chain(v.tensor_reduce(yn, sq[:, :, 1:D], AX.X, ALU.add))
                chain(v.tensor_scalar(sq[:, :, :], x[:, :, 0:D], -1.0, None, ALU.mult))
                chain(v.tensor_copy(sq[:, :, 0:1], x[:, :, 0:1]))
                dve.sem_inc(ready_x, 1)
                chain(v.tensor_copy(d.unsqueeze(2), x[:, :, 0:1]))
                acosh_argument(nc, v, chain, d, t, q)
                ask_power(dve, asked, given, 1)
                chain(v.tensor_tensor(t, t, q, ALU.add))
                dve.sem_inc(ready_x, 1)
                ask_power(dve, asked, given, 2)
                chain(v.tensor_scalar(yn, yn, 1e-7, None, ALU.max))
                chain(v.reciprocal(yn, yn))
                dve.wait_ge(logs, 1)
                chain(v.tensor_tensor(d, d, yn, ALU.mult))
                dve.wait_ge(stored, 32)
                chain(v.tensor_tensor(x[:, :, 0:D], x[:, :, 0:D], spread(d, D), ALU.mult))
                chain(v.memset(x[:, :, 0:1], 0.0))


def edges_hyperbolic(nc, g):
    w = g.w
    with Phase(nc, "hyp") as ph:
        (staged, gather_at, members, turned, turned_c, from_dst, h_kept, taken, squared, logged, rooted, argued, geo,
         joined, src_rows, equal, counted, count_c) = ph.sems(
            "staged gather_at members turned turned_c from_dst h_kept taken squared logged rooted argued geo "
            "joined src_rows equal counted count_c")
        (pre, act1, pre2, act2, score, tanh, weighted, summed, summed_c, opened, scattered, w_in,
         step_a, step_b, step_c, step_d, added, cleared, inverted, kept, mark_a, mark_p) = ph.sems(
            "pre act1 pre2 act2 score tanh weighted summed summed_c opened scattered w_in "
            "step_a step_b step_c step_d added cleared inverted kept mark_a mark_p")
        win, got = ([ph.sem(f"{n}{q}") for q in range(4)] for n in ("win", "got"))
        half = [ph.sem(f"half{n}") for n in range(2)]
        edge = ph.sb("edge", [P, 4, SIDX + 1, K])
        src_at, sum_at = ph.sb("src_at", [P, 4, K], I32), ph.sb("sum_at", [P, 2, K], I32)
        table = ph.sb("table", [P, 2, K, 3 * D])
        from_src = ph.sb("from_src", [P, 4, K, 2 * D])
        spot = g.node[:, :, :].rearrange("p t d -> p (t d)")
        memberT = spot[:, 0:2 * CE].rearrange("p (s k e) -> p s k e", s=2, k=K)
        same = spot[:, 2 * CE:6 * CE].rearrange("p (s k e) -> p s k e", s=4, k=K)
        row = ph.sb("row", [P, K, D])
        hid = ph.sb("hid", [P, 2, K // 2, P])
        from_h = ph.sb("from_h", [P, 2, K, D])
        member = ph.sb("member", [P, K, P], BF16)
        kinds = ph.sb("kinds", [P, K, R], BF16)
        part = ph.sb("part", [P, K, D])
        msg = ph.sb("msg", [P, 2, K, D])
        prod = ph.sb("prod", [P, K, D])
        small = ph.sb("small", [P, 6, K])
        lq, rt, dist, th = (ph.sb(n, [P, K]) for n in ("lq", "rt", "dist", "th"))
        counts = ph.sb("counts", [R, NR])
        w2, w3 = ph.sb("w2", [P, 2, D]), ph.sb("w3", [P, 2])
        b1, b2 = ph.sb("b1", [P, 1]), ph.sb("b2", [P, 1])
        b3 = ph.sb("b3", [P, 2])
        wc = ph.sb("wc", [P, 2, D])
        ps_src = ph.ps("ps_src", [P, K, P])
        ps_a, ps_b = ph.ps("ps_a", [P, 512]), ph.ps("ps_b", [P, 512])
        ps_dst = ph.ps("ps_dst", [P, K // 2, 512])
        ps_cnt = ps_src[0:R]
        ps_pre, ps_score, ps_turn = ps_a[:, :], ps_a[:, 0:K], ps_a[:, :].bitcast(BF16).rearrange("p (k e) -> p k e", k=K)
        ps_pre2, ps_sum = ps_b[:, :], ps_b[:, :].rearrange("p (k d) -> p k d", k=K)
        x_dst, q_dst, h_dst = (ps_dst[:, :, 0:6 * D].rearrange("p a (b n d) -> p a b n d", b=2, n=3)[:, :, :, n, :]
                               for n in range(3))

        def pairs_of(ap):
            return ap.rearrange("p (a b) d -> p a b d", b=2)

        with nc.Block() as block:
            @block.sync
            def _(sp):
                sp.wait_ge(cleared, 3)
                for n in range(2):
                    half_p = slice(n * D, (n + 1) * D)
                    for d, a in ((w2[half_p, n, :], w["L1_gnn_w2"]), (w3[half_p, n:n + 1], w["L1_gnn_w3"]),
                                 (b1[half_p, :], w["L1_gnn_b1"].unsqueeze(1)), (b2[half_p, :], w["L1_gnn_b2"].unsqueeze(1))):
                        sp.dma_start(d, a).then_inc(w_in, 16)
                sp.dma_start(b3[:, 0:1], w["L1_gnn_b3"].partition_broadcast(P)).then_inc(w_in, 16)
                for n in range(2):
                    sp.dma_start(wc[:, n, :], w["L1_gnn_w1"][2 * D + n, :].partition_broadcast(P)).then_inc(w_in, 16)

                def load(c, q, i):
                    sp.wait_ge(from_dst, free2(c))
                    for k, b in enumerate(bases(nc, ENG.SP, g.base, c)):
                        sp.dma_start(table[:, q % 2, k, :], g.hyp_dst[ds(b, P), :]).then_inc(win[q], 16)
                rounds(sp, [(load, 0)])

            @block.gpsimd
            def _(pool):
                pool.sem_inc(scattered, START)
                prime(pool, ph, g, half)

                def gather(c, q, i):
                    pool.wait_ge(joined, free4(c))
                    pool.wait_ge(gather_at, ready(c))
                    pool.sem_inc(opened, 1)
                    for k in range(K):
                        nc.gpsimd.indirect_dma_start(
                            from_src[:, q, k, :], None, g.hyp_src[:, :],
                            bass.IndirectOffsetOnAxis(ap=src_at[:, q, k:k + 1], axis=0)).then_inc(got[q], 16)

                def send(c, q, i):
                    pool.wait_ge(summed_c, ready(c))
                    scatter(nc, pool, g.sum1, msg[:, q % 2], sum_at[:, q % 2], c, half, opened, scattered)
                rounds(pool, [(gather, 3), (send, 0)])
                for h in range(2):
                    pool.wait_ge(half[h], 64 * CHUNKS + 16)

            @block.scalar
            def _(act):
                for q in (staged, gather_at, turned_c, logged, rooted, geo, tanh, summed_c, act1, act2, h_kept):
                    act.sem_inc(q, START)
                act.wait_ge(w_in, 11 * 16)
                nc.scalar.activation(b3[:, 1:2], b3[:, 0:1], ACT.Copy, scale=0.5).then_inc(added, 1)
                act.wait_ge(added, 1)

                def fields(c, q, i):
                    act.wait_ge(weighted, free4(c))
                    alone(act, mark_a)
                    nc.scalar.activation(edge[:, q, :, :], g.edges[:, 0:SIDX + 1, ds(c * K, K)], ACT.Copy
                                         ).then_inc(staged, 1)
                    nc.scalar.activation(src_at[:, q, :], g.edges[:, SRC, ds(c * K, K)], ACT.Copy
                                         ).then_inc(gather_at, 1)

                def turn_out(c, q, i):
                    act.wait_ge(turned, ready(c))
                    act.wait_ge(from_dst, free2(c))
                    nc.scalar.activation(memberT[:, q % 2, :, :], ps_turn[:, :, :], ACT.Copy).then_inc(turned_c, 1)

                def distance(c, q, i):
                    act.wait_ge(squared, ready(c))
                    alone(act, mark_a)
                    nc.scalar.preload_act_table_set("natural_log_exp_and_others")
                    nc.scalar.activation(lq[:, :], small[:, 2, :], ACT.Ln).then_inc(logged, 1)
                    act.wait_ge(logged, ready(c))
                    nc.scalar.activation(rt[:, :], lq[:, :], ACT.Exp, scale=0.5).then_inc(rooted, 1)
                    act.wait_ge(argued, ready(c))
                    nc.scalar.activation(dist[:, :], small[:, 3, :], ACT.Ln, bias=1.0).then_inc(geo, 1)

                def keep_h(c, q, i):
                    act.wait_ge(taken, ready(c))
                    act.wait_ge(weighted, free2(c))
                    nc.scalar.activation(pairs_of(from_h[:, q % 2]), h_dst, ACT.Copy).then_inc(h_kept, 1)

                def layer1(c, q, i):
                    act.wait_ge(pre, ready(c))
                    act.wait_ge(pre2, free1(c))
                    nc.scalar.activation(hid[:, 0].rearrange("p k e -> p (k e)"), ps_pre, ACT.Silu, bias=b1[:, 0:1]
                                         ).then_inc(act1, 1)

                def layer2(c, q, i):
                    act.wait_ge(pre2, ready(c))
                    act.wait_ge(score, free1(c))
                    nc.scalar.activation(hid[:, 1].rearrange("p k e -> p (k e)"), ps_pre2, ACT.Silu, bias=b2[:, 0:1]
                                         ).then_inc(act2, 1)

                def attention(c, q, i):
                    act.wait_ge(score, ready(c))
                    act.wait_ge(weighted, free1(c))
                    nc.scalar.activation(th[:, :], ps_score, ACT.Tanh, scale=0.5, bias=b3[:, 1:2]).then_inc(tanh, 1)

                def out(c, q, i):
                    act.wait_ge(summed, ready(c))
                    act.wait_ge(scattered, free1(c))
                    alone(act, mark_a)
                    nc.scalar.activation(sum_at[:, q % 2, :], g.edges[:, SIDX, ds(c * K, K)], ACT.Copy)
                    nc.scalar.activation(msg[:, q % 2, :, :], ps_sum, ACT.Copy).then_inc(summed_c, 1)
                rounds(act, [(layer1, 0), (layer2, 0), (keep_h, 1), (fields, 3), (attention, 0), (distance, 1),
                             (turn_out, 2), (out, 0)])

            @block.vector
            def _(dve):
                v = nc.vector
                for q in (members, equal, squared, taken, argued, joined, weighted, count_c):
                    dve.sem_inc(q, START)
                v.memset(w2[:, :, :], 0.0).then_inc(cleared, 1)
                v.memset(w3[:, :], 0.0).then_inc(cleared, 1)
                v.memset(counts[:, :], 0.0).then_inc(cleared, 1)
                dve.wait_ge(cleared, 3)
                dve.wait_ge(w_in, 11 * 16)

                def zero_ones(c, q, i):
                    dve.wait_ge(staged, ready(c))
                    dve.wait_ge(counted, free1(c))
                    v.tensor_tensor(member[:, :, :], repeat(g.iota[:, :], K), spread(edge[:, q, REL, :], P), ALU.is_equal
                                    ).then_inc(members, 1)

                def relations(c, q, i):
                    v.tensor_tensor(kinds[:, :, :], repeat(g.iota[:, 0:R], K), spread(edge[:, q, TYPE, :], R),
                                    ALU.is_equal)

                def same_src(c, q, i):
                    dve.wait_ge(src_rows, ready(c))
                    dve.wait_ge(summed, free4(c))
                    v.tensor_tensor(same[:, q], ps_src[:, :, :], spread(edge[:, q, SRC, :], P), ALU.is_equal
                                    ).then_inc(equal, 1)

                def argument(c, q, i):
                    regs = bases(nc, ENG.DVE, g.base, c)
                    src = from_src[:, q, :, 0:D]
                    z, t, square = (small[:, n, :] for n in range(3))

                    def count_tile(k):
                        if k:
                            dve.wait_ge(step_c, c * K + k)
                        window = counts[:, ds(regs[k], P)]
                        v.tensor_tensor(window, window, ps_cnt[:, k, :], ALU.add).then_inc(step_c, 1)

                    dve.wait_ge(from_dst, ready(c))
                    dve.wait_ge(got[q], 16 * K * (i + 1))
                    v.tensor_tensor(pairs_of(prod[:, :, :]), x_dst, pairs_of(from_src[:, q, :, D:2 * D]), ALU.mult
                                    ).then_inc(step_a, 1)
                    dve.wait_ge(counted, ready(c))
                    count_tile(0)
                    dve.wait_ge(step_a, c * 6 + 1)
                    v.tensor_reduce(z, prod[:, :, :], AX.X, ALU.add).then_inc(step_a, 1)
                    count_tile(1)
                    dve.wait_ge(step_a, c * 6 + 2)
                    v.tensor_scalar(z, z, ACOSH_MIN, None, ALU.max).then_inc(step_a, 1)
                    count_tile(2)
                    dve.wait_ge(step_a, c * 6 + 3)
                    v.tensor_scalar(t, z, 1.0, None, ALU.subtract).then_inc(step_a, 1)
                    count_tile(3)
                    dve.wait_ge(step_a, c * 6 + 4)
                    v.scalar_tensor_tensor(square, z, 1.0, t, ALU.add, ALU.mult).then_inc(step_a, 1)
                    count_tile(4)
                    dve.wait_ge(step_a, c * 6 + 5)
                    dve.sem_inc(squared, 1)
                    v.tensor_tensor(pairs_of(src), pairs_of(src), q_dst, ALU.add).then_inc(step_a, 1)
                    count_tile(5)
                    dve.wait_ge(step_a, c * 6 + 6)
                    dve.sem_inc(taken, 1)

                def last_counts(c, q, i):
                    regs = bases(nc, ENG.DVE, g.base, c, K - 2, 2)
                    for n, k in enumerate((K - 2, K - 1)):
                        dve.wait_ge(step_c, c * K + k)
                        window = counts[:, ds(regs[n], P)]
                        v.tensor_tensor(window, window, ps_cnt[:, k, :], ALU.add).then_inc(step_c, 1)
                    dve.wait_ge(step_c, c * K + K)
                    dve.sem_inc(count_c, 1)

                def inputs(c, q, i):
                    chain = Chain(dve, step_b, c * 5)
                    src = from_src[:, q, :, 0:D]
                    dve.wait_ge(rooted, ready(c))
                    chain(v.tensor_tensor(small[:, 3, :], small[:, 1, :], rt[:, :], ALU.add))
                    dve.sem_inc(argued, 1)
                    chain(v.tensor_tensor(prod[:, :, :], spread(edge[:, q, EW1, :], D), repeat(wc[:, 0, :], K), ALU.mult))
                    chain(v.tensor_tensor(src, src, prod[:, :, :], ALU.add))
                    dve.wait_ge(geo, ready(c))
                    chain(v.tensor_tensor(prod[:, :, :], spread(dist[:, :], D), repeat(wc[:, 1, :], K), ALU.mult))
                    dve.wait_ge(pre, free1(c))
                    chain(v.tensor_tensor(row[:, :, :], src, prod[:, :, :], ALU.add))
                    dve.sem_inc(joined, 1)

                def messages(c, q, i):
                    chain = Chain(dve, step_d, c * 2)
                    dve.wait_ge(tanh, ready(c))
                    chain(v.tensor_scalar(small[:, 4, :], th[:, :], 0.5, 0.5, ALU.mult, ALU.add))
                    chain(v.tensor_tensor(small[:, 5, :], small[:, 4, :], edge[:, q, EW1, :], ALU.mult))
                    dve.wait_ge(h_kept, ready(c))
                    dve.wait_ge(summed, free1(c))
                    v.tensor_tensor(part[:, :, :], from_h[:, q % 2], spread(small[:, 5, :], D), ALU.mult
                                    ).then_inc(weighted, 1)
                rounds(dve, [(argument, 1), (zero_ones, 2), (last_counts, 1), (relations, 2), (messages, 0),
                             (same_src, 2), (inputs, 1)])

            @block.tensor
            def _(pe):
                for q in (turned, from_dst, src_rows, counted, summed, pre, pre2, score):
                    pe.sem_inc(q, START)
                pe.wait_ge(w_in, 11 * 16)

                def source_rows(c, q, i):
                    pe.wait_ge(staged, ready(c))
                    pe.wait_ge(count_c, free1(c))
                    for k in range(K):
                        last = nc.tensor.transpose(ps_src[:, k, :], edge[:, q, SRC, k:k + 1].broadcast_to([P, P]),
                                                   g.ident[:, :])
                    last.then_inc(src_rows, 1)

                def turn_members(c, q, i):
                    pe.wait_ge(members, ready(c))
                    pe.wait_ge(tanh, free2(c))
                    for k in range(K):
                        last = nc.tensor.transpose(ps_turn[:, k, :], member[:, k, :], g.ident16[:, :])
                    last.then_inc(turned, 1)

                def count(c, q, i):
                    pe.wait_ge(equal, ready(c))
                    for k in range(K):
                        last = nc.tensor.matmul(ps_cnt[:, k, :], kinds[:, k, :], member[:, k, :], start=True, stop=True)
                    last.then_inc(counted, 1)

                def read_dst(c, q, i):
                    pe.wait_ge(turned_c, ready(c))
                    pe.wait_ge(win[q], 16 * K * (i + 1))
                    pe.wait_ge(taken, free1(c))
                    pe.wait_ge(h_kept, free1(c))
                    for k in range(K):
                        last = nc.tensor.matmul(ps_dst[:, k // 2, k % 2 * 3 * D:(k % 2 + 1) * 3 * D],
                                                memberT[:, q % 2, k, :], table[:, q % 2, k, :], start=True, stop=True)
                    last.then_inc(from_dst, 1)

                def layer1(c, q, i):
                    pe.wait_ge(joined, ready(c))
                    if not isinstance(c, int) or c < CHUNKS - 1:
                        pe.wait_ge(turned_c, ready(c + 1))
                    alone(pe, mark_p)
                    for k in range(0, K, 2):
                        last = nc.tensor.transpose(ps_pre[:, k // 2 * P:(k // 2 + 1) * P],
                                                   row[:, k:k + 2, :].rearrange("p k d -> p (k d)"), g.ident[:, :])
                    last.then_inc(pre, 1)

                def layer2(c, q, i):
                    pe.wait_ge(act1, ready(c))
                    pe.wait_ge(summed_c, free1(c))
                    alone(pe, mark_p)
                    nc.tensor.matmul(ps_pre2, w2[:, :, :].rearrange("p a d -> p (a d)"),
                                     hid[:, 0].rearrange("p k e -> p (k e)"), start=True, stop=True).then_inc(pre2, 1)

                def scores(c, q, i):
                    pe.wait_ge(act2, ready(c))
                    for k in range(0, K, 2):
                        last = nc.tensor.matmul(ps_score[:, k:k + 2], hid[:, 1, k // 2, :], w3[:, :], start=True, stop=True)
                    last.then_inc(score, 1)

                def combine(c, q, i):
                    pe.wait_ge(weighted, ready(c))
                    for k in range(K):
                        last = nc.tensor.matmul(ps_sum[:, k, :], same[:, q, k, :], part[:, k, :], start=True, stop=True)
                    last.then_inc(summed, 1)
                rounds(pe, [(layer1, 0), (layer2, 0), (scores, 0), (turn_members, 2), (source_rows, 2), (combine, 0),
                            (count, 2), (read_dst, 2)])

        columns_to_nodes(nc, g, ph, counts, R, [ps_dst[:, n, :] for n in range(2)])
        with nc.Block() as block:
            @block.vector
            def _(dve):
                chain = Chain(dve, inverted)
                chain(nc.vector.tensor_scalar(g.node[:, :, 0:R], g.node[:, :, 0:R], 1.0, None, ALU.max))
                chain(nc.vector.reciprocal(g.node[:, :, 0:R], g.node[:, :, 0:R]))

            @block.sync
            def _(sp):
                sp.wait_ge(inverted, 2)
                sp.dma_start(nodes_view(g.inv_count, slice(0, R)), g.node[:, :, 0:R]).then_inc(kept, 16)
                sp.wait_ge(kept, 16)


def columns_to_nodes(nc, g, outer, sums, rows, ps):
    with Phase(nc, outer.name + "_turn") as ph:
        staged, turned, copied, mark_a, mark_p, mark_d = ph.sems("staged turned copied mark_a mark_p mark_d")
        stage = ph.sb("stage", [rows, 2, P])
        with nc.Block() as block:
            @block.scalar
            def _(act):
                act.sem_inc(staged, START)

                def body(t, s, i):
                    act.wait_ge(turned, free2(t))
                    alone(act, mark_a)
                    nc.scalar.activation(stage[:, s, :], sums[0:rows, ds(t * P, P)], ACT.Copy).then_inc(staged, 1)
                pairs(act, body, NT)

            @block.tensor
            def _(pe):
                pe.sem_inc(turned, START)

                def body(t, s, i):
                    pe.wait_ge(staged, ready(t))
                    pe.wait_ge(copied, free2(t))
                    alone(pe, mark_p)
                    nc.tensor.matmul(ps[s][:, 0:rows], stage[:, s, :], g.ident[0:rows, 0:rows], start=True, stop=True
                                     ).then_inc(turned, 1)
                pairs(pe, body, NT)

            @block.vector
            def _(dve):
                dve.sem_inc(copied, START)

                def body(t, s, i):
                    dve.wait_ge(turned, ready(t))
                    alone(dve, mark_d)
                    nc.vector.tensor_copy(g.node[:, ds(t, 1), 0:rows].rearrange("p o r -> p (o r)"), ps[s][:, 0:rows]
                                          ).then_inc(copied, 1)
                pairs(dve, body, NT)


def after_hyperbolic(nc, g):
    with Phase(nc, "hyp_end") as ph:
        loaded, used, step, stored, done, asked, given, acted = ph.sems("loaded used step stored done asked given acted")
        part_in = [ph.sem(f"part{n}") for n in range(2)]
        x, y, stat = ph.sb("x", [P, NT, D]), ph.sb("y", [P, NT, D]), ph.sb("stat", [P, 4, NT])
        part = [ph.sb(f"part{n}", [P, NT, D]) for n in range(2)]
        gamma, beta = ph.sb("gamma", [P, D]), ph.sb("beta", [P, D])
        h = g.node[:, :, 0:D]
        with nc.Block() as block:
            @block.sync
            def _(sp):
                sp.dma_start(x[:, :, :], nodes_view(g.xs)).then_inc(loaded, 16)
                sp.dma_start(h, nodes_view(g.hyp_dst, slice(2 * D, 3 * D))).then_inc(loaded, 16)
                sp.dma_start(gamma[:, :], g.w["L1_gnn_gamma"].partition_broadcast(P)).then_inc(loaded, 16)
                sp.dma_start(beta[:, :], g.w["L1_gnn_beta"].partition_broadcast(P)).then_inc(loaded, 16)
                sum_loads(sp, g.sum1, part, part_in, used)
                sp.wait_ge(done, 4)
                sp.dma_start(nodes_view(g.xs), x[:, :, :]).then_inc(stored, 16)
                sp.wait_ge(stored, 16)

            @block.gpsimd
            def _(pool):
                power(nc, g, pool, asked, given, 1, stat[:, 1, :], -0.5)
                power(nc, g, pool, asked, given, 2, stat[:, 2, :], 0.5)
                power(nc, g, pool, asked, given, 3, stat[:, 1, :], -0.5)

            @block.scalar
            def _(act):
                act.wait_ge(done, 2)
                nc.scalar.activation(stat[:, 3, :], stat[:, 2, :], ACT.Tanh, scale=0.5).then_inc(acted, 1)
                act.wait_ge(done, 3)
                nc.scalar.activation(y[:, :, :], y[:, :, :], ACT.Silu).then_inc(acted, 1)

            @block.vector
            def _(dve):
                v = nc.vector
                sum_adds(nc, dve, y, part, part_in, used)
                chain = Chain(dve, step)
                dve.wait_ge(loaded, 64)
                chain(v.tensor_tensor(y[:], y[:], h, ALU.add))
                chain(v.tensor_reduce(stat[:, 0, :], y[:], AX.X, ALU.add))
                chain(v.tensor_scalar(stat[:, 0, :], stat[:, 0, :], 1.0 / D, None, ALU.mult))
                chain(v.tensor_tensor(y[:], y[:], spread(stat[:, 0, :], D), ALU.subtract))
                chain(v.tensor_tensor(part[0][:], y[:], y[:], ALU.mult))
                chain(v.tensor_reduce(stat[:, 1, :], part[0][:], AX.X, ALU.add))
                chain(v.tensor_scalar(stat[:, 1, :], stat[:, 1, :], 1.0 / D, 1e-5, ALU.mult, ALU.add))
                ask_power(dve, asked, given, 1)
                chain(v.tensor_tensor(y[:], y[:], spread(stat[:, 1, :], D), ALU.mult))
                chain(v.tensor_tensor(y[:], y[:], repeat(gamma[:, :], NT), ALU.mult))
                chain(v.tensor_tensor(y[:], y[:], repeat(beta[:, :], NT), ALU.add))
                chain(v.tensor_tensor(part[0][:], y[:], y[:], ALU.mult))
                chain(v.tensor_reduce(stat[:, 2, :], part[0][:, :, 1:D], AX.X, ALU.add))
                ask_power(dve, asked, given, 2)
                chain(v.tensor_scalar(stat[:, 2, :], stat[:, 2, :], 1e-7, None, ALU.max))
                dve.sem_inc(done, 2)
                chain(v.reciprocal(stat[:, 0, :], stat[:, 2, :]))
                dve.wait_ge(acted, 1)
                chain(v.tensor_tensor(stat[:, 0, :], stat[:, 0, :], stat[:, 3, :], ALU.mult))
                chain(v.tensor_tensor(y[:], y[:], spread(stat[:, 0, :], D), ALU.mult))
                dve.sem_inc(done, 1)
                dve.wait_ge(acted, 2)
                chain(v.tensor_tensor(part[0][:], y[:], y[:], ALU.mult))
                chain(v.tensor_reduce(stat[:, 0, :], part[0][:, :, 1:D], AX.X, ALU.add))
                chain(v.tensor_scalar(stat[:, 1, :], stat[:, 0, :], -1.0, 1.0, ALU.mult, ALU.add))
                chain(v.tensor_scalar(stat[:, 1, :], stat[:, 1, :], 1e-7, None, ALU.max))
                chain(v.reciprocal(stat[:, 1, :], stat[:, 1, :]))
                chain(v.tensor_scalar(stat[:, 0, :], stat[:, 0, :], 1.0, None, ALU.add))
                chain(v.tensor_tensor(y[:], y[:], spread(stat[:, 1, :], D), ALU.mult))
                chain(v.tensor_scalar(y[:], y[:], 2.0, None, ALU.mult))
                chain(v.tensor_tensor(y[:, :, 0:1], stat[:, 0, :].unsqueeze(2), stat[:, 1, :].unsqueeze(2), ALU.mult))
                chain(v.tensor_tensor(x[:], x[:], y[:], ALU.add))
                layernorm_relu(nc, dve, chain, x, h, y, stat, asked, given, 3)
                dve.sem_inc(done, 1)


def edges_attention(nc, g, name):
    with Phase(nc, name) as ph:
        (staged, gather_at, members, narrowed, turned, turned_c, dst_at, logit, logit_t, scanned, back, back_u, tops,
         expo, shift_e, shifted, filled, summed, added) = ph.sems(
            "staged gather_at members narrowed turned turned_c dst_at logit logit_t scanned back back_u tops expo "
            "shift_e shifted filled summed added")
        step_a, step_b, step_c, opened, cleared, mark_a, mark_p = ph.sems(
            "step_a step_b step_c opened cleared mark_a mark_p")
        win, mask_in, got = ([ph.sem(f"{n}{q}") for q in range(4)] for n in ("win", "mask_in", "got"))
        rows = D + 2 * H
        edge = ph.sb("edge", [P, 4, END + 1, K])
        src_at = ph.sb("src_at", [P, 4, K], I32)
        table = ph.sb("table", [P, 4, K, 3 * H], BF16)
        masks = ph.sb("masks", [H, 2, 2, CE])
        from_src = ph.sb("from_src", [P, 4, K, D + H])
        spot = g.node[:, :, :].rearrange("p t d -> p (t d)")
        member = spot[:, 0:4 * CE].rearrange("p (s k e) -> p s k e", s=4, k=K)
        memberT = ph.sb("memberT", [P, K, P], BF16)
        leaky = ph.sb("leaky", [P, 2, K, H])
        fwd, top = ph.sb("fwd", [H, 2, CE]), ph.sb("top", [H, CE])
        arg = ph.sb("arg", [P, K, H])
        shift = ph.sb("shift", [H, 2])
        msg = ph.sb("msg", [P, 2, K, rows])
        sums = ph.sb("sums", [rows, NR])
        member16 = ph.sb("member16", [P, K, P], BF16)
        ps_turn = ph.ps("ps_turn", [P, K, P], BF16)
        ps_log, ps_sum = (ph.ps(n, [P, K, P]) for n in ("ps_log", "ps_sum"))
        ps_dst, ps_top = ph.ps("ps_dst", [P, 512]), ph.ps("ps_top", [P, 512])
        dst_v = ps_dst[:, 0:K * H].rearrange("p (k h) -> p k h", k=K)
        top_v = ps_top[:, 0:K * H].rearrange("p (k h) -> p k h", k=K)
        log_flat = ps_log[0:H, :, :].rearrange("p k e -> p (k e)")
        with nc.Block() as block:
            @block.sync
            def _(sp):
                def load_masks(c, q, i):
                    sp.wait_ge(scanned, free2(c))
                    for n, m in enumerate((g.first_mask, g.last_mask)):
                        sp.dma_start(masks[:, q % 2, n, :], m[ds(c * CE, CE)].partition_broadcast(H)
                                     ).then_inc(mask_in[q], 16)

                def load_windows(c, q, i):
                    sp.wait_ge(dst_at, free4(c))
                    for k, b in enumerate(bases(nc, ENG.SP, g.base, c)):
                        sp.dma_start(table[:, q, k, :], g.gat_dst16[ds(b, P), :]).then_inc(win[q], 16)
                rounds(sp, [(load_windows, 3), (load_masks, 1)])

            @block.gpsimd
            def _(pool):
                def gather(c, q, i):
                    pool.wait_ge(filled, free4(c))
                    pool.wait_ge(gather_at, ready(c))
                    pool.sem_inc(opened, 1)
                    for k in range(K):
                        nc.gpsimd.indirect_dma_start(
                            from_src[:, q, k, :], None, g.gat_src[:, :],
                            bass.IndirectOffsetOnAxis(ap=src_at[:, q, k:k + 1], axis=0)).then_inc(got[q], 16)
                rounds(pool, [(gather, 0)])

            @block.scalar
            def _(act):
                for q in (staged, gather_at, turned_c, expo, shift_e):
                    act.sem_inc(q, START)

                def fields(c, q, i):
                    act.wait_ge(filled, free4(c))
                    alone(act, mark_a)
                    nc.scalar.activation(src_at[:, q, :], g.edges[:, SRC, ds(c * K, K)], ACT.Copy
                                         ).then_inc(gather_at, 1)
                    nc.scalar.activation(edge[:, q, :, :], g.edges[:, 0:END + 1, ds(c * K, K)], ACT.Copy
                                         ).then_inc(staged, 1)

                def narrow(c, q, i):
                    act.wait_ge(members, ready(c))
                    act.wait_ge(turned, free1(c))
                    nc.scalar.activation(member16[:, :, :], member[:, q], ACT.Copy).then_inc(narrowed, 1)

                def turn_out(c, q, i):
                    act.wait_ge(turned, ready(c))
                    act.wait_ge(dst_at, free1(c))
                    nc.scalar.activation(memberT[:, :, :], ps_turn[:, :, :], ACT.Copy).then_inc(turned_c, 1)

                def exponents(c, q, i):
                    act.wait_ge(back_u, ready(c))
                    nc.scalar.activation(msg[:, q % 2, :, D:D + H], arg[:, :, :], ACT.Exp).then_inc(expo, 1)

                def exp_shift(c, q, i):
                    act.wait_ge(scanned, ready(c))
                    nc.scalar.activation(shift[:, 1:2], shift[:, 0:1], ACT.Exp).then_inc(shift_e, 1)
                rounds(act, [(fields, 4), (exponents, 1), (narrow, 3), (turn_out, 3), (exp_shift, 2)])

            @block.vector
            def _(dve):
                v = nc.vector
                for q in (members, logit, scanned, back_u, shifted, filled):
                    dve.sem_inc(q, START)
                dve.sem_inc(added, 2 * START)
                v.memset(sums[:, :], 0.0).then_inc(cleared, 1)
                v.memset(fwd[:, 1, :], -BIG).then_inc(cleared, 1)
                dve.wait_ge(cleared, 2)

                def zero_ones(c, q, i):
                    dve.wait_ge(staged, ready(c))
                    dve.wait_ge(summed, half_ready(c, 1) - 8)
                    v.tensor_tensor(member[:, q], repeat(g.iota[:, :], K), spread(edge[:, q, REL, :], P), ALU.is_equal
                                    ).then_inc(members, 1)

                def tops_of(c, q, i):
                    dve.wait_ge(back, ready(c))
                    dve.wait_ge(summed, half_ready(c, 1) - 4)
                    v.tensor_tensor(msg[:, q % 2, :, D + H:rows], top_v, spread(edge[:, q, END, :], H), ALU.mult
                                    ).then_inc(tops, 1)

                def arguments(c, q, i):
                    dve.wait_ge(expo, free1(c))
                    v.tensor_tensor(arg[:, :, :], leaky[:, q % 2], top_v, ALU.subtract).then_inc(back_u, 1)

                def logits(c, q, i):
                    dve.wait_ge(dst_at, ready(c))
                    dve.wait_ge(got[q], 16 * K * (i + 1))
                    v.tensor_tensor(leaky[:, q % 2], dst_v, from_src[:, q, :, D:D + H], ALU.add).then_inc(step_a, 1)

                def leaky_logits(c, q, i):
                    one = leaky[:, q % 2].rearrange("p k h -> p (k h)")
                    dve.wait_ge(step_a, c + 1)
                    v.scalar_tensor_tensor(one, one, LRELU, one, ALU.mult, ALU.max).then_inc(logit, 1)

                def messages(c, q, i):
                    s = q % 2
                    dve.wait_ge(expo, ready(c))
                    v.tensor_tensor(
                        msg[:, s, :, 0:D].rearrange("p k (h c) -> p k h c", h=H),
                        from_src[:, q, :, 0:D].rearrange("p k (h c) -> p k h c", h=H),
                        msg[:, s, :, D:D + H].unsqueeze(3).broadcast_to([P, K, H, D // H]), ALU.mult).then_inc(filled, 1)

                def maxima_so_far(c, q, i):
                    s = q % 2
                    dve.wait_ge(logit_t, ready(c))
                    dve.wait_ge(mask_in[q], 16 * 2 * (i + 1))
                    v.tensor_tensor_scan(fwd[:, s, :], masks[:, s, 0, :], log_flat, fwd[:, 1 - s, CE - 1:CE], ALU.add,
                                         ALU.max).then_inc(step_b, 1)

                def maxima(c, q, i):
                    s = q % 2
                    dve.wait_ge(step_b, c * 3 + 1)
                    dve.wait_ge(back, free1(c))
                    v.tensor_tensor_scan(top[:, ::-1], masks[:, s, 1, ::-1], fwd[:, s, ::-1], -BIG, ALU.add, ALU.max
                                         ).then_inc(step_b, 1)

                def shift_by(c, q, i):
                    dve.wait_ge(step_b, c * 3 + 2)
                    v.tensor_tensor(shift[:, 0:1], fwd[:, 1 - q % 2, CE - 1:CE], top[:, 0:1], ALU.subtract
                                    ).then_inc(step_b, 1)

                def shift_down(c, q, i):
                    dve.wait_ge(step_b, c * 3 + 3)
                    v.tensor_scalar(shift[:, 0:1], shift[:, 0:1], 0.0, None, ALU.min).then_inc(scanned, 1)

                own = []

                def own_window(c, q, i):
                    own[:] = bases(nc, ENG.DVE, g.base, c, 0, 1)

                def rescale(c, q, i):
                    v.tensor_tensor(sums[:, ds(own[0], 1)], sums[:, ds(own[0], 1)], ps_top[0:rows, K * H:K * H + 1],
                                    ALU.mult).then_inc(shifted, 1)

                regs = []

                def windows(c, q, i):
                    regs[:] = bases(nc, ENG.DVE, g.base, c)

                def add(k):
                    def step(c, q, i):
                        if k == 0:
                            dve.wait_ge(shifted, ready(c))
                        else:
                            dve.wait_ge(step_c, c * K + k)
                        if k % 4 == 0:
                            dve.wait_ge(summed, half_ready(c, k // 4))
                        window = sums[:, ds(regs[k], P)]
                        v.tensor_tensor(window, window, ps_sum[0:rows, k, :], ALU.add).then_inc(step_c, 1)
                        if k % 4 == 3:
                            dve.wait_ge(step_c, c * K + k + 1)
                            dve.sem_inc(added, 1)
                    return step
                rounds(dve, [(windows, 0), (own_window, 1), (tops_of, 1), (add(0), 0), (arguments, 1), (add(1), 0),
                             (logits, 2), (add(2), 0), (leaky_logits, 2), (add(3), 0), (messages, 1), (add(4), 0),
                             (maxima_so_far, 2), (add(5), 0), (maxima, 2), (add(6), 0), (shift_by, 2),
                             (add(7), 0), (shift_down, 2), (rescale, 1), (zero_ones, 4)])

            @block.tensor
            def _(pe):
                for q in (turned, dst_at, logit_t, back):
                    pe.sem_inc(q, START)
                pe.sem_inc(summed, 2 * START)

                def turn_members(c, q, i):
                    pe.wait_ge(narrowed, c + 1)
                    pe.wait_ge(turned_c, free1(c))
                    for k in range(K):
                        last = nc.tensor.transpose(ps_turn[:, k, :], member16[:, k, :], g.ident16[:, :])
                    last.then_inc(turned, 1)

                def read_dst(c, q, i):
                    pe.wait_ge(turned_c, ready(c))
                    pe.wait_ge(win[q], 16 * K * (i + 1))
                    pe.wait_ge(logit, free1(c))
                    for k in range(K):
                        for n in range(3):
                            last = nc.tensor.matmul(dst_v[:, k, :], memberT[:, k, :], table[:, q, k, n * H:(n + 1) * H],
                                                    start=n == 0, stop=n == 2)
                    last.then_inc(dst_at, 1)

                def turn_logits(c, q, i):
                    pe.wait_ge(logit, ready(c))
                    pe.wait_ge(scanned, free1(c))
                    for k in range(K):
                        last = nc.tensor.transpose(ps_log[0:H, k, :], leaky[:, q % 2, k, :], g.ident[:, :])
                    last.then_inc(logit_t, 1)

                def turn_maxima(c, q, i):
                    pe.wait_ge(scanned, ready(c))
                    pe.wait_ge(back_u, free1(c))
                    pe.wait_ge(shifted, free1(c))
                    alone(pe, mark_p)
                    for k in range(K):
                        nc.tensor.transpose(top_v[:, k, :], top[:, k * P:(k + 1) * P], g.ident[0:H, 0:H])
                    pe.wait_ge(shift_e, ready(c))
                    nc.tensor.matmul(ps_top[0:rows, K * H:K * H + 1], g.heads[:, 0:rows], shift[:, 1:2], start=True,
                                     stop=True).then_inc(back, 1)

                def product(h):
                    def step(c, q, i):
                        pe.wait_ge(filled, ready(c))
                        pe.wait_ge(tops, c + 1)
                        pe.wait_ge(added, half_ready(c, h) - 2)
                        for k in range(4 * h, 4 * h + 4):
                            last = nc.tensor.matmul(ps_sum[0:rows, k, :], msg[:, q % 2, k, :], member[:, q, k, :],
                                                    start=True, stop=True)
                        last.then_inc(summed, 1)
                    return step
                rounds(pe, [(turn_logits, 2), (product(0), 1), (turn_members, 3), (turn_maxima, 2), (read_dst, 3),
                            (product(1), 1)])
        columns_to_nodes(nc, g, ph, sums, rows, [ps_dst[:, :], ps_top[:, :]])


def after_attention(nc, g, name, bias, last):
    with Phase(nc, name) as ph:
        loaded, step, stored, done, asked, given, exps = ph.sems("loaded step stored done asked given exps")
        tab, ad = ph.sb("tab", [P, NT, D + H]), ph.sb("ad", [P, NT, H])
        top, own = ph.sb("top", [P, NT, H]), ph.sb("own", [P, NT, H])
        bv, stat = ph.sb("bv", [P, D]), ph.sb("stat", [P, 2, NT])
        x = ph.sb("x", [P, NT, D]) if last else None
        num, den, seen = g.node[:, :, 0:D], g.node[:, :, D:D + H], g.node[:, :, D + H:D + 2 * H]

        def by_head(ap):
            return ap.rearrange("p t (h c) -> p t h c", h=H)

        def over_head(ap):
            return ap.unsqueeze(3).broadcast_to([P, NT, H, D // H])

        with nc.Block() as block:
            @block.sync
            def _(sp):
                sp.dma_start(tab[:, :, :], nodes_view(g.gat_src, slice(0, D + H))).then_inc(loaded, 16)
                sp.dma_start(ad[:, :, :], nodes_view(g.gat_dst, slice(0, H))).then_inc(loaded, 16)
                sp.dma_start(bv[:, :], bias.partition_broadcast(P)).then_inc(loaded, 16)
                if last:
                    sp.dma_start(x[:, :, :], nodes_view(g.xs)).then_inc(loaded, 16)
                    sp.wait_ge(done, 1)
                    sp.dma_start(nodes_view(g.xs), x[:, :, :]).then_inc(stored, 16)
                    sp.wait_ge(stored, 16)

            @block.scalar
            def _(act):
                act.wait_ge(exps, 1)
                nc.scalar.activation(top[:, :, :], top[:, :, :], ACT.Exp).then_inc(exps, 1)
                nc.scalar.activation(own[:, :, :], own[:, :, :], ACT.Exp).then_inc(exps, 1)

            if last:
                @block.gpsimd
                def _(pool):
                    power(nc, g, pool, asked, given, 1, stat[:, 1, :], -0.5)

            @block.vector
            def _(dve):
                v = nc.vector
                chain = Chain(dve, step)
                dve.wait_ge(loaded, 16 * (4 if last else 3))
                chain(v.tensor_tensor(ad[:], ad[:], tab[:, :, D:D + H], ALU.add))
                chain(v.tensor_scalar(top[:], ad[:], LRELU, None, ALU.mult))
                chain(v.tensor_tensor(own[:], top[:], ad[:], ALU.max))
                chain(v.tensor_tensor(ad[:], own[:], seen, ALU.max))
                chain(v.tensor_tensor(top[:], seen, ad[:], ALU.subtract))
                chain(v.tensor_tensor(own[:], own[:], ad[:], ALU.subtract))
                dve.sem_inc(exps, 1)
                dve.wait_ge(exps, 3)
                chain(v.tensor_tensor(den, den, top[:], ALU.mult))
                chain(v.tensor_tensor(den, den, own[:], ALU.add))
                chain(v.tensor_scalar(den, den, 1e-16, None, ALU.add))
                chain(v.reciprocal(den, den))
                chain(v.tensor_tensor(by_head(num), by_head(num), over_head(top[:, :, :]), ALU.mult))
                chain(v.tensor_tensor(by_head(tab[:, :, 0:D]), by_head(tab[:, :, 0:D]), over_head(own[:, :, :]), ALU.mult))
                chain(v.tensor_tensor(num, num, tab[:, :, 0:D], ALU.add))
                chain(v.tensor_tensor(by_head(num), by_head(num), over_head(den), ALU.mult))
                chain(v.tensor_tensor(num, num, repeat(bv[:, :], NT), ALU.add))
                if not last:
                    chain(v.tensor_scalar(num, num, 0.0, None, ALU.max))
                else:
                    chain(v.tensor_tensor(x[:], x[:], num, ALU.add))
                    dve.sem_inc(done, 1)
                    layernorm_relu(nc, dve, chain, x, num, tab[:, :, 0:D], stat, asked, given)


def typed_tables(nc, g, name, weights):
    with Phase(nc, name) as ph:
        w_in, split_w, split_h, rest_w, staged, turned, turned_c, made, even, odd, mark_a = ph.sems(
            "w_in split_w split_h rest_w staged turned turned_c made even odd mark_a")
        put = [ph.sem(f"put{s}") for s in range(2)]
        parts = ph.sb("parts", [P, NT, 3, D], BF16)
        stage, ft = ph.sb("stage", [P, 2, 4, D], BF16), ph.sb("ft", [P, 2, 2, P], BF16)
        w16 = ph.sb("w16", [P, 4, R * D], BF16)
        res = ph.sb("res", [P, 2, R * D])
        w = res[:, 0, :]
        psf = [ph.ps(f"psf{s}", [P, 8, P], BF16)[:, 0:2, :] for s in range(2)]
        banks = [ph.ps(f"bank{n}", [P, 512]) for n in range(6)]
        groups = [(q, 8 * q, min(8, R - 8 * q)) for q in range((R + 7) // 8)]
        rows = g.typed.rearrange("(n r) d -> n (r d)", r=R)
        n_even, n_odd = 5, 4

        def copied(q, t):
            return (even, (t + 1) * n_even + q // 2 + 1) if q % 2 == 0 else (odd, (t + 1) * n_odd + q // 2 + 1)

        def copy_out(eng, move, parity, t, s, i):
            eng.wait_ge(put[s], 16 * i + 16)
            for q, r, m in groups:
                if q % 2 == parity:
                    eng.wait_ge(made, (t + 1) * len(groups) + q + 1)
                    move(res[:, s, r * D:(r + m) * D], banks[q % 6][:, 0:m * D]).then_inc((even, odd)[parity], 1)

        with nc.Block() as block:
            @block.sync
            def _(sp):
                prime(sp, ph, g, put)
                for n in range(2):
                    sp.dma_start(w[n * D:(n + 1) * D, :].rearrange("d (r k) -> d r k", r=R),
                                 weights.rearrange("r d k -> d r k")).then_inc(w_in, 16)

                def store(t, s, i):
                    for q in (8, 7):
                        sem, value = copied(q, t)
                        sp.wait_ge(sem, value)
                    sp.dma_start(rows[ds(t * P, P), :], res[:, s, :]).then_inc(put[s], 16)
                pairs(sp, store, NT)
                for s in range(2):
                    sp.wait_ge(put[s], 16 * (NT // 2) + 16)

            @block.gpsimd
            def _(pool):
                for n in range(2):
                    pool.wait_ge(split_w, n + 1)
                    nc.gpsimd.tensor_tensor(w, w, w16[:, n, :], ALU.subtract).then_inc(rest_w, 1)

            @block.scalar
            def _(act):
                act.wait_ge(w_in, 32)
                for n in range(3):
                    if n:
                        act.wait_ge(rest_w, n)
                    nc.scalar.activation(w16[:, n, :], w, ACT.Copy).then_inc(split_w, 1)
                act.wait_ge(split_w, 3)
                nc.scalar.activation(w16[0:D, 3, :], w16[0:D, 0, :], ACT.Copy).then_inc(split_w, 1)
                nc.scalar.activation(w16[D:P, 3, :], w16[D:P, 1, :], ACT.Copy).then_inc(split_w, 1)
                act.sem_inc(staged, START)
                act.sem_inc(even, n_even)
                act.wait_ge(split_h, 5)
                act.wait_ge(split_w, 5)

                def head(t, s, i):
                    act.wait_ge(turned, free2(t))
                    alone(act, mark_a)
                    nc.scalar.activation(stage[:, s, 0:3, :], parts[:, ds(t, 1), :, :].rearrange("p o a d -> p (o a) d"),
                                         ACT.Copy)
                    nc.scalar.activation(stage[:, s, 3, :], parts[:, ds(t, 1), 2, :].rearrange("p o d -> p (o d)"),
                                         ACT.Copy).then_inc(staged, 1)

                def tail(t, s, i):
                    copy_out(act, lambda o, a: nc.scalar.activation(o, a, ACT.Copy), 0, t, s, i)
                skewed(act, head, tail, NT)

            @block.vector
            def _(dve):
                v = nc.vector
                h = g.node[:, :, 0:D]
                chain = Chain(dve, split_h)
                chain(v.tensor_copy(parts[:, :, 0, :], h))
                chain(v.tensor_tensor(h, h, parts[:, :, 0, :], ALU.subtract))
                chain(v.tensor_copy(parts[:, :, 1, :], h))
                chain(v.tensor_tensor(h, h, parts[:, :, 1, :], ALU.subtract))
                chain(v.tensor_copy(parts[:, :, 2, :], h))
                dve.wait_ge(split_w, 5)
                dve.sem_inc(turned_c, START)
                dve.sem_inc(odd, n_odd)

                def head(t, s, i):
                    dve.wait_ge(turned, ready(t))
                    dve.wait_ge(made, t * len(groups) + 1)
                    v.tensor_copy(ft[:, s, :, :], psf[s]).then_inc(turned_c, 1)

                def tail(t, s, i):
                    copy_out(dve, v.tensor_copy, 1, t, s, i)
                skewed(dve, head, tail, NT)

            @block.tensor
            def _(pe):
                pe.sem_inc(turned, START)
                pe.sem_inc(made, len(groups))
                pe.wait_ge(split_w, 5)

                def head(t, s, i):
                    pe.wait_ge(staged, ready(t))
                    pe.wait_ge(turned_c, free2(t))
                    nc.tensor.transpose(psf[s][:, 0, :], stage[:, s, 0:2, :].rearrange("p a d -> p (a d)"), g.ident16[:, :])
                    nc.tensor.transpose(psf[s][:, 1, :], stage[:, s, 2:4, :].rearrange("p a d -> p (a d)"), g.ident16[:, :]
                                        ).then_inc(turned, 1)

                def tail(t, s, i):
                    pe.wait_ge(turned_c, ready(t))
                    for q, r, m in groups:
                        sem, value = copied(q - 6, t) if q >= 6 else copied(q + 6 if q < 3 else q, t - 1)
                        pe.wait_ge(sem, value)
                        for n in range(4):
                            last = nc.tensor.matmul(banks[q % 6][:, 0:m * D], ft[:, s, n // 3, :],
                                                    w16[:, n, r * D:(r + m) * D], start=n == 0, stop=n == 3)
                        last.then_inc(made, 1)
                skewed(pe, head, tail, NT)


def edges_relational(nc, g, name, first):
    with Phase(nc, name) as ph:
        (staged, gather_at, members, turned, turned_c, inverse, chosen, filled, summed, added) = ph.sems(
            "staged gather_at members turned turned_c inverse chosen filled summed added")
        step_a, step_b, opened, cleared, mark_a = ph.sems("step_a step_b opened cleared mark_a")
        win, got = ([ph.sem(f"{n}{q}") for q in range(4)] for n in ("win", "got"))
        edge = ph.sb("edge", [P, 4, FIELDS, K])
        src_at = ph.sb("src_at", [P, 4, K], I32)
        spot = g.node[:, :, :].rearrange("p t d -> p (t d)")
        member = spot[:, 0:4 * CE].rearrange("p (s k e) -> p s k e", s=4, k=K)
        memberT = spot[:, 4 * CE:5 * CE].rearrange("p (k e) -> p k e", k=K)
        table = ph.sb("table", [P, 2, K, R])
        kinds = ph.sb("kinds", [P, K, R])
        inv = ph.sb("inv", [P, 2, K])
        from_src = ph.sb("from_src", [P, 4, K, D])
        msg = ph.sb("msg", [P, 2, K, D])
        sums = ph.sb("sums", [D, NR])
        ps_turn, ps_sum = (ph.ps(n, [P, K, P]) for n in ("ps_turn", "ps_sum"))
        ps_inv = ph.ps("ps_inv", [P, 2, 512])
        inv_v = ps_inv[:, :, 0:4 * R].rearrange("p b (k r) -> p b k r", r=R)
        with nc.Block() as block:
            if first:
                @block.sync
                def _(sp):
                    def load(c, q, i):
                        sp.wait_ge(inverse, free2(c))
                        for k, b in enumerate(bases(nc, ENG.SP, g.base, c)):
                            sp.dma_start(table[:, q % 2, k, :], g.inv_count[ds(b, P), :]).then_inc(win[q], 16)
                    rounds(sp, [(load, 0)])

            @block.gpsimd
            def _(pool):
                def gather(c, q, i):
                    pool.wait_ge(filled, free4(c))
                    pool.wait_ge(gather_at, ready(c))
                    pool.sem_inc(opened, 1)
                    for k in range(K):
                        nc.gpsimd.indirect_dma_start(
                            from_src[:, q, k, :], None, g.typed[:, :],
                            bass.IndirectOffsetOnAxis(ap=src_at[:, q, k:k + 1], axis=0)).then_inc(got[q], 16)
                rounds(pool, [(gather, 0)])

            @block.scalar
            def _(act):
                for q in (staged, gather_at, turned_c):
                    act.sem_inc(q, START)

                def fields(c, q, i):
                    act.wait_ge(filled, free4(c))
                    alone(act, mark_a)
                    nc.scalar.activation(src_at[:, q, :], g.edges[:, SIDX, ds(c * K, K)], ACT.Copy
                                         ).then_inc(gather_at, 1)
                    nc.scalar.activation(edge[:, q, :, :], g.edges[:, :, ds(c * K, K)], ACT.Copy).then_inc(staged, 1)

                def turn_out(c, q, i):
                    act.wait_ge(turned, ready(c))
                    act.wait_ge(inverse, free1(c))
                    for h in range(2):
                        last = nc.scalar.activation(memberT[:, 4 * h:4 * h + 4, :], ps_turn[:, 4 * h:4 * h + 4, :],
                                                    ACT.Copy)
                    last.then_inc(turned_c, 1)
                rounds(act, [(fields, 4)] + ([(turn_out, 3)] if first else []))

            @block.vector
            def _(dve):
                v = nc.vector
                for q in (members, chosen, filled):
                    dve.sem_inc(q, START)
                dve.sem_inc(added, 2 * START)
                for q in (step_a, step_b):
                    dve.sem_inc(q, 1)
                v.memset(sums[:, :], 0.0).then_inc(cleared, 1)
                dve.wait_ge(cleared, 1)

                def zero_ones(c, q, i):
                    dve.wait_ge(staged, ready(c))
                    dve.wait_ge(summed, half_ready(c, 1) - 8)
                    v.tensor_tensor(member[:, q], repeat(g.iota[:, :], K), spread(edge[:, q, REL, :], P), ALU.is_equal
                                    ).then_inc(members, 1)

                def relations(c, q, i):
                    dve.wait_ge(step_a, c * 4 + 1)
                    v.tensor_tensor(kinds[:, :, :], repeat(g.iota[:, 0:R], K), spread(edge[:, q, TYPE, :], R),
                                    ALU.is_equal).then_inc(step_a, 1)

                def choose(c, q, i):
                    kv = kinds[:, :, :].rearrange("p (b k) r -> p b k r", b=2)
                    dve.wait_ge(inverse, ready(c))
                    dve.wait_ge(step_a, c * 4 + 2)
                    v.tensor_tensor(kv, kv, inv_v, ALU.mult).then_inc(step_a, 1)

                def take(c, q, i):
                    dve.wait_ge(step_a, c * 4 + 3)
                    dve.sem_inc(chosen, 1)
                    v.tensor_reduce(inv[:, q % 2, :], kinds[:, :, :], AX.X, ALU.add).then_inc(step_a, 1)

                def keep(c, q, i):
                    dve.wait_ge(step_a, c * 4 + 4)
                    v.tensor_copy(g.edges[:, INV, ds(c * K, K)], inv[:, q % 2, :]).then_inc(step_a, 1)

                def messages(c, q, i):
                    dve.wait_ge(got[q], 16 * K * (i + 1))
                    dve.wait_ge(summed, half_ready(c, 1) - 4)
                    v.tensor_tensor(msg[:, q % 2], from_src[:, q],
                                    spread(inv[:, q % 2, :] if first else edge[:, q, INV, :], D),
                                    ALU.mult).then_inc(filled, 1)

                regs = []

                def windows(c, q, i):
                    regs[:] = bases(nc, ENG.DVE, g.base, c)

                def add(k):
                    def step(c, q, i):
                        dve.wait_ge(step_b, c * K + k + 1)
                        if k % 4 == 0:
                            dve.wait_ge(summed, half_ready(c, k // 4))
                        window = sums[:, ds(regs[k], P)]
                        v.tensor_tensor(window, window, ps_sum[0:D, k, :], ALU.add).then_inc(step_b, 1)
                        if k % 4 == 3:
                            dve.wait_ge(step_b, c * K + k + 2)
                            dve.sem_inc(added, 1)
                    return step
                if first:
                    rounds(dve, [(windows, 0), (add(0), 0), (messages, 1), (add(1), 0), (relations, 2), (add(2), 0),
                                 (choose, 2), (add(3), 0), (take, 2), (add(4), 0), (zero_ones, 3), (add(5), 0),
                                 (keep, 2), (add(6), 0), (add(7), 0)])
                else:
                    rounds(dve, [(windows, 0), (add(0), 0), (add(1), 0), (messages, 1), (add(2), 0), (add(3), 0),
                                 (zero_ones, 3), (add(4), 0), (add(5), 0), (add(6), 0), (add(7), 0)])

            @block.tensor
            def _(pe):
                for q in (turned, inverse):
                    pe.sem_inc(q, START)
                pe.sem_inc(summed, 2 * START)

                def turn_members(c, q, i):
                    pe.wait_ge(members, ready(c))
                    pe.wait_ge(turned_c, free1(c))
                    for k in range(K):
                        last = nc.tensor.transpose(ps_turn[:, k, :], member[:, q, k, :], g.ident[:, :])
                    last.then_inc(turned, 1)

                def from_dst(c, q, i):
                    pe.wait_ge(turned_c, ready(c))
                    pe.wait_ge(win[q], 16 * K * (i + 1))
                    pe.wait_ge(chosen, free1(c))
                    for k in range(K):
                        last = nc.tensor.matmul(inv_v[:, k // 4, k % 4, :], memberT[:, k, :], table[:, q % 2, k, :],
                                                start=True, stop=True)
                    last.then_inc(inverse, 1)

                def product(h):
                    def step(c, q, i):
                        pe.wait_ge(members, ready(c))
                        pe.wait_ge(filled, ready(c))
                        pe.wait_ge(added, half_ready(c, h) - 2)
                        for k in range(4 * h, 4 * h + 4):
                            last = nc.tensor.matmul(ps_sum[0:D, k, :], msg[:, q % 2, k, :], member[:, q, k, :],
                                                    start=True, stop=True)
                        last.then_inc(summed, 1)
                    return step
                if first:
                    rounds(pe, [(from_dst, 2), (product(0), 1), (turn_members, 3), (product(1), 1)])
                else:
                    rounds(pe, [(product(0), 1), (product(1), 1)])
        turn = [ps_inv[:, n, :] for n in range(2)]
        columns_to_nodes(nc, g, ph, sums, D, turn)


def typed_index(nc, g):
    with nc.Block() as block:
        @block.vector
        def _(dve):
            nc.vector.scalar_tensor_tensor(g.edges[:, SIDX, :], g.edges[:, SRC, :], float(R), g.edges[:, TYPE, :],
                                           ALU.mult, ALU.add)


def after_relational(nc, g, name, bias, res_bias, last):
    with Phase(nc, name) as ph:
        loaded, step, stored, done = ph.sems("loaded step stored done")
        own = ph.sb("own", [P, NT, 2 * D])
        bv = ph.sb("bv", [P, 2, D])
        x = ph.sb("x", [P, NT, D]) if last else None
        h = g.node[:, :, 0:D]
        full, rest = N // P, N % P
        with nc.Block() as block:
            @block.sync
            def _(sp):
                sp.dma_start(own[:, :, :], nodes_view(g.hyp_src, slice(0, 2 * D))).then_inc(loaded, 16)
                sp.dma_start(bv[:, 0, :], bias.partition_broadcast(P)).then_inc(loaded, 16)
                sp.dma_start(bv[:, 1, :], res_bias.partition_broadcast(P)).then_inc(loaded, 16)
                if last:
                    sp.dma_start(x[:, :, :], nodes_view(g.xs)).then_inc(loaded, 16)
                    sp.wait_ge(done, 1)
                    sp.dma_start(g.out[0:full * P, :].rearrange("(t p) d -> p t d", p=P), x[:, 0:full, :]
                                 ).then_inc(stored, 16)
                    sp.dma_start(g.out[full * P:N, :], x[0:rest, full, :]).then_inc(stored, 16)
                    sp.wait_ge(stored, 32)

            @block.vector
            def _(dve):
                v = nc.vector
                chain = Chain(dve, step)
                dve.wait_ge(loaded, 16 * (4 if last else 3))
                chain(v.tensor_tensor(h, h, own[:, :, 0:D], ALU.add))
                chain(v.tensor_tensor(h, h, repeat(bv[:, 0, :], NT), ALU.add))
                chain(v.tensor_scalar(h, h, 0.0, None, ALU.max))
                chain(v.tensor_tensor(own[:, :, D:2 * D], own[:, :, D:2 * D], repeat(bv[:, 1, :], NT), ALU.add))
                chain(v.tensor_scalar(own[:, :, D:2 * D], own[:, :, D:2 * D], 0.0, None, ALU.max))
                chain(v.tensor_tensor(h, h, own[:, :, D:2 * D], ALU.add))
                if last:
                    chain(v.tensor_tensor(x[:, :, :], x[:, :, :], h, ALU.add))
                    dve.sem_inc(done, 1)


class Shared:
    pass


def gnn_kernel(nc, w, out, upto=99):
    g = Shared()
    g.w, g.x, g.src, g.dst, g.etype = w, w["x"], w["src"], w["dst"], w["edge_type_65"]
    g.ew, g.ew1, g.out = w["edge_weight"], w["edge_weight1"], out

    def dram(name, shape, dt=F32):
        return nc.dram_tensor(name + "_dram", shape, dt, kind="Internal").ap()

    g.src_p, g.dst_p, g.type_p = (dram(f"{n}_padded", (EP + 32,), I32) for n in ("src", "dst", "type"))
    g.ew_p, g.ew1_p = (dram(f"{n}_padded", (EP + 32,)) for n in ("weight", "weight1"))
    g.first_mask, g.last_mask = dram("first_mask", (EP,)), dram("last_mask", (EP,))
    g.xs = dram("x_now", (NR, D))
    g.sum0 = [dram(f"gcn_sum{k}", (NR + SPARE, D)) for k in range(COPIES)]
    g.sum1 = [dram(f"hyp_sum{k}", (NR + SPARE, D)) for k in range(COPIES)]
    g.gcn_table = dram("gcn_table", (NR, D))
    g.hyp_src = dram("hyp_src", (NR, 2 * D))
    g.hyp_dst = dram("hyp_dst", (NR, 3 * D))
    g.gat_src = dram("gat_src", (NR, D + H))
    g.gat_dst = dram("gat_dst", (NR, H))
    g.gat_dst16 = dram("gat_dst16", (NR, 3 * H), BF16)
    g.inv_count = dram("inv_count", (NR, R))
    g.typed = dram("typed", (NR * R, D))
    with Phase(nc, "all") as ph:
        g.edges = ph.sb("edges", [P, FIELDS, ET])
        g.node = ph.sb("node", [P, NT, D + 2 * H])
        g.base = ph.sb("base", [1, ET], I32)
        g.iota, g.ident, g.lower = (ph.sb(n, [P, P]) for n in ("iota", "ident", "lower"))
        g.ident16 = ph.sb("ident16", [P, P], BF16)
        g.halves = ph.sb("halves", [P, 2])
        g.lane = ph.sb("lane", [P, 1])
        g.ones = ph.sb("ones", [1, P])
        g.heads = ph.sb("heads", [H, D + 2 * H])
        stages = [
            lambda: prepare(nc, g),
            lambda: begin(nc, g),
            lambda: project(nc, g, "gcn_in", [w["L0_gnn_kernel"]], [(g.gcn_table, slice(0, D), slice(0, D))]),
            lambda: edges_gcn(nc, g),
            lambda: after_gcn(nc, g),
            lambda: hyperbolic_in(nc, g),
            lambda: project(nc, g, "hyp_in", [w["L1_gnn_w1"][0:D, :], w["L1_gnn_w1"][D:2 * D, :], None],
                            [(g.hyp_src, slice(0, D), slice(0, D)), (g.hyp_dst, slice(D, 3 * D), slice(D, 3 * D))],
                            first=(w["L1_gnn_W"], w["L1_gnn_b"])),
            lambda: edges_hyperbolic(nc, g),
            lambda: after_hyperbolic(nc, g),
        ]
        for n in (1, 2, 3):
            stages += [
                lambda n=n: project(nc, g, f"gat_in{n}", [w[f"L2_gnn_W{n}"]],
                                    [(g.gat_src, slice(0, D + H), slice(0, D + H)),
                                     (g.gat_dst, slice(0, H), slice(D + H, D + 2 * H))],
                                    dots=(w[f"L2_gnn_a_src{n}"], w[f"L2_gnn_a_dst{n}"]), split=g.gat_dst16),
                lambda n=n: edges_attention(nc, g, f"gat{n}"),
                lambda n=n: after_attention(nc, g, f"gat_end{n}", w[f"L2_gnn_b{n}"], n == 3),
            ]
        stages.append(lambda: typed_index(nc, g))
        for n in range(2):
            stages += [
                lambda n=n: project(nc, g, f"rel_in{n}", [w["L3_gnn_root"][n], w["L3_gnn_res_W"][n]],
                                    [(g.hyp_src, slice(0, 2 * D), slice(0, 2 * D))]),
                lambda n=n: typed_tables(nc, g, f"typed{n}", w["L3_gnn_W"][n]),
                lambda n=n: edges_relational(nc, g, f"rel{n}", n == 0),
                lambda n=n: after_relational(nc, g, f"rel_end{n}", w["L3_gnn_bias"][n], w["L3_gnn_res_b"][n], n == 1),
            ]
        for n, f in enumerate(stages):
            if n < upto:
                f()


_OUT = ((12500, 64), "float32")


def kernel(**inputs):
    import numpy as _np
    import concourse.bacc as _bacc
    from concourse import mybir as _mybir
    from concourse.bass_utils import run_bass_kernel_spmd as _run

    nc = _bacc.Bacc("TRN2", target_bir_lowering=False, num_devices=1)
    arrays, args = {}, {}
    for name, a in inputs.items():
        if name == "node_vec1":
            continue
        arrays[f"in_{name}"] = _np.ascontiguousarray(a)
        args[name] = nc.dram_tensor(f"in_{name}", a.shape, _mybir.dt.from_np(_np.asarray(a).dtype),
                                    kind="ExternalInput").ap()
    out = nc.dram_tensor("out", _OUT[0], _mybir.dt.from_np(_np.dtype(_OUT[1])), kind="ExternalOutput").ap()
    gnn_kernel(nc, args, out)
    return _run(nc, [arrays], core_ids=[0]).results[0]["out"]
```
